# Optimizing a Trainium2 kernel written in Bass

```python
import numpy as np
import jax
import jax.numpy as jnp

def _softmax(x, axis=-1):
    return jax.nn.softmax(x, axis=axis)

def _gelu(x):
    return jax.nn.gelu(x, approximate=True)

def _silu(x):
    return jax.nn.silu(x)

def _sigmoid(x):
    return jax.nn.sigmoid(x)

def _layernorm(x, axis=-1, eps=1e-05):
    m = jnp.mean(x, axis=axis, keepdims=True)
    v = jnp.var(x, axis=axis, keepdims=True)
    return (x - m) / jnp.sqrt(v + eps)

def _scatter_add(tgt, idx, src, axis=0):
    return tgt.at[idx].add(src)

def _segment_sum(src, seg, n):
    return jax.ops.segment_sum(src, seg, n)
kernel_name = 'mk_decoder_preln_d2_seqx_r4_165c09'

def setup_inputs(seed: int=0):
    np.random.seed(seed)
    _w = jnp.asarray

    def _rec_inputs():
        import jax
        import jax.numpy as jnp
        _rk = jax.random.key(seed)
        x = 7.22e-05 + 1 * jax.random.normal(jax.random.fold_in(_rk, 1), (16, 128, 256), jnp.float32)
        _lenS = 128 - jax.random.randint(jax.random.fold_in(_rk, 7), (16,), 0, max(1, 128 // 4) + 1, jnp.int32)
        _lenS2 = 128 - jax.random.randint(jax.random.fold_in(_rk, 8), (16,), 0, max(1, 128 // 4) + 1, jnp.int32)
        _ctx_1024P = jax.random.normal(jax.random.fold_in(_rk, 11), (16, 16, 256), jnp.float32)
        _ctx_1024c = jax.random.dirichlet(jax.random.fold_in(_rk, 511), 0.3 * jnp.ones((16,), jnp.float32), (16, 128))
        _ctx_1024t = jnp.einsum('bsk,bkd->bsd', _ctx_1024c, _ctx_1024P)
        _ctx_1024t = _ctx_1024t * jax.lax.rsqrt(jnp.mean(jnp.square(_ctx_1024t)) + 1e-12) * 0.953939
        ctx_1024 = 4.13588e-05 + 0.999923 * (_ctx_1024t + 0.3 * jax.random.normal(jax.random.fold_in(_rk, 611), (16, 128, 256), jnp.float32))
        itok_Bx1xSx1_0_63 = jax.random.randint(jax.random.fold_in(_rk, 13), (16, 1, 128, 1), 0, 64, jnp.int32)
        _validS = jnp.arange(128)[None, :] < _lenS[:, None]
        _validS2 = jnp.arange(128)[None, :] < _lenS2[:, None]
        _causal = jnp.tril(jnp.ones((128, 128), dtype=bool))
        mask_BxSxS2_bf0 = jnp.logical_not(jnp.ones((16, 128, 128), dtype=bool))
        return (x, ctx_1024, itok_Bx1xSx1_0_63, mask_BxSxS2_bf0)
    x, ctx_1024, itok_Bx1xSx1_0_63, mask_BxSxS2_bf0 = _rec_inputs()

    def _L0_attn_setup():
        import jax, jax.numpy as jnp
        import numpy as np
        D_MODEL = 256
        SCALE = float(np.sqrt(D_MODEL))
        key = jax.random.key(seed)
        k1, k2, k3 = jax.random.split(key, 3)
        input_data = jax.random.normal(k1, (4, 512, D_MODEL), dtype=jnp.float32)
        qk = jax.random.normal(k2, (D_MODEL, D_MODEL), dtype=jnp.float32) / SCALE
        ov = jax.random.normal(k3, (D_MODEL, D_MODEL), dtype=jnp.float32) / SCALE
        return {'input_data': input_data, 'qk': qk, 'ov': ov}
    _L0_attn_all = _L0_attn_setup()
    _L0_attn_in = {k: v for k, v in _L0_attn_all.items() if k in ('qk', 'ov')}
    del _L0_attn_all

    def _L0_xattn_setup():
        import jax, jax.numpy as jnp
        import numpy as np
        N_HEAD = 16
        D_MODEL = 256
        D_HEAD = D_MODEL // N_HEAD
        NEG_FILL = -10000000.0
        key = jax.random.key(seed)
        ks = jax.random.split(key, 10)
        B, S = (4, 512)
        scale = 1.0 / np.sqrt(D_MODEL)
        inp = {'q': jax.random.normal(ks[0], (B, S, D_MODEL), jnp.float32), 'k': jax.random.normal(ks[1], (B, S, D_MODEL), jnp.float32), 'v': jax.random.normal(ks[2], (B, S, D_MODEL), jnp.float32), 'attention_mask': jnp.zeros((B, S, S), dtype=bool), 'Wq': jax.random.normal(ks[3], (D_MODEL, D_MODEL), jnp.float32) * scale, 'bq': jnp.zeros((D_MODEL,), jnp.float32), 'Wk': jax.random.normal(ks[4], (D_MODEL, D_MODEL), jnp.float32) * scale, 'bk': jnp.zeros((D_MODEL,), jnp.float32), 'Wv': jax.random.normal(ks[5], (D_MODEL, D_MODEL), jnp.float32) * scale, 'bv': jnp.zeros((D_MODEL,), jnp.float32)}
        return inp
    _L0_xattn_all = _L0_xattn_setup()
    _L0_xattn_in = {k: v for k, v in _L0_xattn_all.items() if k in ('Wq', 'bq', 'Wk', 'bk', 'Wv', 'bv')}
    del _L0_xattn_all

    def _L0_ffn_setup():
        import jax, jax.numpy as jnp
        import numpy as np
        N_BLOCKS = 16
        BLOCK = 64
        TOP_K = N_BLOCKS // 4
        key = jax.random.key(seed)
        ks = jax.random.split(key, 7)
        D, H = (256, 1024)
        s = lambda k, shape, scale: jax.random.normal(k, shape, dtype=jnp.float32) * scale
        return {'x': s(ks[0], (4, 1024, D), 1.0), 'w_router': s(ks[1], (D, N_BLOCKS), 0.03), 'b_router': s(ks[2], (N_BLOCKS,), 0.01), 'w1': s(ks[3], (H, D), 0.03), 'b1': s(ks[4], (H,), 0.01), 'w2': s(ks[5], (D, H), 0.03), 'b2': s(ks[6], (D,), 0.01)}
    _L0_ffn_all = _L0_ffn_setup()
    _L0_ffn_in = {k: v for k, v in _L0_ffn_all.items() if k in ('w_router', 'b_router', 'w1', 'b1', 'w2', 'b2')}
    del _L0_ffn_all

    def _L1_attn_setup():
        import jax, jax.numpy as jnp
        import numpy as np
        B, L, D, H = (2, 512, 256, 16)
        C = D // H
        SCALE = 1.0 / np.sqrt(D).astype(np.float32)
        key = jax.random.key(seed)
        ks = jax.random.split(key, 5)
        return {'x': jax.random.normal(ks[0], (B, L, D), dtype=jnp.float32), 'w_qkv': jax.random.normal(ks[1], (3 * D, D), dtype=jnp.float32) * (1.0 / np.sqrt(D)), 'b_qkv': jax.random.normal(ks[2], (3 * D,), dtype=jnp.float32) * 0.02, 'w_o': jax.random.normal(ks[3], (D, D), dtype=jnp.float32) * (1.0 / np.sqrt(D)), 'b_o': jax.random.normal(ks[4], (D,), dtype=jnp.float32) * 0.02}
    _L1_attn_all = _L1_attn_setup()
    _L1_attn_in = {k: v for k, v in _L1_attn_all.items() if k in ('w_qkv', 'b_qkv', 'w_o', 'b_o')}
    del _L1_attn_all

    def _L1_xattn_setup():
        import jax, jax.numpy as jnp
        import numpy as np
        HEADS = 16
        WINDOW = 64
        D_MODEL = 256

        def _ln(x, g, b, eps=1e-05):
            m = jnp.mean(x, -1, keepdims=True)
            var = jnp.mean((x - m) ** 2, -1, keepdims=True)
            return (x - m) * jax.lax.rsqrt(var + eps) * g + b

        def _proj(x, g, b, W, bias):
            return _ln(x, g, b) @ W.T + bias

        def _bucket(x, pad_value):
            L = x.shape[-2]
            n = WINDOW * -(-L // WINDOW)
            pads = [(0, 0)] * x.ndim
            pads[-2] = (0, n - L)
            x = jnp.pad(x, pads, constant_values=pad_value)
            return x.reshape(*x.shape[:-2], n // WINDOW, WINDOW, x.shape[-1])

        def _unfold(x, pad_value):
            pads = [(0, 0)] * x.ndim
            pads[-3] = (1, 0)
            prev = jnp.pad(x, pads, constant_values=pad_value)[..., :-1, :, :]
            return jnp.concatenate([prev, x], axis=-2)

        def _rotary(x):
            S, d = (x.shape[-2], x.shape[-1])
            inv = 1.0 / 10000.0 ** (jnp.arange(0, d, 2, dtype=jnp.float32) / d)
            freqs = jnp.arange(S, dtype=jnp.float32)[:, None] * inv[None, :]
            freqs = jnp.repeat(freqs, 2, axis=-1)
            cos, sin = (jnp.cos(freqs).astype(x.dtype), jnp.sin(freqs).astype(x.dtype))
            xp = x.reshape(*x.shape[:-1], d // 2, 2)
            xr = jnp.stack([-xp[..., 1], xp[..., 0]], axis=-1).reshape(x.shape)
            return x * cos + xr * sin

        def _forward(q, k, v, cell, ln_q_w, ln_q_b, w_q, b_q, ln_k_w, ln_k_b, w_k, b_k, ln_v_w, ln_v_b, w_v, b_v, ln_o_w, ln_o_b, w_o, b_o):
            B, L, D = q.shape
            hd = D // HEADS

            def split_heads(x):
                return x.reshape(B, L, HEADS, hd).transpose(0, 2, 1, 3)
            qh = split_heads(_proj(q, ln_q_w, ln_q_b, w_q, b_q))
            kh = split_heads(_proj(k, ln_k_w, ln_k_b, w_k, b_k))
            vh = split_heads(_proj(v, ln_v_w, ln_v_b, w_v, b_v))
            bq = _bucket(qh, -1.0)
            bk = _unfold(_bucket(kh, -1.0), -1.0)
            bv = _unfold(_bucket(vh, -1.0), -1.0)
            nb = bq.shape[2]
            n = nb * WINDOW
            i = _bucket(jnp.arange(n, dtype=jnp.int32)[:, None], -1)
            j = jnp.swapaxes(_unfold(i, -1), -1, -2)
            mask = (i >= j) & (j != -1)
            req = _bucket(cell, -1)
            rek = jnp.swapaxes(_unfold(req, -1), -1, -2)
            mask = mask & (req == rek)
            bq = _rotary(bq)
            bk = _rotary(bk)
            p = jnp.einsum('bhnqd,bhnkd->bhnqk', bq, bk) / jnp.sqrt(jnp.asarray(hd, bq.dtype))
            p = jnp.where(mask, p, jnp.finfo(p.dtype).min)
            a = jax.nn.softmax(p, axis=-1)
            o = jnp.einsum('bhnqk,bhnkd->bhnqd', a, bv)
            o = o.reshape(B, HEADS, n, hd)[:, :, :L]
            o = o.transpose(0, 2, 1, 3).reshape(B, L, D)
            return _proj(o, ln_o_w, ln_o_b, w_o, b_o)
        key = jax.random.key(seed)
        ks = jax.random.split(key, 10)
        B, L, D = (2, 1024, D_MODEL)
        inp = {'q': jax.random.normal(ks[0], (B, L, D), dtype=jnp.float32), 'k': jax.random.normal(ks[1], (B, L, D), dtype=jnp.float32), 'v': jax.random.normal(ks[2], (B, L, D), dtype=jnp.float32), 'cell': jnp.sort(jax.random.randint(ks[3], (B, 1, L, 1), 0, 64, dtype=jnp.int32), axis=2)}
        for idx, name in enumerate(['q', 'k', 'v', 'o']):
            inp[f'ln_{name}_w'] = jnp.ones((D,), jnp.float32)
            inp[f'ln_{name}_b'] = jnp.zeros((D,), jnp.float32)
            inp[f'w_{name}'] = jax.random.normal(ks[4 + idx], (D, D), dtype=jnp.float32) * 0.02
            inp[f'b_{name}'] = jnp.zeros((D,), jnp.float32)
        return inp
    _L1_xattn_all = _L1_xattn_setup()
    _L1_xattn_in = {k: v for k, v in _L1_xattn_all.items() if k in ('ln_q_w', 'ln_q_b', 'w_q', 'b_q', 'ln_k_w', 'ln_k_b', 'w_k', 'b_k', 'ln_v_w', 'ln_v_b', 'w_v', 'b_v', 'ln_o_w', 'ln_o_b', 'w_o', 'b_o')}
    del _L1_xattn_all

    def _L1_ffn_setup():
        import jax, jax.numpy as jnp
        import numpy as np
        H = 256
        I = 128
        E = 8
        TOP_K = 2
        N_SHARED = 2
        SHARED_I = I * N_SHARED
        SCALE = 2.5
        NORM_TOPK = True
        B, S = (2, 256)

        def _swiglu(x, wg, wu, wd):
            g = x @ wg.T
            u = x @ wu.T
            return jax.nn.silu(g) * u @ wd.T
        key = jax.random.key(seed)
        ks = jax.random.split(key, 8)
        std = 0.02
        return {'hidden_states': jax.random.normal(ks[0], (B, S, H), jnp.float32), 'gate_weight': jax.random.normal(ks[1], (E, H), jnp.float32) * std, 'w_gate': jax.random.normal(ks[2], (E, I, H), jnp.float32) * std, 'w_up': jax.random.normal(ks[3], (E, I, H), jnp.float32) * std, 'w_down': jax.random.normal(ks[4], (E, H, I), jnp.float32) * std, 'ws_gate': jax.random.normal(ks[5], (SHARED_I, H), jnp.float32) * std, 'ws_up': jax.random.normal(ks[6], (SHARED_I, H), jnp.float32) * std, 'ws_down': jax.random.normal(ks[7], (H, SHARED_I), jnp.float32) * std}
    _L1_ffn_all = _L1_ffn_setup()
    _L1_ffn_in = {k: v for k, v in _L1_ffn_all.items() if k in ('gate_weight', 'w_gate', 'w_up', 'w_down', 'ws_gate', 'ws_up', 'ws_down')}
    del _L1_ffn_all
    return {'x': x, 'ctx_1024': ctx_1024, 'itok_Bx1xSx1_0_63': itok_Bx1xSx1_0_63, 'mask_BxSxS2_bf0': mask_BxSxS2_bf0, 'L0_attn_qk': _L0_attn_in['qk'], 'L0_attn_ov': _L0_attn_in['ov'], 'L0_xattn_Wq': _L0_xattn_in['Wq'], 'L0_xattn_bq': _L0_xattn_in['bq'], 'L0_xattn_Wk': _L0_xattn_in['Wk'], 'L0_xattn_bk': _L0_xattn_in['bk'], 'L0_xattn_Wv': _L0_xattn_in['Wv'], 'L0_xattn_bv': _L0_xattn_in['bv'], 'L0_ffn_w_router': _L0_ffn_in['w_router'], 'L0_ffn_b_router': _L0_ffn_in['b_router'], 'L0_ffn_w1': _L0_ffn_in['w1'], 'L0_ffn_b1': _L0_ffn_in['b1'], 'L0_ffn_w2': _L0_ffn_in['w2'], 'L0_ffn_b2': _L0_ffn_in['b2'], 'L1_attn_w_qkv': _L1_attn_in['w_qkv'], 'L1_attn_b_qkv': _L1_attn_in['b_qkv'], 'L1_attn_w_o': _L1_attn_in['w_o'], 'L1_attn_b_o': _L1_attn_in['b_o'], 'L1_xattn_ln_q_w': _L1_xattn_in['ln_q_w'], 'L1_xattn_ln_q_b': _L1_xattn_in['ln_q_b'], 'L1_xattn_w_q': _L1_xattn_in['w_q'], 'L1_xattn_b_q': _L1_xattn_in['b_q'], 'L1_xattn_ln_k_w': _L1_xattn_in['ln_k_w'], 'L1_xattn_ln_k_b': _L1_xattn_in['ln_k_b'], 'L1_xattn_w_k': _L1_xattn_in['w_k'], 'L1_xattn_b_k': _L1_xattn_in['b_k'], 'L1_xattn_ln_v_w': _L1_xattn_in['ln_v_w'], 'L1_xattn_ln_v_b': _L1_xattn_in['ln_v_b'], 'L1_xattn_w_v': _L1_xattn_in['w_v'], 'L1_xattn_b_v': _L1_xattn_in['b_v'], 'L1_xattn_ln_o_w': _L1_xattn_in['ln_o_w'], 'L1_xattn_ln_o_b': _L1_xattn_in['ln_o_b'], 'L1_xattn_w_o': _L1_xattn_in['w_o'], 'L1_xattn_b_o': _L1_xattn_in['b_o'], 'L1_ffn_gate_weight': _L1_ffn_in['gate_weight'], 'L1_ffn_w_gate': _L1_ffn_in['w_gate'], 'L1_ffn_w_up': _L1_ffn_in['w_up'], 'L1_ffn_w_down': _L1_ffn_in['w_down'], 'L1_ffn_ws_gate': _L1_ffn_in['ws_gate'], 'L1_ffn_ws_up': _L1_ffn_in['ws_up'], 'L1_ffn_ws_down': _L1_ffn_in['ws_down']}

def reference(x, ctx_1024, itok_Bx1xSx1_0_63, mask_BxSxS2_bf0, L0_attn_qk, L0_attn_ov, L0_xattn_Wq, L0_xattn_bq, L0_xattn_Wk, L0_xattn_bk, L0_xattn_Wv, L0_xattn_bv, L0_ffn_w_router, L0_ffn_b_router, L0_ffn_w1, L0_ffn_b1, L0_ffn_w2, L0_ffn_b2, L1_attn_w_qkv, L1_attn_b_qkv, L1_attn_w_o, L1_attn_b_o, L1_xattn_ln_q_w, L1_xattn_ln_q_b, L1_xattn_w_q, L1_xattn_b_q, L1_xattn_ln_k_w, L1_xattn_ln_k_b, L1_xattn_w_k, L1_xattn_b_k, L1_xattn_ln_v_w, L1_xattn_ln_v_b, L1_xattn_w_v, L1_xattn_b_v, L1_xattn_ln_o_w, L1_xattn_ln_o_b, L1_xattn_w_o, L1_xattn_b_o, L1_ffn_gate_weight, L1_ffn_w_gate, L1_ffn_w_up, L1_ffn_w_down, L1_ffn_ws_gate, L1_ffn_ws_up, L1_ffn_ws_down):
    import jax
    import jax.numpy as jnp

    def _L0_attn_ref(input_data, qk, ov):
        import jax, jax.numpy as jnp
        import numpy as np
        D_MODEL = 256
        SCALE = float(np.sqrt(D_MODEL))
        S = input_data.shape[1]
        scores = jnp.einsum('bsd,de,bte->bst', input_data, qk, input_data) / SCALE
        causal = jnp.tril(jnp.ones((S, S), dtype=bool))
        scores = jnp.where(causal, scores, -jnp.inf)
        attn = jax.nn.softmax(scores, axis=-1)
        return jnp.einsum('bst,btd,de->bse', attn, input_data, ov)

    def _L0_xattn_ref(q, k, v, attention_mask, Wq, bq, Wk, bk, Wv, bv):
        import jax, jax.numpy as jnp
        import numpy as np
        N_HEAD = 16
        D_MODEL = 256
        D_HEAD = D_MODEL // N_HEAD
        NEG_FILL = -10000000.0
        B, Sq, _ = q.shape
        Sk = k.shape[1]
        qh = (q @ Wq.T + bq).reshape(B, Sq, N_HEAD, D_HEAD)
        kh = (k @ Wk.T + bk).reshape(B, Sk, N_HEAD, D_HEAD)
        vh = (v @ Wv.T + bv).reshape(B, Sk, N_HEAD, D_HEAD)
        scores = jnp.einsum('bqhd,bkhd->bhqk', qh, kh) / np.sqrt(D_HEAD)
        scores = jnp.where(attention_mask[:, None, :, :], NEG_FILL, scores)
        probs = jax.nn.softmax(scores, axis=-1)
        out = jnp.einsum('bhqk,bkhd->bqhd', probs, vh)
        return out.reshape(B, Sq, N_HEAD * D_HEAD)

    def _L0_ffn_ref(x, w_router, b_router, w1, b1, w2, b2):
        import jax, jax.numpy as jnp
        import numpy as np
        N_BLOCKS = 16
        BLOCK = 64
        TOP_K = N_BLOCKS // 4
        orig_shape = x.shape
        D = orig_shape[-1]
        xf = x.reshape(-1, D)
        prob = jax.nn.softmax(xf @ w_router + b_router, axis=-1)
        _, idx = jax.lax.top_k(prob, TOP_K)
        mask = (idx[:, :, None] == jnp.arange(N_BLOCKS)[None, None, :]).any(axis=1)
        mask = mask.astype(x.dtype)
        w1b = w1.reshape(N_BLOCKS, BLOCK, D)
        b1b = b1.reshape(N_BLOCKS, BLOCK)
        w2b = jnp.transpose(w2.reshape(D, N_BLOCKS, BLOCK), (1, 2, 0))
        h = jax.nn.relu(jnp.einsum('nd,ebd->neb', xf, w1b) + b1b[None])
        y = jnp.einsum('neb,ebd,ne->nd', h, w2b, mask)
        y = y + b2[None, :]
        return y.reshape(orig_shape)

    def _L1_attn_ref(x, w_qkv, b_qkv, w_o, b_o):
        import jax, jax.numpy as jnp
        import numpy as np
        B, L, D, H = (2, 512, 256, 16)
        C = D // H
        SCALE = 1.0 / np.sqrt(D).astype(np.float32)
        b, l, d = x.shape
        h, c = (H, d // H)
        qkv = jnp.einsum('bld,ed->ble', x, w_qkv) + b_qkv
        q, k, v = jnp.split(qkv, 3, axis=-1)
        q = q.reshape(b, l, h, c)
        k = k.reshape(b, l, h, c)
        v = v.reshape(b, l, h, c)
        attn = jax.nn.softmax(jnp.einsum('blhc,bmhc->bhlm', q, k) * SCALE, axis=-1)
        heads = jnp.einsum('bhlm,bmhc->blhc', attn, v).reshape(b, l, d)
        return jnp.einsum('bld,ed->ble', heads, w_o) + b_o + x

    def _L1_xattn_ref(q, k, v, cell, ln_q_w, ln_q_b, w_q, b_q, ln_k_w, ln_k_b, w_k, b_k, ln_v_w, ln_v_b, w_v, b_v, ln_o_w, ln_o_b, w_o, b_o):
        import jax, jax.numpy as jnp
        import numpy as np
        HEADS = 16
        WINDOW = 64
        D_MODEL = 256

        def _ln(x, g, b, eps=1e-05):
            m = jnp.mean(x, -1, keepdims=True)
            var = jnp.mean((x - m) ** 2, -1, keepdims=True)
            return (x - m) * jax.lax.rsqrt(var + eps) * g + b

        def _proj(x, g, b, W, bias):
            return _ln(x, g, b) @ W.T + bias

        def _bucket(x, pad_value):
            L = x.shape[-2]
            n = WINDOW * -(-L // WINDOW)
            pads = [(0, 0)] * x.ndim
            pads[-2] = (0, n - L)
            x = jnp.pad(x, pads, constant_values=pad_value)
            return x.reshape(*x.shape[:-2], n // WINDOW, WINDOW, x.shape[-1])

        def _unfold(x, pad_value):
            pads = [(0, 0)] * x.ndim
            pads[-3] = (1, 0)
            prev = jnp.pad(x, pads, constant_values=pad_value)[..., :-1, :, :]
            return jnp.concatenate([prev, x], axis=-2)

        def _rotary(x):
            S, d = (x.shape[-2], x.shape[-1])
            inv = 1.0 / 10000.0 ** (jnp.arange(0, d, 2, dtype=jnp.float32) / d)
            freqs = jnp.arange(S, dtype=jnp.float32)[:, None] * inv[None, :]
            freqs = jnp.repeat(freqs, 2, axis=-1)
            cos, sin = (jnp.cos(freqs).astype(x.dtype), jnp.sin(freqs).astype(x.dtype))
            xp = x.reshape(*x.shape[:-1], d // 2, 2)
            xr = jnp.stack([-xp[..., 1], xp[..., 0]], axis=-1).reshape(x.shape)
            return x * cos + xr * sin

        def _forward(q, k, v, cell, ln_q_w, ln_q_b, w_q, b_q, ln_k_w, ln_k_b, w_k, b_k, ln_v_w, ln_v_b, w_v, b_v, ln_o_w, ln_o_b, w_o, b_o):
            B, L, D = q.shape
            hd = D // HEADS

            def split_heads(x):
                return x.reshape(B, L, HEADS, hd).transpose(0, 2, 1, 3)
            qh = split_heads(_proj(q, ln_q_w, ln_q_b, w_q, b_q))
            kh = split_heads(_proj(k, ln_k_w, ln_k_b, w_k, b_k))
            vh = split_heads(_proj(v, ln_v_w, ln_v_b, w_v, b_v))
            bq = _bucket(qh, -1.0)
            bk = _unfold(_bucket(kh, -1.0), -1.0)
            bv = _unfold(_bucket(vh, -1.0), -1.0)
            nb = bq.shape[2]
            n = nb * WINDOW
            i = _bucket(jnp.arange(n, dtype=jnp.int32)[:, None], -1)
            j = jnp.swapaxes(_unfold(i, -1), -1, -2)
            mask = (i >= j) & (j != -1)
            req = _bucket(cell, -1)
            rek = jnp.swapaxes(_unfold(req, -1), -1, -2)
            mask = mask & (req == rek)
            bq = _rotary(bq)
            bk = _rotary(bk)
            p = jnp.einsum('bhnqd,bhnkd->bhnqk', bq, bk) / jnp.sqrt(jnp.asarray(hd, bq.dtype))
            p = jnp.where(mask, p, jnp.finfo(p.dtype).min)
            a = jax.nn.softmax(p, axis=-1)
            o = jnp.einsum('bhnqk,bhnkd->bhnqd', a, bv)
            o = o.reshape(B, HEADS, n, hd)[:, :, :L]
            o = o.transpose(0, 2, 1, 3).reshape(B, L, D)
            return _proj(o, ln_o_w, ln_o_b, w_o, b_o)
        return _forward(q, k, v, cell, ln_q_w, ln_q_b, w_q, b_q, ln_k_w, ln_k_b, w_k, b_k, ln_v_w, ln_v_b, w_v, b_v, ln_o_w, ln_o_b, w_o, b_o)

    def _L1_ffn_ref(hidden_states, gate_weight, w_gate, w_up, w_down, ws_gate, ws_up, ws_down):
        import jax, jax.numpy as jnp
        import numpy as np
        H = 256
        I = 128
        E = 8
        TOP_K = 2
        N_SHARED = 2
        SHARED_I = I * N_SHARED
        SCALE = 2.5
        NORM_TOPK = True
        B, S = (2, 256)

        def _swiglu(x, wg, wu, wd):
            g = x @ wg.T
            u = x @ wu.T
            return jax.nn.silu(g) * u @ wd.T
        b, s, h = hidden_states.shape
        x = hidden_states.reshape(-1, h)
        shared_out = _swiglu(x, ws_gate, ws_up, ws_down)
        logits = x.astype(jnp.float32) @ gate_weight.astype(jnp.float32).T
        scores = jax.nn.sigmoid(logits)
        topk_w, topk_idx = jax.lax.top_k(scores, TOP_K)
        if TOP_K > 1 and NORM_TOPK:
            topk_w = topk_w / (topk_w.sum(-1, keepdims=True) + 1e-20)
        topk_w = topk_w * SCALE
        onehot = jax.nn.one_hot(topk_idx, E, dtype=topk_w.dtype)
        combine = jnp.einsum('tk,tke->te', topk_w, onehot)
        g = jnp.einsum('th,eih->tei', x, w_gate)
        u = jnp.einsum('th,eih->tei', x, w_up)
        hmid = jax.nn.silu(g) * u
        y = jnp.einsum('tei,ehi->teh', hmid, w_down)
        routed_out = jnp.einsum('te,teh->th', combine, y)
        out = (routed_out + shared_out).reshape(b, s, h)
        return out
    x = x + _L0_attn_ref(_layernorm(x, axis=-1), L0_attn_qk, L0_attn_ov)
    x = x + _L0_xattn_ref(_layernorm(x, axis=-1), ctx_1024, ctx_1024, mask_BxSxS2_bf0, L0_xattn_Wq, L0_xattn_bq, L0_xattn_Wk, L0_xattn_bk, L0_xattn_Wv, L0_xattn_bv)
    x = x + _L0_ffn_ref(_layernorm(x, axis=-1), L0_ffn_w_router, L0_ffn_b_router, L0_ffn_w1, L0_ffn_b1, L0_ffn_w2, L0_ffn_b2)
    x = x + _L1_attn_ref(_layernorm(x, axis=-1), L1_attn_w_qkv, L1_attn_b_qkv, L1_attn_w_o, L1_attn_b_o)
    x = x + _L1_xattn_ref(_layernorm(x, axis=-1), ctx_1024, ctx_1024, itok_Bx1xSx1_0_63, L1_xattn_ln_q_w, L1_xattn_ln_q_b, L1_xattn_w_q, L1_xattn_b_q, L1_xattn_ln_k_w, L1_xattn_ln_k_b, L1_xattn_w_k, L1_xattn_b_k, L1_xattn_ln_v_w, L1_xattn_ln_v_b, L1_xattn_w_v, L1_xattn_b_v, L1_xattn_ln_o_w, L1_xattn_ln_o_b, L1_xattn_w_o, L1_xattn_b_o)
    x = x + _L1_ffn_ref(_layernorm(x, axis=-1), L1_ffn_gate_weight, L1_ffn_w_gate, L1_ffn_w_up, L1_ffn_w_down, L1_ffn_ws_gate, L1_ffn_ws_up, L1_ffn_ws_down)
    return x

_drawn_inputs = setup_inputs


def setup_inputs(seed=0):
    import zlib

    import numpy as np

    out = dict(_drawn_inputs(seed))
    spreads = {'L0_xattn_bq': (0.0, 0.1),
     'L0_xattn_bk': (0.0, 0.8),
     'L0_xattn_bv': (0.0, 0.1),
     'L1_xattn_ln_q_w': (1.0, 0.6),
     'L1_xattn_ln_q_b': (0.0, 0.8),
     'L1_xattn_b_q': (0.0, 0.8),
     'L1_xattn_ln_k_w': (1.0, 0.6),
     'L1_xattn_ln_k_b': (0.0, 0.8),
     'L1_xattn_b_k': (0.0, 0.8),
     'L1_xattn_ln_v_w': (1.0, 0.6),
     'L1_xattn_ln_v_b': (0.0, 0.524),
     'L1_xattn_b_v': (0.0, 0.1),
     'L1_xattn_ln_o_w': (1.0, 0.552),
     'L1_xattn_ln_o_b': (0.0, 0.629),
     'L1_xattn_b_o': (0.0, 0.1)}
    factors = {'L0_ffn_b_router': 3.074,
     'L0_ffn_b1': 8.0,
     'L0_ffn_b2': 6.083,
     'L1_attn_b_qkv': 5.356,
     'L1_attn_b_o': 6.54,
     'L1_xattn_w_q': 8.0,
     'L1_xattn_w_k': 8.0,
     'L1_ffn_gate_weight': 6.868,
     'L1_ffn_w_gate': 6.102,
     'L1_ffn_w_up': 6.034,
     'L1_ffn_w_down': 6.035,
     'L1_ffn_ws_gate': 7.678,
     'L1_ffn_ws_up': 7.532,
     'L1_ffn_ws_down': 7.569}
    for name, (base, spread) in spreads.items():
        noise = np.random.default_rng([zlib.crc32(name.encode()), seed]).standard_normal(out[name].shape)
        drawn = base * np.exp(spread * noise) if base else spread * noise
        out[name] = jnp.asarray(drawn.astype(out[name].dtype))
    for name, factor in factors.items():
        out[name] = (out[name] * factor).astype(out[name].dtype)
    return out
```

```python
from contextlib import ExitStack

import numpy as np

import concourse.bass as bass
from concourse import mybir

P = 128
F32 = mybir.dt.float32
BF16 = mybir.dt.bfloat16
U8 = mybir.dt.uint8
I32 = mybir.dt.int32
ALU = mybir.AluOpType
ACT = mybir.ActivationFunctionType
AX = mybir.AxisListType

B, S, D = 16, 128, 256
C = D // P
H, DH = 16, 16
PAIRS = B // 2
T = 2 * S
NB, BLOCK, TOPB = 16, 64, 4
FF = NB * BLOCK // P
E, EI, SHI = 8, 128, 256
SH = SHI // P
TOPE = 2
ROUTE_SCALE = 2.5
EPS = 1e-5
NEG = -1.0e30

VEC = {}
for _name, _n in (("bq0", C), ("bk0", C), ("b1", FF), ("bq1", C), ("bk1", C), ("gq", C), ("gk", C),
                  ("gv", C), ("go", C), ("even", 1), ("odd", 1)):
    VEC[_name] = (sum(n for _, n in VEC.values()), _n)
NVEC = sum(n for _, n in VEC.values())
ROWS = {}
for _name, _n in (("bv0", D), ("br", NB), ("b2", D), ("bv1", D), ("bo1", D), ("bxq", D), ("bxk", D),
                  ("bxv", D), ("bxo", D), ("cosq", DH), ("sinq", DH), ("cosk", DH), ("sink", DH)):
    ROWS[_name] = (sum(n for _, n in ROWS.values()), _n)
NROW = sum(n for _, n in ROWS.values())


def program(nc, x, ctxT, ctx, tokq, tokk, mask, ident, causal, expand, vec, rows, lnb,
            w_qk, w_ov, w_q0, w_k0, w_v0, w_r0, w_1, w_2, w_qkv, w_o1, w_x, w_g, w_gate, w_up,
            w_down, ws_gate, ws_up, ws_down, out):
    stack = ExitStack()
    with stack:
        def sb(name, shape, dt=F32):
            return stack.enter_context(nc.sbuf_tensor(name, shape, dt))

        def sem(name):
            return stack.enter_context(nc.semaphore(name))

        X = sb("X", [P, B, D])
        idn = sb("idn", [P, P])
        idnb = sb("idnb", [P, P], BF16)
        caus = sb("caus", [P, P])
        expb = sb("expb", [P, FF * P], BF16)
        vecs = sb("vecs", [P, NVEC])
        rws = sb("rws", [P, NROW])
        lnbs = sb("lnbs", [P, 4, C, P])
        bias4 = sb("bias4", [P, 4, D])
        mask4 = sb("mask4", [P, B, S // 4], I32)
        mask8 = mask4[:].rearrange("p b s -> p (b s)").bitcast(U8).rearrange("p (b s) -> p b s", b=B)
        tq = sb("tq", [P, B], I32)
        mb0 = sb("mb0", [P, B, S], BF16)
        mb1 = sb("mb1", [P, B, S], BF16)
        allm = sb("allm", [P, B])
        scl0 = sb("scl0", [P, B])
        mhalf = sb("mhalf", [P, 4])
        Wqk, Wov = sb("Wqk", [P, C, D]), sb("Wov", [P, C, D])
        Wq0, Wk0, Wv0 = sb("Wq0", [P, C, D]), sb("Wk0", [P, C, D]), sb("Wv0", [P, C, D])
        Wr0 = sb("Wr0", [P, C, NB])
        W1, W2 = sb("W1", [P, C, FF * P]), sb("W2", [P, FF, D])
        Wqkv, Wo1 = sb("Wqkv", [P, C, 3 * D]), sb("Wo1", [P, C, D])
        Wx = sb("Wx", [P, 4, C, D])
        Wg = sb("Wg", [P, C, E])
        Wgate, Wup = sb("Wgate", [P, C, E * EI]), sb("Wup", [P, C, E * EI])
        Wdown = sb("Wdown", [P, E, D])
        Wsg, Wsu, Wsd = sb("Wsg", [P, C, SHI]), sb("Wsu", [P, C, SHI]), sb("Wsd", [P, SH, D])

        def V(name, c=0):
            o = VEC[name][0] + c
            return vecs[:, o:o + 1]

        def R(name):
            o, n = ROWS[name]
            return rws[:, o:o + n]

        two = range(2)
        bst = [sb(f"bst{r}", [P, 2, 6]) for r in two]
        mv = [sb(f"mv{r}", [P, 2, 2]) for r in two]
        ve = [sb(f"ve{r}", [P, 2]) for r in two]
        rstd = [sb(f"rstd{r}", [P, 2]) for r in two]
        xn = [sb(f"xn{r}", [P, 2, D]) for r in two]
        xnT = [sb(f"xnT{r}", [P, C, T]) for r in two]

        names = ["pj0", "pj1", "sc0", "sc1", "tp0", "tp1", "ov0", "ov1"]
        bank = {n: stack.enter_context(nc.psum_tensor(n, [P, 512], F32)) for n in names}
        filled = {n: sem(f"filled_{n}") for n in names}
        drained = {n: sem(f"drained_{n}") for n in names}
        used = dict.fromkeys(names, 0)

        qT = [sb(f"qT{r}", [P, C, T]) for r in two]
        kM = [sb(f"kM{r}", [P, C, 2, 2, S]) for r in two]
        va = [sb(f"va{r}", [P, 2, H, DH + 1]) for r in two]
        mx = [sb(f"mx{r}", [P, 4]) for r in two]
        sh = [sb(f"sh{r}", [P, 4, S]) for r in two]
        pr = [sb(f"pr{r}", [P, 4, S]) for r in two]
        pT = [sb(f"pT{r}", [P, 4, S]) for r in two]
        rin = [sb(f"rin{r}", [P, H]) for r in two]
        hd = [sb(f"hd{r}", [P, 2, D]) for r in two]
        cbst = [sb(f"cbst{r}", [P, 2, 6]) for r in two]
        cmv = [sb(f"cmv{r}", [P, 2, 2]) for r in two]
        cve = [sb(f"cve{r}", [P, 2]) for r in two]
        crs = [sb(f"crs{r}", [P, 2]) for r in two]
        v2 = [sb(f"v2{r}", [P, 2]) for r in two]
        rq = [sb(f"rq{r}", [P, 2]) for r in two]
        cn = [sb(f"cn{r}", [P, 2, D]) for r in two]
        cnT = [sb(f"cnT{r}", [P, C, T]) for r in two]
        cT = [sb(f"cT{r}", [P, C, T]) for r in two]
        cx = [sb(f"cx{r}", [P, 2, D]) for r in two]
        hst = sb("hst", [P, 2, 6])
        hmv = sb("hmv", [P, 2, 2])
        hve = sb("hve", [P, 2])
        hrs = sb("hrs", [P, 2])
        hdT = sb("hdT", [P, C, T])
        hT = [sb(f"hT{r}", [P, FF, T]) for r in two]
        tk = hT[0][:].rearrange("p a b -> p (a b)").bitcast(I32).rearrange("p (b s) -> p b s", b=B)
        expd = hT[1][:].rearrange("p a b -> p (a b)")[:, 0:FF * P]
        parts = [hT[i // 2][:].rearrange("p a b -> p (a b)")[:, (i % 2) * 1024:(i % 2 + 1) * 1024]
                 .rearrange("p (i j d) -> p i j d", i=2, j=2) for i in range(4)]
        rt, rc, rs, ro = parts
        lg = sb("lg", [P, 2, NB])
        lmx = sb("lmx", [P, 2])
        lsh = sb("lsh", [P, 2, NB])
        le = sb("le", [P, 2, NB + 8 - TOPB])
        ls = sb("ls", [P, 2, E + 8 - TOPE])
        nmx = [sb(f"nmx{r}", [P, 2]) for r in two]
        rsum = [sb(f"rsum{r}", [P, 2]) for r in two]
        tops5 = sb("tops5", [P, 2, 8])
        kept5 = sb("kept5", [P, 2, E + 8 - TOPE])
        deni, rden = sb("deni", [P, 2]), sb("rden", [P, 2])
        sel = sb("sel", [P, 2, E])
        v3, v4, v5 = ([sb(f"{n}{r}", [P, 2]) for r in two] for n in ("va3", "va4", "va5"))
        hn = sb("hn", [P, 2, D])
        top = sb("top", [P, 2, 8])
        tops = sb("tops", [P, 2, 8])
        kept = sb("kept", [P, 2, NB + 8 - TOPB])
        nm = sb("nm", [P, 2, P])
        nmT = [sb(f"nmT{r}", [P, T], BF16) for r in two]
        sg = [sb(f"sg{r}", [P, T]) for r in two]
        hm = [sb(f"hm{r}", [P, T]) for r in two]
        comb = [sb(f"comb{r}", [P, 2, E]) for r in two]
        den = sb("den", [P, 2])
        started = sb("started", [P, 5])

        def sems(names):
            return [sem(n) for n in names.split()]

        s_x0, s_x1, s_const, s_mask = sems("s_x0 s_x1 s_const s_mask")
        s_ct, s_cx = sems("s_ct0 s_ct1"), sems("s_cx0 s_cx1")
        s_w = [sem(f"s_w{f}") for f in range(6)]
        s_small = sem("s_small")
        s_bf, s_eq, s_mb = sems("s_bf s_eq s_mb")
        s_fold, s_folded = sems("s_fold s_folded")
        (st_done, mv_done, ve_done, rstd_done, xn_done, xnT_done) = sems(
            "st_done mv_done ve_done rstd_done xn_done xnT_done")
        x_ready = [sem(f"x_ready{f}") for f in range(5)]
        xadd = sem("xadd")
        s_out = sem("s_out")
        uT_done, mx0_done, nmx0_done, sm0_done, ri0_done, pT0_done, aT_done = sems(
            "uT_done mx0_done nmx0_done sm0_done ri0_done pT0_done aT_done")
        q_done, k_done, v_done, mx_done, sub_done, exp_done, pT_done, pv_done, ri_done, hd_done = sems(
            "q_done k_done v_done mx_done sub_done exp_done pT_done pv_done ri_done hd_done")
        xmid = sem("xmid")
        cst_done, cmv_done, cve_done, crs_done, cn_done, cnT_done = sems(
            "cst_done cmv_done cve_done crs_done cn_done cnT_done")
        v2_done, rq_done = sems("v2_done rq_done")
        rt_done, rc_done, rs_done, ro_done = sems("rt_done rc_done rs_done ro_done")
        hst_done, hmv_done, hve_done, hrs_done, hn_done = sems("hst_done hmv_done hve_done hrs_done hn_done")
        lg_done, lmx_done, lsh_done, le_done, top_done, tops_done, kept_done, nm_done, nmT_done = sems(
            "lg_done lmx_done lsh_done le_done top_done tops_done kept_done nm_done nmT_done")
        sig_done, top5_done, tops5_done, den_done, kept5_done, sel_done, rden_done, comb_done = sems(
            "sig_done top5_done tops5_done den_done kept5_done sel_done rden_done comb_done")
        sg_done, hm_done, acc_done = sems("sg_done hm_done acc_done")

        def least(n):
            return max(n, 0) if isinstance(n, int) else n

        def past(n):
            return n + 1

        count_reg = {}

        def apart(eng, n):
            if isinstance(n, int):
                return max(n, 0)
            if eng not in count_reg:
                count_reg[eng] = stack.enter_context(eng.register("count"))
            eng.reg_mov(count_reg[eng], n)
            eng.wait_ge(s_const, 64)
            return count_reg[eng]

        def steps(eng, body):
            body(-1, 1)
            body(0, 0)
            with eng.Fori(1, PAIRS - 2, 2) as t:
                body(t, 1)
                body(t + 1, 0)
            body(PAIRS - 1, 1)
            body(PAIRS, 0)

        def on(t, lo, hi):
            return not isinstance(t, int) or lo <= t <= hi

        PJ_BEFORE = [(1, 1), (2, 2), (2, 1), (2, 2), (4, 3), (1, 1)]
        PJ_AFTER = [(0, 0), (0, 0), (0, 0), (1, 1), (1, 1), (0, 0)]
        PJ_AFTER_D = [(0, 0), (0, 0), (0, 0), (1, 0), (1, 0), (0, 0)]
        PJ_FOLD = 2

        def pj_base(f, b, after=PJ_AFTER):
            n = sum(PAIRS * (PJ_BEFORE[g][b] + after[g][b]) for g in range(f))
            return n + PJ_FOLD * (f >= 3)

        def pj_before(f, b, p, i, after=PJ_AFTER):
            n = pj_base(f, b, after) + PJ_BEFORE[f][b] * p + i
            return n + after[f][b] * (max(p - 2, 0) if isinstance(p, int) else p - 2)

        def pj_after(f, b, p, i, after=PJ_AFTER):
            n = pj_base(f, b, after) + after[f][b] * p + i
            return n + PJ_BEFORE[f][b] * (min(p + 3, PAIRS) if isinstance(p, int) else p + 3)

        def dr_before(f, b, p, i):
            return pj_before(f, b, p, i, PJ_AFTER_D)

        def dr_step(f, b, p):
            done = p - 1 if not isinstance(p, int) else max(p - 1, 0)
            return pj_base(f, b, PJ_AFTER_D) + PJ_BEFORE[f][b] * (p + 1) + PJ_AFTER_D[f][b] * done

        def dr_after(f, b, p, i):
            return pj_after(f, b, p, i, PJ_AFTER_D)

        PER_PAIR = {"sc0": [1, 4, 2, 4, 4, 5], "sc1": [0, 4, 2, 4, 4, 5],
                    "tp0": [1, 4, 2, 4, 4, 5], "tp1": [1, 4, 2, 4, 4, 5],
                    "ov0": [0, 1, 0, 1, 1, 0], "ov1": [0, 1, 0, 1, 1, 0]}

        def use(f, name, p, i=0):
            return PAIRS * sum(PER_PAIR[name][:f]) + PER_PAIR[name][f] * p + i

        ATT = {1: 0, 3: 1, 4: 2}

        def group(f, p, n):
            return PAIRS * 8 * ATT[f] + 8 * p + n

        def pair(f, p):
            return PAIRS * f + p

        def att(f, p):
            return PAIRS * ATT[f] + p

        def landed(p, r):
            return 8 * p + 16 - 8 * r

        def xadds(f, n):
            return PAIRS * (f - 2) + n

        block = stack.enter_context(nc.Block())

        def xp(p):
            return X[:, bass.ds(2 * p, 2), :]

        def xs(p, j):
            return X[:, bass.ds(2 * p + j, 1), :].rearrange("p o d -> p (o d)")

        def heads(ap):
            return ap.rearrange("p (h d) -> p h d", h=H)

        def over(ap, n):
            return ap.unsqueeze(1).to_broadcast([P, n, ap.shape[1]])

        def along(ap, n):
            return ap.unsqueeze(2).to_broadcast([P, ap.shape[1], n])

        def four(name):
            return bank[name][:, :].rearrange("p (a s) -> p a s", a=4)

        @block.sync
        def _(sp):
            sp.dma_start(X[:, 0:2, :], x[:, 0:2, :]).then_inc(s_x0, 16)
            for dst, src in ((idn, ident), (caus, causal), (vecs, vec), (rws, rows)):
                sp.dma_start(dst[:], src).then_inc(s_const, 16)
            for dst, src in ((Wqk, w_qk), (Wov, w_ov)):
                sp.dma_start(dst[:], src).then_inc(s_w[0], 16)
            sp.dma_start(X[:, 2:B, :], x[:, 2:B, :]).then_inc(s_x1, 16)
            for dst, src in ((mask4[:], mask), (tq[:], tokq), (tk, tokk)):
                sp.dma_start(dst, src).then_inc(s_mask, 16)
            for r in two:
                sp.dma_start(cT[r][:], ctxT[:, :, r * T:(r + 1) * T]).then_inc(s_ct[r], 16)
            for dst, src in ((Wq0, w_q0), (Wk0, w_k0), (Wv0, w_v0)):
                sp.dma_start(dst[:], src).then_inc(s_w[1], 16)
            for dst, src in ((Wr0[:], w_r0), (W1[:], w_1), (W2[:], w_2), (expd, expand)):
                sp.dma_start(dst, src).then_inc(s_w[2], 16)
            for dst, src in ((Wqkv, w_qkv), (Wo1, w_o1)):
                sp.dma_start(dst[:], src).then_inc(s_w[3], 16)
            for dst, src in ((Wx, w_x), (lnbs, lnb)):
                sp.dma_start(dst[:], src).then_inc(s_w[4], 16)
            for dst, src in ((Wg, w_g), (Wgate, w_gate), (Wup, w_up), (Wdown, w_down),
                             (Wsg, ws_gate), (Wsu, ws_up), (Wsd, ws_down)):
                sp.dma_start(dst[:], src).then_inc(s_w[5], 16)
            with sp.Fori(2, PAIRS - 1, 2) as p:
                for r in two:
                    sp.wait_ge(filled["pj1"], least(pj_before(1, 1, p + r - 2, 1) + 1))
                    sp.dma_start(cT[r][:], ctxT[:, :, bass.ds((p + r) * T, T)]).then_inc(s_ct[r], 16)
            for r in two:
                sp.dma_start(cx[r][:], ctx[:, 2 * r:2 * r + 2, :]).then_inc(s_cx[r], 16)
            with sp.Fori(2, PAIRS - 1, 2) as p:
                for r in two:
                    sp.wait_ge(cn_done, least(p + r - 1))
                    sp.dma_start(cx[r][:], ctx[:, bass.ds(2 * (p + r), 2), :]).then_inc(s_cx[r], 16)
            for p in range(PAIRS):
                sp.wait_ge(drained["tp1"], use(5, "tp1", p, 4) + 1)
                sp.dma_start(out[:, 2 * p:2 * p + 2, :], X[:, 2 * p:2 * p + 2, :]).then_inc(s_out, 16)
            sp.wait_ge(s_out, 16 * PAIRS)

        @block.tensor
        def _(pe):
            mm = nc.tensor.matmul

            def turn(f, p, r):
                pe.wait_ge(xn_done, pair(f, p) + 1)
                pe.wait_ge(drained["pj0"], least(dr_before(f, 0, p, 0)))
                turn_pair("pj0", xn[r])

            def turn_pair(name, src):
                for c in range(C):
                    for j in two:
                        o = c * T + j * S
                        last = nc.tensor.transpose(bank[name][:, o:o + S], src[:, j, c * P:(c + 1) * P], idn[:])
                last.then_inc(filled[name], 1)

            def across(name, w, act, col=0):
                for o in range(C):
                    for c in range(C):
                        last = mm(bank[name][:, o * T:(o + 1) * T], w[:, c, col + o * P:col + (o + 1) * P],
                                  act[:, c, :], start=c == 0, stop=c == C - 1)
                last.then_inc(filled[name], 1)

            def along_tokens(name, act, w, n=D, col=0):
                for j in two:
                    for c in range(C):
                        last = mm(bank[name][:, j * n:(j + 1) * n], act[:, c, j * S:(j + 1) * S],
                                  w[:, c, col:col + n], start=c == 0, stop=c == C - 1)
                last.then_inc(filled[name], 1)

            pe.wait_ge(s_const, 64)
            pe.wait_ge(s_w[0], 32)

            def body(t, r):
                q = 1 - r
                if on(t, 1, PAIRS):
                    p = t - 1
                    pe.wait_ge(sm0_done, p + 1)
                    for j in two:
                        last = nc.tensor.transpose(bank["tp0"][:, j * S:(j + 1) * S], pr[q][:, j, :], idn[:])
                    last.then_inc(filled["tp0"], 1)
                if on(t, 0, PAIRS - 1):
                    pe.wait_ge(drained["pj1"], dr_before(0, 1, t, 0) + 1)
                    pe.wait_ge(drained["sc0"], least(use(0, "sc0", t)))
                    for j in two:
                        s = slice(j * S, (j + 1) * S)
                        for c in range(C):
                            last = mm(bank["sc0"][:, s], qT[r][:, c, s], xnT[r][:, c, s],
                                      start=c == 0, stop=c == C - 1)
                    last.then_inc(filled["sc0"], 1)
                if on(t, 1, PAIRS):
                    p = t - 1
                    pe.wait_ge(drained["tp0"], use(0, "tp0", p) + 1)
                    for c in range(C):
                        for j in two:
                            o = c * T + j * S
                            last = mm(bank["tp1"][:, o:o + S], xn[q][:, j, c * P:(c + 1) * P], pT[q][:, j, :],
                                      start=True, stop=True)
                    last.then_inc(filled["tp1"], 1)
                    pe.wait_ge(drained["tp1"], use(0, "tp1", p) + 1)
                    pe.wait_ge(x_ready[0], past(p))
                    along_tokens("ov0", cnT[q], Wov)
                if on(t, -1, PAIRS - 2):
                    p = t + 1
                    turn(0, p, q)
                    pe.wait_ge(drained["pj0"], dr_before(0, 0, p, 0) + 1)
                    pe.wait_ge(drained["pj1"], least(dr_before(0, 1, p, 0)))
                    across("pj1", Wqk, xnT[q])

            steps(pe, body)

            def scores(f, p, r, n, masks):
                name, j, g = f"sc{n % 2}", n // 4, n % 4
                pe.wait_ge(drained[name], least(use(f, name, p, n // 2)))
                if masks is not None:
                    mm(bank[name][:, :], idnb[:],
                       masks[:, bass.ds(2 * p + j, 1), :].to_broadcast([P, 4, S]), start=True, stop=False,
                       skip_group_check=True)
                rows32 = slice(32 * g, 32 * g + 32)
                for c in range(C):
                    last = mm(bank[name][:, c * T:(c + 1) * T], qT[r][rows32, c, j * S:(j + 1) * S],
                              kM[r][rows32, c, j, :, :], start=masks is None, stop=True,
                              skip_group_check=True)
                last.then_inc(filled[name], 1)

            def turn_probs(f, p, n):
                name = f"tp{n % 2}"
                pe.wait_ge(exp_done, group(f, p, n) + 1)
                pe.wait_ge(drained[name], least(use(f, name, p, n // 2)))
                for i in range(4):
                    last = nc.tensor.transpose(bank[name][:, i * S:(i + 1) * S], pr[n % 2][:, i, :], idn[:])
                last.then_inc(filled[name], 1)

            def probs_times_values(f, p, r, n):
                j, g = n // 4, n % 4
                pe.wait_ge(drained[f"tp{n % 2}"], use(f, f"tp{n % 2}", p, n // 2) + 1)
                if g == 0:
                    pe.wait_ge(drained[f"ov{j}"], least(use(f, f"ov{j}", p)))
                    if isinstance(p, int) and p == 0 and j == 0 and f != 4:
                        pe.wait_ge(x_ready[f - 1], past(PAIRS))
                for i in range(4):
                    h = 8 * (i // 2) + 2 * g + i % 2
                    last = mm(bank[f"ov{j}"][:, h * (DH + 1):(h + 1) * (DH + 1)], pT[n % 2][:, i, :],
                              va[r][:, j, h, :], start=True, stop=True)
                last.then_inc(pv_done, 1)

            def attention(f, masks, before, after, qkv):
                def body(t, r):
                    q = 1 - r
                    for n in range(8):
                        if on(t, 0, PAIRS - 1):
                            if n == 0:
                                qkv(t)
                            scores(f, t, r, n, masks)
                        if n >= 2 and on(t, 0, PAIRS - 1):
                            turn_probs(f, t, n - 2)
                        if n < 2 and on(t, 1, PAIRS):
                            turn_probs(f, t - 1, n + 6)
                        if n >= 3 and on(t, 0, PAIRS - 1):
                            probs_times_values(f, t, r, n - 3)
                        if n < 3 and on(t, 1, PAIRS):
                            probs_times_values(f, t - 1, q, n + 5)
                        if n in before and on(t, -1, PAIRS - 2):
                            before[n](t + 1, q)
                        if n in after and on(t, 1, PAIRS):
                            after[n](t - 1, q)

                steps(pe, body)

            pe.wait_ge(s_w[1], 48)
            pe.wait_ge(s_mb, 2)
            pe.wait_ge(s_bf, 1)

            def project_q(p, r):
                pe.wait_ge(drained["pj0"], dr_before(1, 0, p, 0) + 1)
                pe.wait_ge(drained["pj1"], least(dr_before(1, 1, p, 0)))
                across("pj1", Wq0, xnT[r])

            def project_k(p, r):
                pe.wait_ge(s_ct[r], landed(p, r))
                pe.wait_ge(drained["pj0"], least(dr_before(1, 0, p, 1)))
                across("pj0", Wk0, cT[r])

            def project_v(p, r):
                pe.wait_ge(drained["pj1"], least(dr_before(1, 1, p, 1)))
                along_tokens("pj1", cT[r], Wv0)

            def ready(p):
                for b in two:
                    pe.wait_ge(drained[f"pj{b}"], least(dr_step(1, b, p)))

            attention(1, mb0, {2: lambda p, r: turn(1, p, r), 3: project_q, 4: project_k, 5: project_v},
                      {}, ready)

            pe.wait_ge(s_w[2], 64)
            pe.wait_ge(s_bf, 2)

            def body(t, r):
                q = 1 - r
                for c in range(FF):
                    if c == 0 and on(t, -1, PAIRS - 2):
                        turn(2, t + 1, q)
                    if c == 2 and on(t, -1, PAIRS - 2):
                        p = t + 1
                        pe.wait_ge(drained["pj0"], dr_before(2, 0, p, 0) + 1)
                        pe.wait_ge(drained["pj1"], least(dr_before(2, 1, p, 0)))
                        along_tokens("pj1", xnT[q], Wr0, NB)
                    if on(t, 0, PAIRS - 1):
                        if c == 0:
                            pe.wait_ge(drained["pj0"], dr_before(2, 0, t, 1) + 1)
                        name = ("sc0", "sc1", "tp0", "tp1")[c % 4]
                        pe.wait_ge(drained[name], least(use(2, name, t, c // 4)))
                        mm(bank[name][:, 0:T], expb[:, c * P:(c + 1) * P], nmT[r][:, :], start=True, stop=False)
                        for d in range(C):
                            last = mm(bank[name][:, 0:T], W1[:, d, c * P:(c + 1) * P], xnT[r][:, d, :],
                                      start=False, stop=d == C - 1)
                        last.then_inc(filled[name], 1)
                    if c in (3, 7) and on(t, 1, PAIRS):
                        j = c // 4
                        if j == 0:
                            pe.wait_ge(drained["tp1"], least(use(2, "tp1", t - 1, 1) + 1))
                            pe.wait_ge(x_ready[2], least(past(t - 1)))
                        for d in range(FF):
                            last = mm(bank["ov0"][:, j * D:(j + 1) * D], hT[q][:, d, j * S:(j + 1) * S],
                                      W2[:, d, :], start=d == 0, stop=d == FF - 1)
                        if j == 1:
                            last.then_inc(filled["ov0"], 1)
                if on(t, -1, PAIRS - 2):
                    p = t + 1
                    pe.wait_ge(nm_done, p + 1)
                    pe.wait_ge(drained["pj0"], least(dr_before(2, 0, p, 1)))
                    for j in two:
                        last = nc.tensor.transpose(bank["pj0"][:, j * S:(j + 1) * S], nm[:, j, :], idn[:])
                    last.then_inc(filled["pj0"], 1)

            steps(pe, body)

            pe.wait_ge(s_w[4], 32)
            for i in range(4):
                name = f"pj{i % 2}"
                pe.wait_ge(drained[name], least(pj_base(3, i % 2, PJ_AFTER_D) - PJ_FOLD + i // 2))
                for c in range(C):
                    last = mm(bank[name][:, 0:D], lnbs[:, i, c, :], Wx[:, i, c, :], start=c == 0, stop=c == C - 1)
                last.then_inc(filled[name], 1)

            pe.wait_ge(s_w[3], 32)

            def project_q(p, r):
                pe.wait_ge(drained["pj0"], dr_before(3, 0, p, 0) + 1)
                pe.wait_ge(drained["pj1"], least(dr_before(3, 1, p, 0)))
                pe.wait_ge(x_ready[3], least(past(p - 2)))
                across("pj1", Wqkv, xnT[r], 0)

            def project_k(p, r):
                pe.wait_ge(drained["pj0"], least(dr_before(3, 0, p, 1)))
                across("pj0", Wqkv, xnT[r], D)

            def project_v(p, r):
                pe.wait_ge(drained["pj1"], least(dr_before(3, 1, p, 1)))
                along_tokens("pj1", xnT[r], Wqkv, D, 2 * D)

            def turn_heads(p, r):
                for j in two:
                    pe.wait_ge(drained[f"ov{j}"], use(3, f"ov{j}", p) + 1)
                pe.wait_ge(drained["pj0"], least(dr_after(3, 0, p, 0)))
                turn_pair("pj0", hd[r])

            def project_out(p, r):
                pe.wait_ge(drained["pj0"], dr_after(3, 0, p, 0) + 1)
                pe.wait_ge(drained["pj1"], least(dr_after(3, 1, p, 0)))
                pe.wait_ge(x_ready[3], past(p))
                along_tokens("pj1", hdT, Wo1)

            def ready(p):
                for b in two:
                    pe.wait_ge(drained[f"pj{b}"], least(dr_step(3, b, p)))

            attention(3, None, {2: lambda p, r: turn(3, p, r), 3: project_q, 4: project_k, 5: project_v},
                      {5: turn_heads, 6: project_out}, ready)

            pe.wait_ge(s_folded, 4)
            pe.wait_ge(s_mb, 3)
            pe.wait_ge(x_ready[3], past(PAIRS))

            def turn_both(p, r):
                turn(4, p, r)
                pe.wait_ge(cn_done, p + 1)
                pe.wait_ge(drained["pj1"], least(dr_before(4, 1, p, 0)))
                pe.wait_ge(x_ready[4], least(past(p - 2)))
                turn_pair("pj1", cn[r])

            def project_qk(p, r):
                pe.wait_ge(drained["pj0"], dr_before(4, 0, p, 0) + 1)
                along_tokens("pj0", xnT[r], Wx[:, 0])
                pe.wait_ge(drained["pj1"], dr_before(4, 1, p, 0) + 1)
                along_tokens("pj1", cnT[r], Wx[:, 1])

            def project_v(p, r):
                pe.wait_ge(drained["pj0"], least(dr_before(4, 0, p, 2)))
                along_tokens("pj0", cnT[r], Wx[:, 2])

            def turn_rotated(p, r):
                pe.wait_ge(ro_done, 2 * p + 2)
                pe.wait_ge(drained["pj1"], least(dr_before(4, 1, p, 2)))
                turn_pair("pj1", ro[:, 0])
                pe.wait_ge(drained["pj0"], least(dr_before(4, 0, p, 3)))
                turn_pair("pj0", ro[:, 1])

            def turn_heads(p, r):
                pe.wait_ge(hn_done, p + 1)
                pe.wait_ge(drained["pj0"], least(dr_after(4, 0, p, 0)))
                turn_pair("pj0", hn)

            def project_out(p, r):
                pe.wait_ge(drained["pj0"], dr_after(4, 0, p, 0) + 1)
                pe.wait_ge(drained["pj1"], least(dr_after(4, 1, p, 0)))
                pe.wait_ge(x_ready[4], past(p))
                along_tokens("pj1", hdT, Wx[:, 3])

            def ready(p):
                for b in two:
                    pe.wait_ge(drained[f"pj{b}"], least(dr_step(4, b, p)))

            def last_slot(p, r):
                turn_heads(p, r)
                project_out(p, r)

            attention(4, mb1, {2: turn_both, 3: project_qk, 4: project_v, 7: turn_rotated},
                      {7: last_slot}, ready)

            pe.wait_ge(s_w[5], 7 * 16)

            def up(t, r, e):
                name = f"sc{e % 2}"
                if isinstance(t, int) and t == 0 and e < 2:
                    pe.wait_ge(drained[name], least(use(5, name, 0)))
                else:
                    pe.wait_ge(hm_done, least(10 * t + e - 1))
                for i, w in enumerate((Wgate, Wup) if e < E else (Wsg, Wsu)):
                    o = e * P if e < E else (e - E) * P
                    for c in range(C):
                        last = mm(bank[name][:, i * T:(i + 1) * T], w[:, c, o:o + P], xnT[r][:, c, :],
                                  start=c == 0, stop=c == C - 1)
                last.then_inc(filled[name], 1)

            def down(t, e):
                name = f"tp{e % 2}"
                pe.wait_ge(hm_done, 10 * t + e + 1)
                pe.wait_ge(drained[name], least(use(5, name, t, e // 2)))
                w = Wdown[:, e, :] if e < E else Wsd[:, e - E, :]
                for j in two:
                    last = mm(bank[name][:, j * D:(j + 1) * D], hm[e % 2][:, j * S:(j + 1) * S], w,
                              start=True, stop=True)
                last.then_inc(filled[name], 1)

            def body(t, r):
                q = 1 - r
                if on(t, 0, PAIRS - 1):
                    pe.wait_ge(drained["pj0"], dr_before(5, 0, t, 0) + 1)
                for e in range(E + SH):
                    if on(t, 0, PAIRS - 1):
                        up(t, r, e)
                        if e >= 2:
                            down(t, e - 2)
                    if on(t, 1, PAIRS) and e < 2:
                        down(t - 1, E + SH - 2 + e)
                    if e == 3 and on(t, -1, PAIRS - 2):
                        turn(5, t + 1, q)
                    if e == 5 and on(t, -1, PAIRS - 2):
                        pe.wait_ge(drained["pj0"], dr_before(5, 0, t + 1, 0) + 1)
                        if isinstance(t, int) and t == -1:
                            pe.wait_ge(drained["pj1"], least(dr_before(5, 1, 0, 0)))
                            pe.wait_ge(x_ready[4], past(PAIRS))
                        else:
                            pe.wait_ge(sig_done, t + 1)
                        along_tokens("pj1", xnT[q], Wg, E)

            steps(pe, body)

        @block.vector
        def _(dve):
            v = nc.vector

            def stats(src, b, m, s_b, s_m, n):
                for j in two:
                    last = v.bn_stats(b[:, j, :], src(j))
                last.then_inc(s_b, 1)
                dve.wait_ge(s_b, apart(dve, n + 1))
                for j in two:
                    last = v.bn_aggr(m[:, j, :], b[:, j, :])
                last.then_inc(s_m, 1)

            def x_stats(f, p, r):
                if f == 0:
                    dve.wait_ge(s_x0 if isinstance(p, int) and p == 0 else s_x1, 16)
                else:
                    dve.wait_ge(x_ready[f - 1], past(p + 1))
                stats(lambda j: xs(p, j), bst[r], mv[r], st_done, mv_done, pair(f, p))

            def normalise(dst, src, m, s, done):
                for j in two:
                    last = v.tensor_scalar(dst[:, j, :], src(j), m[:, j, 0:1], s[:, j:j + 1],
                                           ALU.subtract, ALU.mult)
                last.then_inc(done, 1)

            def x_norm(f, p, r):
                if f == 4:
                    dve.wait_ge(rq_done, p + 1)
                else:
                    dve.wait_ge(rstd_done, pair(f, p) + 1)
                if f == 3:
                    dve.wait_ge(xadd, least(xadds(3, p - 1)))
                normalise(xn[r], lambda j: xs(p, j), mv[r], rq[r] if f == 4 else rstd[r], xn_done)

            for f in (0, 2, 3, 4):
                v.memset(started[:, f:f + 1], 0.0).then_inc(x_ready[f], 1)
            dve.wait_ge(s_const, 64)
            v.tensor_copy(idnb[:], idn[:]).then_inc(s_bf, 1)

            def body(t, r):
                q = 1 - r
                if on(t, -1, PAIRS - 2):
                    x_stats(0, t + 1, q)
                if on(t, 0, PAIRS - 1):
                    dve.wait_ge(filled["sc0"], use(0, "sc0", t) + 1)
                    v.tensor_tensor(sh[r][:, 0:2, :], bank["sc0"][:, 0:T].rearrange("p (j s) -> p j s", j=2),
                                    over(caus[:], 2), ALU.add).then_inc(drained["sc0"], 1)
                    dve.wait_ge(drained["sc0"], use(0, "sc0", t) + 1)
                    v.tensor_reduce(mx[r][:, 0:2], sh[r][:, 0:2, :], AX.X, ALU.max).then_inc(mx0_done, 1)
                    dve.wait_ge(mx0_done, t + 1)
                    v.tensor_scalar(nmx[r][:, 0:2], mx[r][:, 0:2], -1.0 / 16.0, None, ALU.mult).then_inc(nmx0_done, 1)
                if on(t, 1, PAIRS):
                    p = t - 1
                    dve.wait_ge(sm0_done, p + 1)
                    v.reciprocal(rin[q][:, 0:2], rsum[q][:, 0:2]).then_inc(ri0_done, 1)
                if on(t, -1, PAIRS - 2):
                    if on(t, 1, PAIRS):
                        dve.wait_ge(filled["tp1"], least(use(0, "tp1", t - 1) + 1))
                    x_norm(0, t + 1, q)
                if on(t, 1, PAIRS):
                    p = t - 1
                    dve.wait_ge(ri0_done, p + 1)
                    dve.wait_ge(filled["ov0"], p + 1)
                    for j in two:
                        last = v.scalar_tensor_tensor(xs(p, j), bank["ov0"][:, j * D:(j + 1) * D],
                                                      rin[q][:, j:j + 1], xs(p, j), ALU.mult, ALU.add)
                    last.then_inc(x_ready[0], 1)

            steps(dve, body)

            dve.wait_ge(s_mask, 48)
            v.tensor_scalar(mb0[:], mask8, -4.0e7, None, ALU.mult).then_inc(s_mb, 1)
            v.tensor_reduce(allm[:], mask8, AX.X, ALU.min).then_inc(s_eq, 1)
            dve.wait_ge(s_eq, 1)
            v.tensor_scalar(scl0[:], allm[:], -0.25, 0.25, ALU.mult, ALU.add).then_inc(s_mb, 1)
            v.tensor_tensor(mb1[:], tk, along(tq[:], S), ALU.not_equal).then_inc(s_eq, 1)
            dve.wait_ge(s_eq, 2)
            v.scalar_tensor_tensor(mb1[:], mb1[:], NEG, over(caus[:], B), ALU.mult, ALU.add).then_inc(s_mb, 1)

            def less_max(f, p, n):
                name, i = f"sc{n % 2}", n % 2
                dve.wait_ge(filled[name], use(f, name, p, n // 2) + 1)
                v.tensor_reduce(mx[i][:, :], four(name), AX.X, ALU.max).then_inc(mx_done, 1)
                dve.wait_ge(mx_done, group(f, p, n) + 1)
                dve.wait_ge(exp_done, least(group(f, p, n) - 1))
                v.tensor_tensor(sh[i][:], four(name), along(mx[i][:, :], S), ALU.subtract).then_inc(drained[name], 1)

            def norm_heads(f, p, r, j):
                ob = bank[f"ov{j}"][:, 0:H * (DH + 1)].rearrange("p (h d) -> p h d", h=H)
                dve.wait_ge(pv_done, least(group(f, p, 4 * j + 4)))
                v.reciprocal(rin[j][:], ob[:, :, DH:DH + 1].rearrange("p h o -> p (h o)")).then_inc(ri_done, 1)
                dve.wait_ge(ri_done, 2 * att(f, p) + j + 1)
                v.tensor_tensor(heads(hd[r][:, j, :]), ob[:, :, 0:DH], along(rin[j][:], DH),
                                ALU.mult).then_inc(drained[f"ov{j}"], 1)

            def masked_keys(name, r, bias, done):
                for o in range(C):
                    src = bank[name][:, o * T:(o + 1) * T].rearrange("p (j s) -> p j s", j=2)
                    for i, m in enumerate(("even", "odd")):
                        if bias:
                            last = v.tensor_scalar(kM[r][:, o, :, i, :], src, V(bias, o), V(m), ALU.add, ALU.mult)
                        else:
                            last = v.tensor_scalar(kM[r][:, o, :, i, :], src, V(m), None, ALU.mult)
                last.then_inc(done, 1)

            def values(name, r, bias):
                for j in two:
                    last = v.tensor_tensor(va[r][:, j, :, 0:DH], heads(bank[name][:, j * D:(j + 1) * D]),
                                           heads(bias), ALU.add)
                last.then_inc(drained[name], 1)

            def add_to_x(name, p, done, n):
                dve.wait_ge(xadd, n)
                v.tensor_tensor(xp(p), bank[name][:, :].rearrange("p (j d) -> p j d", j=2), xp(p),
                                ALU.add).then_inc(done, 1)

            def attention(f, before, after, norm_after):
                def body(t, r):
                    q = 1 - r
                    for n in range(8):
                        if on(t, 0, PAIRS - 1):
                            less_max(f, t, n)
                        if n == 0 and on(t, -1, PAIRS - 2):
                            x_stats(f, t + 1, q)
                        if n == 1 and on(t, -1, PAIRS - 2):
                            x_norm(f, t + 1, q)
                        if n == 3 and on(t, 1, PAIRS):
                            norm_heads(f, t - 1, q, 1)
                        if n in before and on(t, -1, PAIRS - 2):
                            before[n](t + 1, q)
                        if n in after and on(t, 1, PAIRS):
                            after[n](t - 1, q)
                        if n == 7 and on(t, 0, PAIRS - 1):
                            norm_after(t)
                            norm_heads(f, t, r, 0)

                steps(dve, body)

            def keys(p, r):
                dve.wait_ge(filled["pj0"], pj_before(1, 0, p, 1) + 1)
                masked_keys("pj0", r, "bk0", drained["pj0"])

            def vals(p, r):
                dve.wait_ge(filled["pj1"], pj_before(1, 1, p, 1) + 1)
                values("pj1", r, R("bv0"))

            attention(1, {5: keys, 6: vals}, {}, lambda t: dve.wait_ge(x_ready[1], least(past(t - 1))))

            dve.wait_ge(s_w[2], 64)
            v.tensor_copy(expb[:], expd).then_inc(s_bf, 1)

            def body(t, r):
                q = 1 - r
                p = t + 1
                if on(t, -1, PAIRS - 2):
                    x_stats(2, p, q)
                    x_norm(2, p, q)
                    dve.wait_ge(filled["pj1"], pj_before(2, 1, p, 0) + 1)
                    v.tensor_tensor(lg[:], bank["pj1"][:, 0:2 * NB].rearrange("p (j e) -> p j e", j=2),
                                    over(R("br"), 2), ALU.add).then_inc(drained["pj1"], 1)
                    dve.wait_ge(drained["pj1"], dr_before(2, 1, p, 0) + 1)
                    v.tensor_reduce(lmx[:], lg[:], AX.X, ALU.max).then_inc(lmx_done, 1)
                    dve.wait_ge(lmx_done, p + 1)
                    v.tensor_tensor(lsh[:], lg[:], along(lmx[:], NB), ALU.subtract).then_inc(lsh_done, 1)
                    dve.wait_ge(le_done, apart(dve, p + 1))
                    for j in two:
                        last = v.max(top[:, j, :], le[:, j, :])
                    last.then_inc(top_done, 1)
                    dve.wait_ge(top_done, p + 1)
                    v.tensor_copy(tops[:, :, 0:TOPB], top[:, :, 0:TOPB]).then_inc(tops_done, 1)
                    dve.wait_ge(tops_done, apart(dve, p + 1))
                    for j in two:
                        last = v.match_replace(kept[:, j, :], tops[:, j, :], le[:, j, :], -2.0)
                    last.then_inc(kept_done, 1)
                    dve.wait_ge(kept_done, p + 1)
                    v.tensor_scalar(nm[:, :, 0:NB], kept[:, :, 0:NB], -1.5, None, ALU.is_gt).then_inc(nm_done, 1)
                if on(t, 1, PAIRS):
                    dve.wait_ge(filled["ov0"], PAIRS + t)
                    add_to_x("ov0", t - 1, x_ready[2], xadds(2, t))

            steps(dve, body)

            for i, name in enumerate(("bxq", "bxk", "bxv", "bxo")):
                dve.wait_ge(filled[f"pj{i % 2}"], pj_base(3, i % 2) - PJ_FOLD + i // 2 + 1)
                v.tensor_tensor(bias4[:, i, :], bank[f"pj{i % 2}"][:, 0:D], R(name),
                                ALU.add).then_inc(drained[f"pj{i % 2}"], 1)

            def keys(p, r):
                dve.wait_ge(filled["pj0"], pj_before(3, 0, p, 1) + 1)
                masked_keys("pj0", r, "bk1", drained["pj0"])

            def vals(p, r):
                dve.wait_ge(filled["pj1"], pj_before(3, 1, p, 1) + 1)
                values("pj1", r, R("bv1"))

            def residual(p, r):
                dve.wait_ge(filled["pj1"], pj_after(3, 1, p, 0) + 1)
                add_to_x("pj1", p, x_ready[3], xadds(3, p + 1))

            attention(3, {5: keys, 6: vals}, {7: residual}, lambda t: None)

            def cs(r):
                return lambda j: cx[r][:, j, :]

            def ctx_stats(p, r):
                dve.wait_ge(s_cx[r], landed(p, r))
                stats(cs(r), cbst[r], cmv[r], cst_done, cmv_done, p)

            def ctx_norm(p, r):
                dve.wait_ge(crs_done, p + 1)
                normalise(cn[r], cs(r), cmv[r], crs[r], cn_done)

            def biased(p, r):
                for i in two:
                    dve.wait_ge(filled[f"pj{i}"], pj_before(4, i, p, 1) + 1)
                    dve.wait_ge(rc_done, 2 * p)
                    v.tensor_tensor(rt[:, i], bank[f"pj{i}"][:, :].rearrange("p (j d) -> p j d", j=2),
                                    over(bias4[:, i, :], 2), ALU.add).then_inc(drained[f"pj{i}"], 1)

            def swapped(p, r):
                for i, name in enumerate(("sinq", "sink")):
                    dve.wait_ge(drained[f"pj{i}"], dr_before(4, i, p, 1) + 1)
                    dve.wait_ge(ro_done, 2 * p)
                    src = rt[:, i].rearrange("p j (h d) -> p (j h) d", d=DH)
                    dst = rs[:, i].rearrange("p j (h d) -> p (j h) d", d=DH)
                    sine = over(R(name), 2 * H)
                    v.tensor_tensor(dst[:, :, 0:DH:2], src[:, :, 1:DH:2], sine[:, :, 0:DH:2], ALU.mult)
                    v.tensor_tensor(dst[:, :, 1:DH:2], src[:, :, 0:DH:2], sine[:, :, 1:DH:2],
                                    ALU.mult).then_inc(rs_done, 1)

            def vals(p, r):
                dve.wait_ge(filled["pj0"], pj_before(4, 0, p, 2) + 1)
                values("pj0", r, bias4[:, 2, :])

            def keys(p, r):
                dve.wait_ge(filled["pj0"], pj_before(4, 0, p, 3) + 1)
                masked_keys("pj0", r, None, drained["pj0"])

            def head_stats(p, r):
                for j in two:
                    dve.wait_ge(drained[f"ov{j}"], use(4, f"ov{j}", p) + 1)
                stats(lambda j: hd[r][:, j, :], hst, hmv, hst_done, hmv_done, p)

            def head_norm(p, r):
                dve.wait_ge(hrs_done, p + 1)
                normalise(hn, lambda j: hd[r][:, j, :], hmv, hrs, hn_done)

            def residual(p, r):
                dve.wait_ge(filled["pj1"], pj_after(4, 1, p, 0) + 1)
                add_to_x("pj1", p, x_ready[4], xadds(4, p + 1))

            attention(4, {0: ctx_stats, 1: ctx_norm, 4: biased, 5: lambda p, r: (swapped(p, r), vals(p, r)),
                          7: keys},
                      {3: head_stats, 4: head_norm, 7: residual}, lambda t: None)

            def body(t, r):
                q = 1 - r
                for e in range(E + SH):
                    if on(t, 0, PAIRS - 1):
                        dve.wait_ge(sg_done, 10 * t + e + 1)
                        dve.wait_ge(filled[f"tp{e % 2}"], least(use(5, f"tp{e % 2}", t, e // 2)))
                        v.tensor_tensor(hm[e % 2][:], sg[e % 2][:], bank[f"sc{e % 2}"][:, T:2 * T],
                                        ALU.mult).then_inc(hm_done, 1)
                    if e >= 2 and on(t, 0, PAIRS - 1):
                        accumulate(t, r, e - 2)
                    if e < 2 and on(t, 1, PAIRS):
                        accumulate(t - 1, q, E + SH - 2 + e)
                    p = t + 1
                    if e == 2 and on(t, -1, PAIRS - 2):
                        x_stats(5, p, q)
                    if e == 3 and on(t, -1, PAIRS - 2):
                        x_norm(5, p, q)
                    if e == 6 and on(t, -1, PAIRS - 2):
                        weights(p, q)

            def accumulate(p, r, e):
                name = f"tp{e % 2}"
                dve.wait_ge(filled[name], use(5, name, p, e // 2) + 1)
                if e:
                    other = f"tp{(e - 1) % 2}"
                    dve.wait_ge(drained[other], least(use(5, other, p, (e - 1) // 2) + 1))
                if e < E:
                    for j in two:
                        last = v.scalar_tensor_tensor(xs(p, j), bank[name][:, j * D:(j + 1) * D],
                                                      comb[r][:, j, e:e + 1], xs(p, j), ALU.mult, ALU.add)
                else:
                    last = v.tensor_tensor(xp(p), bank[name][:, :].rearrange("p (j d) -> p j d", j=2), xp(p),
                                           ALU.add)
                last.then_inc(drained[name], 1)

            def weights(p, r):
                dve.wait_ge(sig_done, apart(dve, p + 1))
                for j in two:
                    last = v.max(top[:, j, :], ls[:, j, :])
                last.then_inc(top5_done, 1)
                dve.wait_ge(top5_done, p + 1)
                v.tensor_copy(tops5[:, :, 0:TOPE], top[:, :, 0:TOPE]).then_inc(tops5_done, 1)
                v.tensor_reduce(den[:], top[:, :, 0:TOPE], AX.X, ALU.add).then_inc(den_done, 1)
                dve.wait_ge(tops5_done, apart(dve, p + 1))
                for j in two:
                    last = v.match_replace(kept5[:, j, :], tops5[:, j, :], ls[:, j, :], -2.0)
                last.then_inc(kept5_done, 1)
                dve.wait_ge(den_done, p + 1)
                v.tensor_scalar(deni[:], den[:], 1e-20, None, ALU.add).then_inc(sel_done, 1)
                dve.wait_ge(kept5_done, p + 1)
                v.scalar_tensor_tensor(sel[:], kept5[:, :, 0:E], -1.5, ls[:, :, 0:E], ALU.is_lt,
                                       ALU.mult).then_inc(sel_done, 1)
                dve.wait_ge(sel_done, 2 * p + 2)
                v.reciprocal(rden[:], deni[:]).then_inc(rden_done, 1)
                dve.wait_ge(rden_done, p + 1)
                for j in two:
                    last = v.tensor_scalar(comb[r][:, j, :], sel[:, j, :], rden[:, j:j + 1], ROUTE_SCALE,
                                           ALU.mult, ALU.mult)
                last.then_inc(comb_done, 1)

            steps(dve, body)

        @block.scalar
        def _(act):
            a = nc.scalar.activation

            def copy_out(name, dst, n):
                act.wait_ge(filled[name], n + 1)
                src = bank[name][:, 0:int(np.prod(dst.shape[1:]))]
                if len(dst.shape) == 3:
                    src = src.rearrange("p (a b) -> p a b", b=dst.shape[-1])
                a(dst, src, ACT.Copy).then_inc(drained[name], 1)

            def body(t, r):
                q = 1 - r
                p = t - 1
                if on(t, 1, PAIRS):
                    copy_out("tp0", pT[q][:, 0:2, :], use(0, "tp0", p))
                if on(t, 0, PAIRS - 1):
                    act.wait_ge(nmx0_done, t + 1)
                    for j in two:
                        last = a(pr[r][:, j, :], sh[r][:, j, :], ACT.Exp, bias=nmx[r][:, j:j + 1], scale=1.0 / 16.0,
                                 accum_out=rsum[r][:, j:j + 1])
                    last.then_inc(sm0_done, 1)
                if on(t, 1, PAIRS):
                    copy_out("tp1", cnT[q][:], use(0, "tp1", p))
                if on(t, -1, PAIRS - 2):
                    copy_out("pj0", xnT[q][:], pj_before(0, 0, t + 1, 0))
                    copy_out("pj1", qT[q][:], pj_before(0, 1, t + 1, 0))

            steps(act, body)

            def attention(f, scale, before, after):
                def exps(p, n):
                    i = n % 2
                    act.wait_ge(drained[f"sc{i}"], use(f, f"sc{i}", p, n // 2) + 1)
                    free = use(f, f"tp{i}", p, n // 2)
                    act.wait_ge(filled[f"tp{i}"], apart(act, free) if f == 1 else least(free))
                    a(pr[i][:], sh[i][:], ACT.Exp, scale=scale(p, n // 4)).then_inc(exp_done, 1)

                def probs_out(p, n):
                    act.wait_ge(pv_done, least(group(f, p, n) - 1))
                    name = f"tp{n % 2}"
                    act.wait_ge(filled[name], use(f, name, p, n // 2) + 1)
                    a(pT[n % 2][:], four(name), ACT.Copy).then_inc(drained[name], 1)

                def body(t, r):
                    q = 1 - r
                    for n in range(8):
                        if on(t, 0, PAIRS - 1):
                            exps(t, n)
                        if n >= 2 and on(t, 0, PAIRS - 1):
                            probs_out(t, n - 2)
                        if n < 2 and on(t, 1, PAIRS):
                            probs_out(t - 1, n + 6)
                        if n in before and on(t, -1, PAIRS - 2):
                            before[n](t + 1, q)
                        if n in after and on(t, 1, PAIRS):
                            after[n](t - 1, q)

                steps(act, body)

            def queries(f, bias):
                def part(p, r):
                    act.wait_ge(filled["pj1"], pj_before(f, 1, p, 0) + 1)
                    for o in range(C):
                        last = a(qT[r][:, o, :], bank["pj1"][:, o * T:(o + 1) * T], ACT.Identity, bias=V(bias, o))
                    last.then_inc(drained["pj1"], 1)
                return part

            act.wait_ge(s_mb, 2)
            attention(1, lambda p, j: scl0[:, bass.ds(2 * p + j, 1)],
                      {2: lambda p, r: copy_out("pj0", xnT[r][:], pj_before(1, 0, p, 0)),
                       3: queries(1, "bq0")}, {})

            def body(t, r):
                q = 1 - r
                p = t + 1
                for c in range(FF):
                    if on(t, 0, PAIRS - 1):
                        name = ("sc0", "sc1", "tp0", "tp1")[c % 4]
                        act.wait_ge(filled[name], use(2, name, t, c // 4) + 1)
                        a(hT[r][:, c, :], bank[name][:, 0:T], ACT.Relu, bias=V("b1", c)).then_inc(drained[name], 1)
                    if c == 1 and on(t, -1, PAIRS - 2):
                        copy_out("pj0", xnT[q][:], pj_before(2, 0, p, 0))
                    if c == 5 and on(t, -1, PAIRS - 2):
                        act.wait_ge(lsh_done, p + 1)
                        a(le[:, :, 0:NB], lsh[:], ACT.Exp).then_inc(le_done, 1)
                if on(t, -1, PAIRS - 2):
                    copy_out("pj0", nmT[q][:, :], pj_before(2, 0, p, 1))

            steps(act, body)

            attention(3, lambda p, j: 1.0 / 16.0,
                      {2: lambda p, r: copy_out("pj0", xnT[r][:], pj_before(3, 0, p, 0)), 3: queries(3, "bq1")},
                      {5: lambda p, r: copy_out("pj0", hdT[:], pj_after(3, 0, p, 0))})

            def both(p, r):
                copy_out("pj0", xnT[r][:], pj_before(4, 0, p, 0))
                copy_out("pj1", cnT[r][:], pj_before(4, 1, p, 0))

            attention(4, lambda p, j: 0.25,
                      {2: both, 7: lambda p, r: copy_out("pj1", qT[r][:], pj_before(4, 1, p, 2))},
                      {7: lambda p, r: copy_out("pj0", hdT[:], pj_after(4, 0, p, 0))})

            def body(t, r):
                q = 1 - r
                p = t + 1
                for e in range(E + SH):
                    if on(t, 0, PAIRS - 1):
                        act.wait_ge(filled[f"sc{e % 2}"], use(5, f"sc{e % 2}", t, e // 2) + 1)
                        act.wait_ge(hm_done, least(10 * t + e - 1))
                        a(sg[e % 2][:], bank[f"sc{e % 2}"][:, 0:T], ACT.Silu).then_inc(sg_done, 1)
                    if e == 3 and on(t, -1, PAIRS - 2):
                        copy_out("pj0", xnT[q][:], pj_before(5, 0, p, 0))
                    if e == 5 and on(t, -1, PAIRS - 2):
                        act.wait_ge(filled["pj1"], pj_before(5, 1, p, 0) + 1)
                        act.wait_ge(comb_done, p)
                        a(ls[:, :, 0:E], bank["pj1"][:, 0:2 * E].rearrange("p (j e) -> p j e", j=2),
                          ACT.Sigmoid).then_inc(sig_done, 1)

            steps(act, body)

        @block.gpsimd
        def _(pool):
            g = nc.gpsimd
            g.memset(started[:, 1:2], 0.0).then_inc(x_ready[1], 1)
            g.memset(mhalf[:], -0.5).then_inc(s_small, 1)
            for r in two:
                g.memset(va[r][:, :, :, DH:DH + 1], 1.0).then_inc(s_small, 1)
            g.memset(nm[:], 0.0).then_inc(s_small, 1)
            g.memset(tops[:], -1.0).then_inc(s_small, 1)
            g.memset(tops5[:], -1.0).then_inc(s_small, 1)
            g.memset(le[:], -1.0).then_inc(s_small, 1)
            g.memset(ls[:], -1.0).then_inc(s_small, 1)
            pool.wait_ge(s_small, 1)

            def inverse(m, e, dst, s_in, s_mid, s_out_, n):
                pool.wait_ge(s_in, apart(pool, n + 1))
                g.tensor_scalar(e[:], m[:, :, 1:2].rearrange("p j o -> p (j o)"), EPS, None, ALU.add).then_inc(s_mid, 1)
                pool.wait_ge(s_mid, apart(pool, n + 1))
                g.tensor_tensor(dst[:], e[:], mhalf[:, 0:2], ALU.pow).then_inc(s_out_, 1)

            def x_inverse(f, p, r):
                inverse(mv[r], ve[r], rstd[r], mv_done, ve_done, rstd_done, pair(f, p))

            def body(t, r):
                if on(t, -1, PAIRS - 2):
                    x_inverse(0, t + 1, 1 - r)

            steps(pool, body)

            def body(t, r):
                q = 1 - r
                if on(t, -1, PAIRS - 2):
                    x_inverse(1, t + 1, q)
                if on(t, 1, PAIRS):
                    for j in two:
                        pool.wait_ge(drained[f"ov{j}"], apart(pool, use(1, f"ov{j}", t - 1) + 1))
                    g.tensor_tensor(xp(t - 1), xp(t - 1), hd[q][:], ALU.add).then_inc(x_ready[1], 1)

            steps(pool, body)

            def body(t, r):
                if on(t, -1, PAIRS - 2):
                    x_inverse(2, t + 1, 1 - r)
                    pool.wait_ge(xn_done, apart(pool, pair(2, t + 1) + 1))
                    g.tensor_tensor(xp(t + 1), xp(t + 1), over(R("b2"), 2), ALU.add).then_inc(xadd, 1)

            steps(pool, body)

            for i, name in enumerate(("gq", "gk", "gv", "go")):
                pool.wait_ge(filled[f"pj{i % 2}"], pj_base(3, i % 2) - PJ_FOLD + i // 2 + 1)
                for c in range(C):
                    last = g.tensor_scalar(Wx[:, i, c, :], Wx[:, i, c, :], V(name, c), None, ALU.mult)
                last.then_inc(s_folded, 1)

            def body(t, r):
                q = 1 - r
                p = t + 1
                if on(t, -1, PAIRS - 2):
                    x_inverse(3, p, q)
                    pool.wait_ge(xn_done, apart(pool, pair(3, p) + 1))
                    g.tensor_tensor(xp(p), xp(p), xn[q][:], ALU.add).then_inc(xmid, 1)
                    pool.wait_ge(xmid, apart(pool, p + 1))
                    g.tensor_tensor(xp(p), xp(p), over(R("bo1"), 2), ALU.add).then_inc(xadd, 1)

            steps(pool, body)

            def body(t, r):
                q = 1 - r
                p = t + 1
                if on(t, -1, PAIRS - 2):
                    x_inverse(4, p, q)
                    pool.wait_ge(rstd_done, apart(pool, pair(4, p) + 1))
                    g.tensor_tensor(v2[q][:], rstd[q][:], rstd[q][:], ALU.mult).then_inc(v2_done, 1)
                    pool.wait_ge(v2_done, apart(pool, 4 * p + 1))
                    g.tensor_tensor(v3[q][:], v2[q][:], mv[q][:, :, 1:2].rearrange("p j o -> p (j o)"),
                                    ALU.mult).then_inc(v2_done, 1)
                    pool.wait_ge(v2_done, apart(pool, 4 * p + 2))
                    g.tensor_scalar(v4[q][:], v3[q][:], EPS, None, ALU.add).then_inc(v2_done, 1)
                    pool.wait_ge(v2_done, apart(pool, 4 * p + 3))
                    g.tensor_tensor(v5[q][:], v4[q][:], mhalf[:, 0:2], ALU.pow).then_inc(v2_done, 1)
                    pool.wait_ge(v2_done, apart(pool, 4 * p + 4))
                    g.tensor_tensor(rq[q][:], v5[q][:], rstd[q][:], ALU.mult).then_inc(rq_done, 1)
                    inverse(cmv[q], cve[q], crs[q], cmv_done, cve_done, crs_done, p)
                    pool.wait_ge(xn_done, apart(pool, pair(4, p) + 1))
                    g.tensor_tensor(xp(p), xp(p), over(bias4[:, 3, :], 2), ALU.add).then_inc(xadd, 1)
                if on(t, 1, PAIRS):
                    inverse(hmv, hve, hrs, hmv_done, hve_done, hrs_done, t - 1)
                if on(t, -1, PAIRS - 2):
                    for i, name in enumerate(("cosq", "cosk")):
                        pool.wait_ge(drained[f"pj{i}"], apart(pool, dr_before(4, i, p, 1) + 1))
                        g.tensor_tensor(rc[:, i].rearrange("p j (h d) -> p (j h) d", d=DH),
                                        rt[:, i].rearrange("p j (h d) -> p (j h) d", d=DH),
                                        over(R(name), 2 * H), ALU.mult).then_inc(rc_done, 1)
                    for i in two:
                        pool.wait_ge(rc_done, apart(pool, 2 * p + i + 1))
                        pool.wait_ge(rs_done, apart(pool, 2 * p + i + 1))
                        g.tensor_tensor(ro[:, i], rc[:, i], rs[:, i], ALU.add).then_inc(ro_done, 1)

            steps(pool, body)

            def body(t, r):
                if on(t, -1, PAIRS - 2):
                    x_inverse(5, t + 1, 1 - r)

            steps(pool, body)



def kernel(**inputs):
    import concourse.bacc as bacc
    from concourse.bass_utils import run_bass_kernel_spmd

    g = {k: np.asarray(v) for k, v in inputs.items()}

    def tok(a):
        return a.transpose(1, 0, 2)

    def chunks(w):
        return w.reshape(-1, P, w.shape[1]).transpose(1, 0, 2)

    def cols(a):
        return a.reshape(-1, P).T

    def rep(a):
        return np.broadcast_to(a.reshape(1, -1), (P, a.size))

    one = np.float32
    inv = (one(1.0) / one(10000.0) ** (np.arange(0, DH, 2, dtype=np.float32) / one(DH))).astype(one)
    at = np.arange(S, dtype=np.float32)
    sign = np.where(np.arange(DH) % 2, 1.0, -1.0).astype(one)

    def angles(pos):
        return np.repeat((pos[:, None] * inv[None, :]).astype(one), 2, axis=1).astype(np.float64)

    aq, ak = angles(at - S // 2), angles(at)
    half = (np.arange(P) // DH) % 2
    vec = {"bq0": cols(g["L0_xattn_bq"]), "bk0": cols(g["L0_xattn_bk"]), "b1": cols(g["L0_ffn_b1"]),
           "bq1": cols(g["L1_attn_b_qkv"][:D]), "bk1": cols(g["L1_attn_b_qkv"][D:2 * D]),
           "gq": cols(g["L1_xattn_ln_q_w"]), "gk": cols(g["L1_xattn_ln_k_w"]),
           "gv": cols(g["L1_xattn_ln_v_w"]), "go": cols(g["L1_xattn_ln_o_w"]),
           "even": (half == 0).astype(one)[:, None], "odd": (half == 1).astype(one)[:, None]}
    rows = {"bv0": rep(g["L0_xattn_bv"]), "br": rep(g["L0_ffn_b_router"]), "b2": rep(g["L0_ffn_b2"]),
            "bv1": rep(g["L1_attn_b_qkv"][2 * D:]), "bo1": rep(g["L1_attn_b_o"]),
            "bxq": rep(g["L1_xattn_b_q"]), "bxk": rep(g["L1_xattn_b_k"]),
            "bxv": rep(g["L1_xattn_b_v"]), "bxo": rep(g["L1_xattn_b_o"]),
            "cosq": np.cos(aq).astype(one), "sinq": (np.sin(aq) * sign).astype(one),
            "cosk": np.cos(ak).astype(one), "sink": (np.sin(ak) * sign).astype(one)}
    expand = np.zeros((P, FF * P), one)
    for b in range(NB):
        expand[b, b * BLOCK:(b + 1) * BLOCK] = NEG
    causal = np.where(np.tril(np.ones((S, S), bool)), 0.0, NEG).astype(one)
    tokens = g["itok_Bx1xSx1_0_63"].reshape(B, S)
    wx = [g[f"L1_xattn_w_{n}"].T for n in "qkvo"]
    lnb = [np.broadcast_to(cols(g[f"L1_xattn_ln_{n}_b"])[:, :, None], (P, C, P)) for n in "qkvo"]
    arrays = dict(
        x=tok(g["x"]), ctxT=chunks(g["ctx_1024"].reshape(B * S, D).T), ctx=tok(g["ctx_1024"]),
        tokq=tokens.T, tokk=np.broadcast_to(tokens[None], (P, B, S)),
        mask=np.ascontiguousarray(g["mask_BxSxS2_bf0"].transpose(1, 0, 2)).view(np.int32), ident=np.eye(P, dtype=one),
        causal=causal, expand=expand, vec=np.concatenate([vec[n] for n in VEC], 1),
        rows=np.concatenate([rows[n] for n in ROWS], 1), lnb=np.stack(lnb, 1),
        w_qk=chunks(g["L0_attn_qk"]), w_ov=chunks(g["L0_attn_ov"]),
        w_q0=chunks(g["L0_xattn_Wq"].T), w_k0=chunks(g["L0_xattn_Wk"].T), w_v0=chunks(g["L0_xattn_Wv"].T),
        w_r0=chunks(g["L0_ffn_w_router"]), w_1=chunks(g["L0_ffn_w1"].T), w_2=chunks(g["L0_ffn_w2"].T),
        w_qkv=chunks(g["L1_attn_w_qkv"].T), w_o1=chunks(g["L1_attn_w_o"].T),
        w_x=np.stack([chunks(w) for w in wx], 1), w_g=chunks(g["L1_ffn_gate_weight"].T),
        w_gate=chunks(g["L1_ffn_w_gate"].reshape(E * EI, D).T), w_up=chunks(g["L1_ffn_w_up"].reshape(E * EI, D).T),
        w_down=g["L1_ffn_w_down"].transpose(2, 0, 1), ws_gate=chunks(g["L1_ffn_ws_gate"].T),
        ws_up=chunks(g["L1_ffn_ws_up"].T), ws_down=chunks(g["L1_ffn_ws_down"].T))
    nc = bacc.Bacc("TRN2", target_bir_lowering=False, num_devices=1)
    feed, args = {}, {}
    for name, a in arrays.items():
        a = np.ascontiguousarray(a)
        feed[f"in_{name}"] = a
        args[name] = nc.dram_tensor(f"in_{name}", a.shape, mybir.dt.from_np(a.dtype), kind="ExternalInput").ap()
    args["out"] = nc.dram_tensor("out_x", (P, B, D), F32, kind="ExternalOutput").ap()
    program(nc, **args)
    got = run_bass_kernel_spmd(nc, [feed], core_ids=[0]).results[0]["out_x"]
    return np.ascontiguousarray(got.transpose(1, 0, 2))
```

```python
from contextlib import ExitStack

import numpy as np

import concourse.bass as bass
from concourse import mybir

P = 128
F32 = mybir.dt.float32
BF16 = mybir.dt.bfloat16
F16 = mybir.dt.float16
U8 = mybir.dt.uint8
I32 = mybir.dt.int32
ALU = mybir.AluOpType
ACT = mybir.ActivationFunctionType
AX = mybir.AxisListType

B, S, D = 16, 128, 256
C = D // P
H, DH = 16, 16
PAIRS = B // 2
T = 2 * S
NB, BLOCK, TOPB = 16, 64, 4
FF = NB * BLOCK // P
E, EI, SHI = 8, 128, 256
SH = SHI // P
TOPE = 2
ROUTE_SCALE = 2.5
EPS = 1e-5
NEG = -1.0e30

VEC = {}
for _name, _n in (("bq0", C), ("bk0", C), ("b1", FF), ("bq1", C), ("bk1", C), ("gq", C), ("gk", C),
                  ("gv", C), ("go", C), ("even", 1), ("odd", 1)):
    VEC[_name] = (sum(n for _, n in VEC.values()), _n)
NVEC = sum(n for _, n in VEC.values())
ROWS = {}
for _name, _n in (("bv0", D), ("br", NB), ("b2", D), ("bv1", D), ("bo1", D), ("bxq", D), ("bxk", D),
                  ("bxv", D), ("bxo", D), ("cosq", DH), ("sinq", DH), ("cosk", DH), ("sink", DH)):
    ROWS[_name] = (sum(n for _, n in ROWS.values()), _n)
NROW = sum(n for _, n in ROWS.values())


def program(nc, x, ctxT, ctx, tokq, tokk, mask, ident, causal, expand, vec, rows, lnb,
            w_qk, w_ov, w_q0, w_k0, w_v0, w_r0, w_1, w_2, w_qkv, w_o1, w_x, w_g, w_gate, w_up,
            w_down, ws_gate, ws_up, ws_down, out):
    stack = ExitStack()
    with stack:
        def sb(name, shape, dt=F32):
            return stack.enter_context(nc.sbuf_tensor(name, shape, dt))

        def sem(name):
            return stack.enter_context(nc.semaphore(name))

        X = sb("X", [P, B, D])
        idn = sb("idn", [P, P])
        idnb = sb("idnb", [P, P], BF16)
        caus = sb("caus", [P, P])
        expb = sb("expb", [P, FF * P], BF16)
        vecs = sb("vecs", [P, NVEC])
        rws = sb("rws", [P, NROW])
        lnbs = sb("lnbs", [P, 4, C, P])
        bias4 = sb("bias4", [P, 4, D])
        mask4 = sb("mask4", [P, B, S // 4], I32)
        mask8 = mask4[:].rearrange("p b s -> p (b s)").bitcast(U8).rearrange("p (b s) -> p b s", b=B)
        tq = sb("tq", [P, B], I32)
        mb0 = sb("mb0", [P, B, S], BF16)
        mb1 = sb("mb1", [P, B, S], BF16)
        bq = [sb(f"bq{i}", [P, C]) for i in range(2)]
        mhalf = sb("mhalf", [P, 4])
        Wqk, Wov = sb("Wqk", [P, C, D]), sb("Wov", [P, C, D])
        Wq0, Wk0, Wv0 = sb("Wq0", [P, C, D]), sb("Wk0", [P, C, D]), sb("Wv0", [P, C, D])
        Wr0 = sb("Wr0", [P, C, NB])
        W1, W2 = sb("W1", [P, C, FF * P]), sb("W2", [P, FF, D])
        Wqkv, Wo1 = sb("Wqkv", [P, C, 3 * D]), sb("Wo1", [P, C, D])
        Wx = sb("Wx", [P, 4, C, D])
        Wg = sb("Wg", [P, C, E])
        Wgate, Wup = sb("Wgate", [P, C, E * EI]), sb("Wup", [P, C, E * EI])
        Wdown = sb("Wdown", [P, E, D])
        Wsg, Wsu, Wsd = sb("Wsg", [P, C, SHI]), sb("Wsu", [P, C, SHI]), sb("Wsd", [P, SH, D])

        def V(name, c=0):
            o = VEC[name][0] + c
            return vecs[:, o:o + 1]

        def R(name):
            o, n = ROWS[name]
            return rws[:, o:o + n]

        two = range(2)
        bst = [sb(f"bst{r}", [P, 2, 6]) for r in two]
        mv = [sb(f"mv{r}", [P, 2, 2]) for r in two]
        ve = [sb(f"ve{r}", [P, 2]) for r in two]
        rstd = [sb(f"rstd{r}", [P, 2]) for r in two]
        xn = [sb(f"xn{r}", [P, 2, D]) for r in two]
        xnT = [sb(f"xnT{r}", [P, C, T]) for r in two]

        names = ["pj0", "pj1", "sc0", "sc1", "tp0", "tp1", "ov0", "ov1"]
        bank = {n: stack.enter_context(nc.psum_tensor(n, [P, 512], F32)) for n in names}
        filled = {n: sem(f"filled_{n}") for n in names}
        drained = {n: sem(f"drained_{n}") for n in names}
        used = dict.fromkeys(names, 0)

        qT = [sb(f"qT{r}", [P, C, T]) for r in two]
        kM = [sb(f"kM{r}", [P, C, 2, 2, S]) for r in two]
        vf, vrest = sb("vf", [P, 2, D]), sb("vrest", [P, 2, D])
        v16 = [sb(f"v16{r}", [P, 2, H, 3, DH], BF16) for r in two]
        mx = [sb(f"mx{r}", [P, 4]) for r in two]
        sh = [sb(f"sh{r}", [P, 2, S]) for r in two]
        pr = [sb(f"pr{r}", [P, 4, S]) for r in two]
        pT = [sb(f"pT{r}", [P, 2, S]) for r in two]
        pH = [sb(f"pH{r}", [P, 4, S], F16) for r in two]
        pL = [sb(f"pL{r}", [P, 4, S], F16) for r in two]
        psum = [sb(f"psum{r}", [P, H]) for r in two]
        hb = [sb(f"hb{r}", [P, H, DH]) for r in two]
        rin = [sb(f"rin{r}", [P, H]) for r in two]
        hd = [sb(f"hd{r}", [P, 2, D]) for r in two]
        cbst = [sb(f"cbst{r}", [P, 2, 6]) for r in two]
        cmv = [sb(f"cmv{r}", [P, 2, 2]) for r in two]
        cve = [sb(f"cve{r}", [P, 2]) for r in two]
        crs = [sb(f"crs{r}", [P, 2]) for r in two]
        v2 = [sb(f"v2{r}", [P, 2]) for r in two]
        rq = [sb(f"rq{r}", [P, 2]) for r in two]
        cn = [sb(f"cn{r}", [P, 2, D]) for r in two]
        cnT = [sb(f"cnT{r}", [P, C, T]) for r in two]
        cT = [sb(f"cT{r}", [P, C, T]) for r in two]
        cx = cT
        hst = sb("hst", [P, 2, 6])
        hmv = sb("hmv", [P, 2, 2])
        hve = sb("hve", [P, 2])
        hrs = sb("hrs", [P, 2])
        hdT = sb("hdT", [P, C, T])
        hT = [sb(f"hT{r}", [P, FF, T]) for r in two]
        tk = hT[0][:].rearrange("p a b -> p (a b)").bitcast(I32).rearrange("p (b s) -> p b s", b=B)
        expd = hT[1][:].rearrange("p a b -> p (a b)")[:, 0:FF * P]
        parts = [hT[i // 2][:].rearrange("p a b -> p (a b)")[:, (i % 2) * 1024:(i % 2 + 1) * 1024]
                 .rearrange("p (i j d) -> p i j d", i=2, j=2) for i in range(4)]
        rt, rc, rs, ro = parts
        lg = sb("lg", [P, 2, NB])
        lmx = sb("lmx", [P, 2])
        lsh = sb("lsh", [P, 2, NB])
        le = sb("le", [P, 2, NB + 8 - TOPB])
        ls = sb("ls", [P, 2, E + 8 - TOPE])
        nmx = [sb(f"nmx{r}", [P, 2]) for r in two]
        rsum = [sb(f"rsum{r}", [P, 2]) for r in two]
        tops5 = sb("tops5", [P, 2, 8])
        kept5 = sb("kept5", [P, 2, E + 8 - TOPE])
        deni, rden = sb("deni", [P, 2]), sb("rden", [P, 2])
        sel = sb("sel", [P, 2, E])
        v3, v4, v5 = ([sb(f"{n}{r}", [P, 2]) for r in two] for n in ("va3", "va4", "va5"))
        hn = sb("hn", [P, 2, D])
        top = sb("top", [P, 2, 8])
        tops = sb("tops", [P, 2, 8])
        kept = sb("kept", [P, 2, NB + 8 - TOPB])
        nm = sb("nm", [P, 2, P])
        nmT = [sb(f"nmT{r}", [P, T], BF16) for r in two]
        sg = [sb(f"sg{r}", [P, T]) for r in two]
        hm = [sb(f"hm{r}", [P, T]) for r in two]
        comb = [sb(f"comb{r}", [P, 2, E]) for r in two]
        den = sb("den", [P, 2])
        started = sb("started", [P, 5])

        def sems(names):
            return [sem(n) for n in names.split()]

        s_x0, s_x1, s_const, s_mask = sems("s_x0 s_x1 s_const s_mask")
        s_ct, s_cx = sems("s_ct0 s_ct1"), sems("s_cx0 s_cx1")
        s_w = [sem(f"s_w{f}") for f in range(6)]
        s_small = sem("s_small")
        s_bf, s_eq, s_mb = sems("s_bf s_eq s_mb")
        s_fold, s_folded = sems("s_fold s_folded")
        (st_done, mv_done, ve_done, rstd_done, xn_done, xnT_done) = sems(
            "st_done mv_done ve_done rstd_done xn_done xnT_done")
        x_ready = [sem(f"x_ready{f}") for f in range(5)]
        xadd = sem("xadd")
        s_out = sem("s_out")
        uT_done, mx0_done, nmx0_done, sm0_done, ri0_done, pT0_done, aT_done = sems(
            "uT_done mx0_done nmx0_done sm0_done ri0_done pT0_done aT_done")
        mx_done, pH_done, pv_done, hb_done, vf_done, va_done, vrest_done, vb_done, vc_done = sems(
            "mx_done pH_done pv_done hb_done vf_done va_done vrest_done vb_done vc_done")
        xmid = sem("xmid")
        cst_done, cmv_done, cve_done, crs_done, cn_done, cnT_done = sems(
            "cst_done cmv_done cve_done crs_done cn_done cnT_done")
        v2_done, rq_done = sems("v2_done rq_done")
        rt_done, rc_done, rs_done, ro_done = sems("rt_done rc_done rs_done ro_done")
        hst_done, hmv_done, hve_done, hrs_done, hn_done = sems("hst_done hmv_done hve_done hrs_done hn_done")
        lg_done, lmx_done, lsh_done, le_done, top_done, tops_done, kept_done, nm_done, nmT_done = sems(
            "lg_done lmx_done lsh_done le_done top_done tops_done kept_done nm_done nmT_done")
        sig_done, top5_done, tops5_done, den_done, kept5_done, sel_done, rden_done, comb_done = sems(
            "sig_done top5_done tops5_done den_done kept5_done sel_done rden_done comb_done")
        sg_done, hm_done, acc_done = sems("sg_done hm_done acc_done")

        def least(n):
            return max(n, 0) if isinstance(n, int) else n

        def past(n):
            return n + 1

        count_reg = {}

        def apart(eng, n):
            if isinstance(n, int):
                return max(n, 0)
            if eng not in count_reg:
                count_reg[eng] = stack.enter_context(eng.register("count"))
            eng.reg_mov(count_reg[eng], n)
            eng.wait_ge(s_const, 64)
            return count_reg[eng]

        def steps(eng, body):
            body(-1, 1)
            body(0, 0)
            with eng.Fori(1, PAIRS - 2, 2) as t:
                body(t, 1)
                body(t + 1, 0)
            body(PAIRS - 1, 1)
            body(PAIRS, 0)

        def on(t, lo, hi):
            return not isinstance(t, int) or lo <= t <= hi

        PJ_BEFORE = [(1, 1), (2, 2), (2, 1), (2, 2), (4, 3), (1, 1)]
        PJ_AFTER = [(0, 0), (0, 0), (0, 0), (1, 1), (1, 1), (0, 0)]
        PJ_AFTER_D = [(0, 0), (0, 0), (0, 0), (1, 0), (1, 0), (0, 0)]
        PJ_FOLD = 2

        def pj_base(f, b, after=PJ_AFTER):
            n = sum(PAIRS * (PJ_BEFORE[g][b] + after[g][b]) for g in range(f))
            return n + PJ_FOLD * (f >= 3)

        def pj_before(f, b, p, i, after=PJ_AFTER):
            n = pj_base(f, b, after) + PJ_BEFORE[f][b] * p + i
            return n + after[f][b] * (max(p - 2, 0) if isinstance(p, int) else p - 2)

        def pj_after(f, b, p, i, after=PJ_AFTER):
            n = pj_base(f, b, after) + after[f][b] * p + i
            return n + PJ_BEFORE[f][b] * (min(p + 3, PAIRS) if isinstance(p, int) else p + 3)

        def dr_before(f, b, p, i):
            return pj_before(f, b, p, i, PJ_AFTER_D)

        def dr_step(f, b, p):
            done = p - 1 if not isinstance(p, int) else max(p - 1, 0)
            return pj_base(f, b, PJ_AFTER_D) + PJ_BEFORE[f][b] * (p + 1) + PJ_AFTER_D[f][b] * done

        def dr_after(f, b, p, i):
            return pj_after(f, b, p, i, PJ_AFTER_D)

        PER_PAIR = {"sc0": [1, 4, 2, 4, 4, 5], "sc1": [0, 4, 2, 4, 4, 5],
                    "tp0": [1, 4, 2, 4, 4, 5], "tp1": [1, 4, 2, 4, 4, 5],
                    "ov0": [0, 1, 0, 1, 1, 0], "ov1": [0, 1, 0, 1, 1, 0]}

        def use(f, name, p, i=0):
            return PAIRS * sum(PER_PAIR[name][:f]) + PER_PAIR[name][f] * p + i

        ATT = {1: 0, 3: 1, 4: 2}

        def group(f, p, n):
            return PAIRS * 8 * ATT[f] + 8 * p + n

        def head(g, i):
            return 8 * (i // 2) + 2 * g + i % 2

        def pair(f, p):
            return PAIRS * f + p

        def att(f, p):
            return PAIRS * ATT[f] + p

        def landed(p, r):
            return 8 * p + 16 - 8 * r

        def xadds(f, n):
            return PAIRS * (f - 2) + n

        block = stack.enter_context(nc.Block())

        def xp(p):
            return X[:, bass.ds(2 * p, 2), :]

        def xs(p, j):
            return X[:, bass.ds(2 * p + j, 1), :].rearrange("p o d -> p (o d)")

        def heads(ap):
            return ap.rearrange("p (h d) -> p h d", h=H)

        def over(ap, n):
            return ap.unsqueeze(1).to_broadcast([P, n, ap.shape[1]])

        def along(ap, n):
            return ap.unsqueeze(2).to_broadcast([P, ap.shape[1], n])

        def four(name):
            return bank[name][:, :].rearrange("p (a s) -> p a s", a=4)

        @block.sync
        def _(sp):
            sp.dma_start(X[:, 0:2, :], x[:, 0:2, :]).then_inc(s_x0, 16)
            for dst, src in ((idn, ident), (caus, causal), (vecs, vec), (rws, rows)):
                sp.dma_start(dst[:], src).then_inc(s_const, 16)
            for dst, src in ((Wqk, w_qk), (Wov, w_ov)):
                sp.dma_start(dst[:], src).then_inc(s_w[0], 16)
            sp.dma_start(X[:, 2:B, :], x[:, 2:B, :]).then_inc(s_x1, 16)
            for dst, src in ((mask4[:], mask), (tq[:], tokq), (tk, tokk)):
                sp.dma_start(dst, src).then_inc(s_mask, 16)
            for r in two:
                sp.dma_start(cT[r][:], ctxT[:, :, r * T:(r + 1) * T]).then_inc(s_ct[r], 16)
            for dst, src in ((Wq0, w_q0), (Wk0, w_k0), (Wv0, w_v0)):
                sp.dma_start(dst[:], src).then_inc(s_w[1], 16)
            for dst, src in ((Wr0[:], w_r0), (W1[:], w_1), (W2[:], w_2), (expd, expand)):
                sp.dma_start(dst, src).then_inc(s_w[2], 16)
            for dst, src in ((Wqkv, w_qkv), (Wo1, w_o1)):
                sp.dma_start(dst[:], src).then_inc(s_w[3], 16)
            for dst, src in ((Wx, w_x), (lnbs, lnb)):
                sp.dma_start(dst[:], src).then_inc(s_w[4], 16)
            for dst, src in ((Wg, w_g), (Wgate, w_gate), (Wup, w_up), (Wdown, w_down),
                             (Wsg, ws_gate), (Wsu, ws_up), (Wsd, ws_down)):
                sp.dma_start(dst[:], src).then_inc(s_w[5], 16)
            with sp.Fori(2, PAIRS - 1, 2) as p:
                for r in two:
                    sp.wait_ge(filled["pj0"], pj_before(1, 0, p + r - 2, 1) + 1)
                    sp.dma_start(cT[r][:], ctxT[:, :, bass.ds((p + r) * T, T)]).then_inc(s_ct[r], 16)
            for r in two:
                sp.wait_ge(filled["pj0"], pj_before(1, 0, PAIRS - 2 + r, 1) + 1)
                sp.dma_start(cx[r][:], ctx[:, 2 * r:2 * r + 2, :]).then_inc(s_cx[r], 16)
            with sp.Fori(2, PAIRS - 1, 2) as p:
                for r in two:
                    sp.wait_ge(cn_done, least(p + r - 1))
                    sp.dma_start(cx[r][:], ctx[:, bass.ds(2 * (p + r), 2), :]).then_inc(s_cx[r], 16)
            for p in range(PAIRS):
                sp.wait_ge(drained["tp1"], use(5, "tp1", p, 4) + 1)
                sp.dma_start(out[:, 2 * p:2 * p + 2, :], X[:, 2 * p:2 * p + 2, :]).then_inc(s_out, 16)
            sp.wait_ge(s_out, 16 * PAIRS)

        @block.tensor
        def _(pe):
            mm = nc.tensor.matmul

            def turn(f, p, r):
                pe.wait_ge(xn_done, pair(f, p) + 1)
                pe.wait_ge(drained["pj0"], least(dr_before(f, 0, p, 0)))
                turn_pair("pj0", xn[r])

            def turn_pair(name, src):
                for c in range(C):
                    for j in two:
                        o = c * T + j * S
                        last = nc.tensor.transpose(bank[name][:, o:o + S], src[:, j, c * P:(c + 1) * P], idn[:])
                last.then_inc(filled[name], 1)

            def across(name, w, act, col=0):
                for o in range(C):
                    for c in range(C):
                        last = mm(bank[name][:, o * T:(o + 1) * T], w[:, c, col + o * P:col + (o + 1) * P],
                                  act[:, c, :], start=c == 0, stop=c == C - 1)
                last.then_inc(filled[name], 1)

            def along_tokens(name, act, w, n=D, col=0):
                for j in two:
                    for c in range(C):
                        last = mm(bank[name][:, j * n:(j + 1) * n], act[:, c, j * S:(j + 1) * S],
                                  w[:, c, col:col + n], start=c == 0, stop=c == C - 1)
                last.then_inc(filled[name], 1)

            pe.wait_ge(s_const, 64)
            pe.wait_ge(s_w[0], 32)

            def body(t, r):
                q = 1 - r
                if on(t, 1, PAIRS):
                    p = t - 1
                    pe.wait_ge(sm0_done, p + 1)
                    for j in two:
                        last = nc.tensor.transpose(bank["tp0"][:, j * S:(j + 1) * S], pr[q][:, j, :], idn[:])
                    last.then_inc(filled["tp0"], 1)
                if on(t, 0, PAIRS - 1):
                    pe.wait_ge(drained["pj1"], dr_before(0, 1, t, 0) + 1)
                    pe.wait_ge(drained["sc0"], least(use(0, "sc0", t)))
                    for j in two:
                        s = slice(j * S, (j + 1) * S)
                        for c in range(C):
                            last = mm(bank["sc0"][:, s], qT[r][:, c, s], xnT[r][:, c, s],
                                      start=c == 0, stop=c == C - 1)
                    last.then_inc(filled["sc0"], 1)
                if on(t, 1, PAIRS):
                    p = t - 1
                    pe.wait_ge(drained["tp0"], use(0, "tp0", p) + 1)
                    for c in range(C):
                        for j in two:
                            o = c * T + j * S
                            last = mm(bank["tp1"][:, o:o + S], xn[q][:, j, c * P:(c + 1) * P], pT[q][:, j, :],
                                      start=True, stop=True)
                    last.then_inc(filled["tp1"], 1)
                if on(t, -1, PAIRS - 2):
                    turn(0, t + 1, q)
                if on(t, 1, PAIRS):
                    pe.wait_ge(drained["tp1"], use(0, "tp1", p) + 1)
                    pe.wait_ge(x_ready[0], past(p))
                    along_tokens("ov0", cnT[q], Wov)
                if on(t, -1, PAIRS - 2):
                    p = t + 1
                    pe.wait_ge(drained["pj0"], dr_before(0, 0, p, 0) + 1)
                    pe.wait_ge(drained["pj1"], least(dr_before(0, 1, p, 0)))
                    across("pj1", Wqk, xnT[q])

            steps(pe, body)

            def scores(f, p, r, n, masks):
                name, j, g = f"sc{n % 2}", n // 4, n % 4
                pe.wait_ge(drained[name], least(use(f, name, p, n // 2)))
                if masks is not None:
                    mm(bank[name][:, :], idnb[:],
                       masks[:, bass.ds(2 * p + j, 1), :].to_broadcast([P, 4, S]), start=True, stop=False,
                       skip_group_check=True)
                rows32 = slice(32 * g, 32 * g + 32)
                for c in range(C):
                    last = mm(bank[name][:, c * T:(c + 1) * T], qT[r][rows32, c, j * S:(j + 1) * S],
                              kM[r][rows32, c, j, :, :], start=masks is None, stop=True,
                              skip_group_check=True)
                last.then_inc(filled[name], 1)

            def turn_probs(f, p, n):
                name = f"tp{n % 2}"
                pe.wait_ge(drained[f"sc{n % 2}"], use(f, f"sc{n % 2}", p, n // 2) + 1)
                pe.wait_ge(drained[name], least(use(f, name, p, n // 2)))
                for i in range(4):
                    last = nc.tensor.transpose(bank[name][:, i * S:(i + 1) * S], pr[n % 2][:, i, :], idn[:])
                last.then_inc(filled[name], 1)

            def probs_times_values(f, p, r, n):
                j, g = n // 4, n % 4
                pe.wait_ge(drained[f"tp{n % 2}"], use(f, f"tp{n % 2}", p, n // 2) + 1)
                if g == 0 and isinstance(p, int) and p == 0 and j == 0 and f != 4:
                    pe.wait_ge(x_ready[f - 1], past(PAIRS))
                if n == 0:
                    pe.wait_ge(vc_done, att(f, p) + 1)
                for i in range(4):
                    h = head(g, i)
                    o = bank[f"ov{j}"][:, h * 2 * DH:(h + 1) * 2 * DH]
                    mm(o, pH[n % 2][:, i, :], v16[r][:, j, h, 0:2, :], start=True, stop=False,
                       skip_group_check=True)
                    mm(o[:, DH:2 * DH], pH[n % 2][:, i, :], v16[r][:, j, h, 2, :], start=False, stop=False,
                       skip_group_check=True)
                    last = mm(o, pL[n % 2][:, i, :], v16[r][:, j, h, 0:2, :], start=False, stop=True,
                              skip_group_check=True)
                last.then_inc(pv_done, 1)

            def attention(f, masks, before, after, qkv):
                def body(t, r):
                    q = 1 - r
                    for n in range(8):
                        if on(t, 0, PAIRS - 1):
                            if n == 0:
                                qkv(t)
                            scores(f, t, r, n, masks)
                        if n >= 2 and on(t, 0, PAIRS - 1):
                            turn_probs(f, t, n - 2)
                        if n < 2 and on(t, 1, PAIRS):
                            turn_probs(f, t - 1, n + 6)
                        if n >= 4 and on(t, 0, PAIRS - 1):
                            probs_times_values(f, t, r, n - 4)
                        if n < 4 and on(t, 1, PAIRS):
                            probs_times_values(f, t - 1, q, n + 4)
                        if n in before and on(t, -1, PAIRS - 2):
                            before[n](t + 1, q)
                        if n in after and on(t, 1, PAIRS):
                            after[n](t - 1, q)

                steps(pe, body)

            pe.wait_ge(s_w[1], 48)
            pe.wait_ge(s_mb, 1)
            pe.wait_ge(s_bf, 1)

            def project_q(p, r):
                pe.wait_ge(drained["pj1"], least(dr_before(1, 1, p, 1)))
                across("pj1", Wq0, xnT[r])

            def project_k(p, r):
                pe.wait_ge(drained["pj0"], dr_before(1, 0, p, 0) + 1)
                across("pj0", Wk0, cT[r])

            def project_v(p, r):
                pe.wait_ge(s_ct[r], landed(p, r))
                pe.wait_ge(drained["pj1"], least(dr_before(1, 1, p, 0)))
                along_tokens("pj1", cT[r], Wv0)

            def ready(p):
                for b in two:
                    pe.wait_ge(drained[f"pj{b}"], least(dr_step(1, b, p)))

            attention(1, mb0, {2: lambda p, r: turn(1, p, r), 3: project_v, 4: project_k, 5: project_q},
                      {}, ready)

            pe.wait_ge(s_w[2], 64)
            pe.wait_ge(s_bf, 2)

            def second(p, r, j):
                if j == 0:
                    pe.wait_ge(drained["tp1"], use(2, "tp1", p, 1) + 1)
                    pe.wait_ge(x_ready[2], past(p))
                for d in range(FF):
                    last = mm(bank["ov0"][:, j * D:(j + 1) * D], hT[r][:, d, j * S:(j + 1) * S],
                              W2[:, d, :], start=d == 0, stop=d == FF - 1)
                if j == 1:
                    last.then_inc(filled["ov0"], 1)

            def body(t, r):
                q = 1 - r
                if on(t, 1, PAIRS):
                    second(t - 1, q, 0)
                if on(t, 0, PAIRS - 1):
                    pe.wait_ge(nm_done, t + 1)
                    pe.wait_ge(drained["pj0"], dr_before(2, 0, t, 1))
                    for j in two:
                        last = nc.tensor.transpose(bank["pj0"][:, j * S:(j + 1) * S], nm[:, j, :], idn[:])
                    last.then_inc(filled["pj0"], 1)
                if on(t, 1, PAIRS):
                    second(t - 1, q, 1)
                if on(t, 0, PAIRS - 1):
                    pe.wait_ge(drained["pj0"], dr_before(2, 0, t, 1) + 1)
                for c in range(FF):
                    if c == 1 and on(t, -1, PAIRS - 2):
                        turn(2, t + 1, q)
                    if c == 3 and on(t, -1, PAIRS - 2):
                        p = t + 1
                        pe.wait_ge(drained["pj0"], dr_before(2, 0, p, 0) + 1)
                        pe.wait_ge(drained["pj1"], dr_before(2, 1, p, 0))
                        along_tokens("pj1", xnT[q], Wr0, NB)
                    if on(t, 0, PAIRS - 1):
                        name = ("sc0", "sc1", "tp0", "tp1")[c % 4]
                        pe.wait_ge(drained[name], use(2, name, t, c // 4))
                        mm(bank[name][:, 0:T], expb[:, c * P:(c + 1) * P], nmT[r][:, :], start=True, stop=False)
                        for d in range(C):
                            last = mm(bank[name][:, 0:T], W1[:, d, c * P:(c + 1) * P], xnT[r][:, d, :],
                                      start=False, stop=d == C - 1)
                        last.then_inc(filled[name], 1)

            steps(pe, body)

            pe.wait_ge(s_w[4], 32)
            for i in range(4):
                name = f"pj{i % 2}"
                pe.wait_ge(drained[name], least(pj_base(3, i % 2, PJ_AFTER_D) - PJ_FOLD + i // 2))
                for c in range(C):
                    last = mm(bank[name][:, 0:D], lnbs[:, i, c, :], Wx[:, i, c, :], start=c == 0, stop=c == C - 1)
                last.then_inc(filled[name], 1)

            pe.wait_ge(s_w[3], 32)

            def project_q(p, r):
                pe.wait_ge(drained["pj1"], least(dr_before(3, 1, p, 1)))
                across("pj1", Wqkv, xnT[r], 0)

            def project_k(p, r):
                pe.wait_ge(drained["pj0"], least(dr_before(3, 0, p, 1)))
                across("pj0", Wqkv, xnT[r], D)

            def project_v(p, r):
                pe.wait_ge(drained["pj0"], dr_before(3, 0, p, 0) + 1)
                pe.wait_ge(drained["pj1"], least(dr_before(3, 1, p, 0)))
                pe.wait_ge(x_ready[3], least(past(p - 2)))
                along_tokens("pj1", xnT[r], Wqkv, D, 2 * D)

            def turn_heads(p, r):
                for j in two:
                    pe.wait_ge(drained[f"ov{j}"], use(3, f"ov{j}", p) + 1)
                pe.wait_ge(drained["pj0"], least(dr_after(3, 0, p, 0)))
                turn_pair("pj0", hd[r])

            def project_out(p, r):
                pe.wait_ge(drained["pj0"], dr_after(3, 0, p, 0) + 1)
                pe.wait_ge(drained["pj1"], least(dr_after(3, 1, p, 0)))
                pe.wait_ge(x_ready[3], past(p))
                along_tokens("pj1", hdT, Wo1)

            def ready(p):
                for b in two:
                    pe.wait_ge(drained[f"pj{b}"], least(dr_step(3, b, p)))

            attention(3, None, {2: lambda p, r: turn(3, p, r), 3: project_v, 4: project_k, 5: project_q},
                      {7: lambda p, r: (turn_heads(p, r), project_out(p, r))}, ready)

            pe.wait_ge(s_folded, 4)
            pe.wait_ge(s_mb, 2)
            pe.wait_ge(x_ready[3], past(PAIRS))

            def turn_both(p, r):
                turn(4, p, r)
                pe.wait_ge(cn_done, p + 1)
                pe.wait_ge(drained["pj1"], least(dr_before(4, 1, p, 0)))
                pe.wait_ge(x_ready[4], least(past(p - 2)))
                turn_pair("pj1", cn[r])

            def project_qk(p, r):
                pe.wait_ge(drained["pj0"], dr_before(4, 0, p, 0) + 1)
                along_tokens("pj0", xnT[r], Wx[:, 0])
                pe.wait_ge(drained["pj1"], dr_before(4, 1, p, 0) + 1)
                along_tokens("pj1", cnT[r], Wx[:, 1])

            def project_v(p, r):
                pe.wait_ge(drained["pj0"], least(dr_before(4, 0, p, 2)))
                along_tokens("pj0", cnT[r], Wx[:, 2])

            def turn_rotated(p, r):
                pe.wait_ge(ro_done, 2 * p + 2)
                pe.wait_ge(drained["pj1"], least(dr_before(4, 1, p, 2)))
                turn_pair("pj1", ro[:, 0])
                pe.wait_ge(drained["pj0"], least(dr_before(4, 0, p, 3)))
                turn_pair("pj0", ro[:, 1])

            def turn_heads(p, r):
                pe.wait_ge(hn_done, p + 1)
                pe.wait_ge(drained["pj0"], least(dr_after(4, 0, p, 0)))
                turn_pair("pj0", hn)

            def project_out(p, r):
                pe.wait_ge(drained["pj0"], dr_after(4, 0, p, 0) + 1)
                pe.wait_ge(drained["pj1"], least(dr_after(4, 1, p, 0)))
                pe.wait_ge(x_ready[4], past(p))
                along_tokens("pj1", hdT, Wx[:, 3])

            def ready(p):
                for b in two:
                    pe.wait_ge(drained[f"pj{b}"], least(dr_step(4, b, p)))

            def last_slot(p, r):
                turn_heads(p, r)
                project_out(p, r)

            attention(4, mb1, {2: turn_both, 3: project_qk, 4: project_v, 7: turn_rotated},
                      {7: last_slot}, ready)

            pe.wait_ge(s_w[5], 7 * 16)

            def up(t, r, e):
                name = f"sc{e % 2}"
                if isinstance(t, int) and t == 0 and e < 2:
                    pe.wait_ge(drained[name], least(use(5, name, 0)))
                else:
                    pe.wait_ge(hm_done, least(10 * t + e - 1))
                for i, w in enumerate((Wgate, Wup) if e < E else (Wsg, Wsu)):
                    o = e * P if e < E else (e - E) * P
                    for c in range(C):
                        last = mm(bank[name][:, i * T:(i + 1) * T], w[:, c, o:o + P], xnT[r][:, c, :],
                                  start=c == 0, stop=c == C - 1)
                last.then_inc(filled[name], 1)

            def down(t, e):
                name = f"tp{e % 2}"
                pe.wait_ge(hm_done, 10 * t + e + 1)
                pe.wait_ge(drained[name], least(use(5, name, t, e // 2)))
                w = Wdown[:, e, :] if e < E else Wsd[:, e - E, :]
                for j in two:
                    last = mm(bank[name][:, j * D:(j + 1) * D], hm[e % 2][:, j * S:(j + 1) * S], w,
                              start=True, stop=True)
                last.then_inc(filled[name], 1)

            def body(t, r):
                q = 1 - r
                if on(t, 0, PAIRS - 1):
                    pe.wait_ge(drained["pj0"], dr_before(5, 0, t, 0) + 1)
                for e in range(E + SH):
                    if on(t, 0, PAIRS - 1):
                        up(t, r, e)
                        if e >= 2:
                            down(t, e - 2)
                    if on(t, 1, PAIRS) and e < 2:
                        down(t - 1, E + SH - 2 + e)
                    if e == 4 and on(t, -1, PAIRS - 2):
                        turn(5, t + 1, q)
                    if e == 6 and on(t, -1, PAIRS - 2):
                        pe.wait_ge(drained["pj0"], dr_before(5, 0, t + 1, 0) + 1)
                        if isinstance(t, int) and t == -1:
                            pe.wait_ge(drained["pj1"], least(dr_before(5, 1, 0, 0)))
                            pe.wait_ge(x_ready[4], past(PAIRS))
                        else:
                            pe.wait_ge(sig_done, t + 1)
                        along_tokens("pj1", xnT[q], Wg, E)

            steps(pe, body)

        @block.vector
        def _(dve):
            v = nc.vector

            def stats(src, b, m, s_b, s_m, n):
                for j in two:
                    last = v.bn_stats(b[:, j, :], src(j))
                last.then_inc(s_b, 1)
                dve.wait_ge(s_b, apart(dve, n + 1))
                for j in two:
                    last = v.bn_aggr(m[:, j, :], b[:, j, :])
                last.then_inc(s_m, 1)

            def x_stats(f, p, r):
                if f == 0:
                    dve.wait_ge(s_x0 if isinstance(p, int) and p == 0 else s_x1, 16)
                else:
                    dve.wait_ge(x_ready[f - 1], past(p + 1))
                stats(lambda j: xs(p, j), bst[r], mv[r], st_done, mv_done, pair(f, p))

            def normalise(dst, src, m, s, done):
                for j in two:
                    last = v.tensor_scalar(dst[:, j, :], src(j), m[:, j, 0:1], s[:, j:j + 1],
                                           ALU.subtract, ALU.mult)
                last.then_inc(done, 1)

            def x_norm(f, p, r):
                if f == 4:
                    dve.wait_ge(rq_done, p + 1)
                else:
                    dve.wait_ge(rstd_done, pair(f, p) + 1)
                if f == 3:
                    dve.wait_ge(xadd, least(xadds(3, p - 1)))
                normalise(xn[r], lambda j: xs(p, j), mv[r], rq[r] if f == 4 else rstd[r], xn_done)

            for f in (0, 2, 3, 4):
                v.memset(started[:, f:f + 1], 0.0).then_inc(x_ready[f], 1)
            dve.wait_ge(s_const, 64)
            for i in two:
                o = VEC[f"bq{i}"][0]
                v.tensor_scalar(bq[i][:], vecs[:, o:o + C], (0.25, 0.0625)[i], None, ALU.mult)
            v.tensor_copy(idnb[:], idn[:]).then_inc(s_bf, 1)

            def body(t, r):
                q = 1 - r
                if on(t, -1, PAIRS - 2):
                    x_stats(0, t + 1, q)
                if on(t, 0, PAIRS - 1):
                    dve.wait_ge(filled["sc0"], use(0, "sc0", t) + 1)
                    v.tensor_tensor(sh[r][:, 0:2, :], bank["sc0"][:, 0:T].rearrange("p (j s) -> p j s", j=2),
                                    over(caus[:], 2), ALU.add).then_inc(drained["sc0"], 1)
                    dve.wait_ge(drained["sc0"], use(0, "sc0", t) + 1)
                    v.tensor_reduce(mx[r][:, 0:2], sh[r][:, 0:2, :], AX.X, ALU.max).then_inc(mx0_done, 1)
                    dve.wait_ge(mx0_done, t + 1)
                    v.tensor_scalar(nmx[r][:, 0:2], mx[r][:, 0:2], -1.0 / 16.0, None, ALU.mult).then_inc(nmx0_done, 1)
                if on(t, 1, PAIRS):
                    p = t - 1
                    dve.wait_ge(sm0_done, p + 1)
                    v.reciprocal(rin[q][:, 0:2], rsum[q][:, 0:2]).then_inc(ri0_done, 1)
                if on(t, -1, PAIRS - 2):
                    if on(t, 1, PAIRS):
                        dve.wait_ge(filled["tp1"], least(use(0, "tp1", t - 1) + 1))
                    x_norm(0, t + 1, q)
                if on(t, 1, PAIRS):
                    p = t - 1
                    dve.wait_ge(ri0_done, p + 1)
                    dve.wait_ge(filled["ov0"], p + 1)
                    for j in two:
                        last = v.scalar_tensor_tensor(xs(p, j), bank["ov0"][:, j * D:(j + 1) * D],
                                                      rin[q][:, j:j + 1], xs(p, j), ALU.mult, ALU.add)
                    last.then_inc(x_ready[0], 1)

            steps(dve, body)

            dve.wait_ge(s_mask, 48)
            v.tensor_scalar(mb0[:], mask8, NEG, None, ALU.mult).then_inc(s_mb, 1)
            v.tensor_tensor(mb1[:], tk, along(tq[:], S), ALU.not_equal).then_inc(s_eq, 1)
            dve.wait_ge(s_eq, 1)
            v.scalar_tensor_tensor(mb1[:], mb1[:], NEG, over(caus[:], B), ALU.mult, ALU.add).then_inc(s_mb, 1)

            def maxima(f, p, n):
                name = f"sc{n % 2}"
                dve.wait_ge(filled[name], use(f, name, p, n // 2) + 1)
                v.tensor_reduce(mx[n % 2][:, :], four(name), AX.X, ALU.max, negate=True).then_inc(mx_done, 1)

            def low_probs(f, p, n):
                name = f"tp{n % 2}"
                dve.wait_ge(pH_done, group(f, p, n) + 1)
                v.tensor_tensor(pL[n % 2][:], four(name), pH[n % 2][:], ALU.subtract).then_inc(drained[name], 1)

            def inverse_sums(f, p, j):
                for i in two:
                    dve.wait_ge(drained[f"sc{i}"], use(f, f"sc{i}", p, 2 * j + 1) + 1)
                v.reciprocal(rin[j][:], psum[j][:])

            def norm_heads(f, p, r, j):
                dve.wait_ge(pv_done, group(f, p, 4 * j + 4))
                v.tensor_reduce(hb[j][:], bank[f"ov{j}"][:, :].rearrange("p (h a d) -> p h d a", h=H, a=2),
                                AX.X, ALU.add).then_inc(hb_done, 1)
                dve.wait_ge(hb_done, 2 * att(f, p) + j + 1)
                v.tensor_tensor(heads(hd[r][:, j, :]), hb[j][:], along(rin[j][:], DH),
                                ALU.mult).then_inc(drained[f"ov{j}"], 1)

            def masked_keys(name, r, bias, o, done):
                src = bank[name][:, o * T:(o + 1) * T].rearrange("p (j s) -> p j s", j=2)
                for i, m in enumerate(("even", "odd")):
                    if bias:
                        last = v.tensor_scalar(kM[r][:, o, :, i, :], src, V(bias, o), V(m), ALU.add, ALU.mult)
                    else:
                        last = v.tensor_scalar(kM[r][:, o, :, i, :], src, V(m), None, ALU.mult)
                if o == C - 1:
                    last.then_inc(done, 1)

            def values(f, p, name, bias):
                dve.wait_ge(vc_done, least(att(f, p)))
                v.tensor_tensor(vf[:], bank[name][:, :].rearrange("p (j d) -> p j d", j=2), over(bias, 2),
                                ALU.add).then_inc(drained[name], 1)

            def add_to_x(name, p, done, n):
                dve.wait_ge(xadd, n)
                v.tensor_tensor(xp(p), bank[name][:, :].rearrange("p (j d) -> p j d", j=2), xp(p),
                                ALU.add).then_inc(done, 1)

            def attention(f, before, after):
                def body(t, r):
                    q = 1 - r
                    for n in range(8):
                        if on(t, 0, PAIRS - 1):
                            maxima(f, t, n)
                        if n >= 3 and on(t, 0, PAIRS - 1):
                            low_probs(f, t, n - 3)
                        if n < 3 and on(t, 1, PAIRS):
                            low_probs(f, t - 1, n + 5)
                        if n == 0 and on(t, 1, PAIRS):
                            inverse_sums(f, t - 1, 1)
                            norm_heads(f, t - 1, q, 0)
                        if n == 4 and on(t, 1, PAIRS):
                            norm_heads(f, t - 1, q, 1)
                        if n == 4 and on(t, 0, PAIRS - 1):
                            inverse_sums(f, t, 0)
                        if n == 0 and on(t, -1, PAIRS - 2):
                            x_stats(f, t + 1, q)
                        if n == (2 if f == 4 else 1) and on(t, -1, PAIRS - 2):
                            x_norm(f, t + 1, q)
                        if n in before and on(t, -1, PAIRS - 2):
                            before[n](t + 1, q)
                        if n in after and on(t, 1, PAIRS):
                            after[n](t - 1, q)

                steps(dve, body)

            def keys(p, r, o):
                dve.wait_ge(filled["pj0"], pj_before(1, 0, p, 1) + 1)
                masked_keys("pj0", r, "bk0", o, drained["pj0"])

            def vals(p, r):
                dve.wait_ge(filled["pj1"], pj_before(1, 1, p, 0) + 1)
                values(1, p, "pj1", R("bv0"))

            attention(1, {4: vals, 5: lambda p, r: keys(p, r, 0), 6: lambda p, r: keys(p, r, 1)}, {})

            dve.wait_ge(s_w[2], 64)
            v.tensor_copy(expb[:], expd).then_inc(s_bf, 1)

            def body(t, r):
                q = 1 - r
                p = t + 1
                if on(t, -1, PAIRS - 2):
                    x_stats(2, p, q)
                    x_norm(2, p, q)
                if on(t, 1, PAIRS):
                    dve.wait_ge(filled["ov0"], PAIRS + t)
                    add_to_x("ov0", t - 1, x_ready[2], xadds(2, t))
                if on(t, -1, PAIRS - 2):
                    dve.wait_ge(filled["pj1"], pj_before(2, 1, p, 0) + 1)
                    v.tensor_tensor(lg[:], bank["pj1"][:, 0:2 * NB].rearrange("p (j e) -> p j e", j=2),
                                    over(R("br"), 2), ALU.add).then_inc(drained["pj1"], 1)
                    dve.wait_ge(drained["pj1"], dr_before(2, 1, p, 0) + 1)
                    v.tensor_reduce(lmx[:], lg[:], AX.X, ALU.max).then_inc(lmx_done, 1)
                    dve.wait_ge(lmx_done, p + 1)
                    v.tensor_tensor(lsh[:], lg[:], along(lmx[:], NB), ALU.subtract).then_inc(lsh_done, 1)
                    dve.wait_ge(le_done, apart(dve, p + 1))
                    for j in two:
                        last = v.max(top[:, j, :], le[:, j, :])
                    last.then_inc(top_done, 1)
                    dve.wait_ge(top_done, p + 1)
                    v.tensor_copy(tops[:, :, 0:TOPB], top[:, :, 0:TOPB]).then_inc(tops_done, 1)
                    dve.wait_ge(tops_done, apart(dve, p + 1))
                    for j in two:
                        last = v.match_replace(kept[:, j, :], tops[:, j, :], le[:, j, :], -2.0)
                    last.then_inc(kept_done, 1)
                    dve.wait_ge(kept_done, p + 1)
                    v.tensor_scalar(nm[:, :, 0:NB], kept[:, :, 0:NB], -1.5, None, ALU.is_gt).then_inc(nm_done, 1)

            steps(dve, body)

            for i, name in enumerate(("bxq", "bxk", "bxv", "bxo")):
                dve.wait_ge(filled[f"pj{i % 2}"], pj_base(3, i % 2) - PJ_FOLD + i // 2 + 1)
                v.tensor_tensor(bias4[:, i, :], bank[f"pj{i % 2}"][:, 0:D], R(name),
                                ALU.add).then_inc(drained[f"pj{i % 2}"], 1)

            def keys(p, r, o):
                dve.wait_ge(filled["pj0"], pj_before(3, 0, p, 1) + 1)
                masked_keys("pj0", r, "bk1", o, drained["pj0"])

            def vals(p, r):
                dve.wait_ge(filled["pj1"], pj_before(3, 1, p, 0) + 1)
                values(3, p, "pj1", R("bv1"))

            def residual(p, r):
                dve.wait_ge(filled["pj1"], pj_after(3, 1, p, 0) + 1)
                add_to_x("pj1", p, x_ready[3], xadds(3, p + 1))

            attention(3, {4: vals, 5: lambda p, r: keys(p, r, 0), 6: lambda p, r: keys(p, r, 1)}, {7: residual})

            def cs(r):
                return lambda j: cx[r][:, j, :]

            def ctx_stats(p, r):
                dve.wait_ge(s_cx[r], landed(p, r))
                stats(cs(r), cbst[r], cmv[r], cst_done, cmv_done, p)

            def ctx_norm(p, r):
                dve.wait_ge(crs_done, p + 1)
                normalise(cn[r], cs(r), cmv[r], crs[r], cn_done)

            def biased(p, r):
                for i in two:
                    dve.wait_ge(filled[f"pj{i}"], pj_before(4, i, p, 1) + 1)
                    dve.wait_ge(rc_done, 2 * p)
                    v.tensor_tensor(rt[:, i], bank[f"pj{i}"][:, :].rearrange("p (j d) -> p j d", j=2),
                                    over(bias4[:, i, :], 2), ALU.add).then_inc(drained[f"pj{i}"], 1)

            def swapped(p, r):
                for i, name in enumerate(("sinq", "sink")):
                    dve.wait_ge(drained[f"pj{i}"], dr_before(4, i, p, 1) + 1)
                    dve.wait_ge(ro_done, 2 * p)
                    src = rt[:, i].rearrange("p j (h d) -> p (j h) d", d=DH)
                    dst = rs[:, i].rearrange("p j (h d) -> p (j h) d", d=DH)
                    sine = over(R(name), 2 * H)
                    v.tensor_tensor(dst[:, :, 0:DH:2], src[:, :, 1:DH:2], sine[:, :, 0:DH:2], ALU.mult)
                    v.tensor_tensor(dst[:, :, 1:DH:2], src[:, :, 0:DH:2], sine[:, :, 1:DH:2],
                                    ALU.mult).then_inc(rs_done, 1)

            def vals(p, r):
                dve.wait_ge(filled["pj0"], pj_before(4, 0, p, 2) + 1)
                values(4, p, "pj0", bias4[:, 2, :])

            def keys(p, r):
                dve.wait_ge(filled["pj0"], pj_before(4, 0, p, 3) + 1)
                for o in range(C):
                    masked_keys("pj0", r, None, o, drained["pj0"])

            def head_stats(p, r):
                for j in two:
                    dve.wait_ge(drained[f"ov{j}"], use(4, f"ov{j}", p) + 1)
                stats(lambda j: hd[r][:, j, :], hst, hmv, hst_done, hmv_done, p)

            def head_norm(p, r):
                dve.wait_ge(hrs_done, p + 1)
                normalise(hn, lambda j: hd[r][:, j, :], hmv, hrs, hn_done)

            def residual(p, r):
                dve.wait_ge(filled["pj1"], pj_after(4, 1, p, 0) + 1)
                add_to_x("pj1", p, x_ready[4], xadds(4, p + 1))

            attention(4, {0: ctx_stats, 1: ctx_norm, 4: biased, 5: lambda p, r: (swapped(p, r), vals(p, r)),
                          7: keys},
                      {5: head_stats, 6: head_norm, 7: residual})

            def body(t, r):
                q = 1 - r
                for e in range(E + SH):
                    if on(t, 0, PAIRS - 1):
                        dve.wait_ge(sg_done, 10 * t + e + 1)
                        dve.wait_ge(filled[f"tp{e % 2}"], least(use(5, f"tp{e % 2}", t, e // 2)))
                        v.tensor_tensor(hm[e % 2][:], sg[e % 2][:], bank[f"sc{e % 2}"][:, T:2 * T],
                                        ALU.mult).then_inc(hm_done, 1)
                    if e >= 2 and on(t, 0, PAIRS - 1):
                        accumulate(t, r, e - 2)
                    if e < 2 and on(t, 1, PAIRS):
                        accumulate(t - 1, q, E + SH - 2 + e)
                    p = t + 1
                    if e == 0 and on(t, -1, PAIRS - 2):
                        x_stats(5, p, q)
                    if e == 1 and on(t, -1, PAIRS - 2):
                        x_norm(5, p, q)
                    if e == 7 and on(t, -1, PAIRS - 2):
                        weights(p, q)

            def accumulate(p, r, e):
                name = f"tp{e % 2}"
                dve.wait_ge(filled[name], use(5, name, p, e // 2) + 1)
                if e:
                    other = f"tp{(e - 1) % 2}"
                    dve.wait_ge(drained[other], least(use(5, other, p, (e - 1) // 2) + 1))
                if e < E:
                    for j in two:
                        last = v.scalar_tensor_tensor(xs(p, j), bank[name][:, j * D:(j + 1) * D],
                                                      comb[r][:, j, e:e + 1], xs(p, j), ALU.mult, ALU.add)
                else:
                    last = v.tensor_tensor(xp(p), bank[name][:, :].rearrange("p (j d) -> p j d", j=2), xp(p),
                                           ALU.add)
                last.then_inc(drained[name], 1)

            def weights(p, r):
                dve.wait_ge(sig_done, apart(dve, p + 1))
                for j in two:
                    last = v.max(top[:, j, :], ls[:, j, :])
                last.then_inc(top5_done, 1)
                dve.wait_ge(top5_done, p + 1)
                v.tensor_copy(tops5[:, :, 0:TOPE], top[:, :, 0:TOPE]).then_inc(tops5_done, 1)
                v.tensor_reduce(den[:], top[:, :, 0:TOPE], AX.X, ALU.add).then_inc(den_done, 1)
                dve.wait_ge(tops5_done, apart(dve, p + 1))
                for j in two:
                    last = v.match_replace(kept5[:, j, :], tops5[:, j, :], ls[:, j, :], -2.0)
                last.then_inc(kept5_done, 1)
                dve.wait_ge(den_done, p + 1)
                v.tensor_scalar(deni[:], den[:], 1e-20, None, ALU.add).then_inc(sel_done, 1)
                dve.wait_ge(kept5_done, p + 1)
                v.scalar_tensor_tensor(sel[:], kept5[:, :, 0:E], -1.5, ls[:, :, 0:E], ALU.is_lt,
                                       ALU.mult).then_inc(sel_done, 1)
                dve.wait_ge(sel_done, 2 * p + 2)
                v.reciprocal(rden[:], deni[:]).then_inc(rden_done, 1)
                dve.wait_ge(rden_done, p + 1)
                for j in two:
                    last = v.tensor_scalar(comb[r][:, j, :], sel[:, j, :], rden[:, j:j + 1], ROUTE_SCALE,
                                           ALU.mult, ALU.mult)
                last.then_inc(comb_done, 1)

            steps(dve, body)

        @block.scalar
        def _(act):
            a = nc.scalar.activation

            def copy_out(name, dst, n, scale=1.0):
                act.wait_ge(filled[name], n + 1)
                src = bank[name][:, 0:int(np.prod(dst.shape[1:]))]
                if len(dst.shape) == 3:
                    src = src.rearrange("p (a b) -> p a b", b=dst.shape[-1])
                a(dst, src, ACT.Copy, scale=scale).then_inc(drained[name], 1)

            def body(t, r):
                q = 1 - r
                p = t - 1
                if on(t, 1, PAIRS):
                    copy_out("tp0", pT[q][:, 0:2, :], use(0, "tp0", p))
                if on(t, 0, PAIRS - 1):
                    act.wait_ge(nmx0_done, t + 1)
                    for j in two:
                        last = a(pr[r][:, j, :], sh[r][:, j, :], ACT.Exp, bias=nmx[r][:, j:j + 1], scale=1.0 / 16.0,
                                 accum_out=rsum[r][:, j:j + 1])
                    last.then_inc(sm0_done, 1)
                if on(t, 1, PAIRS):
                    copy_out("tp1", cnT[q][:], use(0, "tp1", p))
                if on(t, -1, PAIRS - 2):
                    copy_out("pj0", xnT[q][:], pj_before(0, 0, t + 1, 0))
                    copy_out("pj1", qT[q][:], pj_before(0, 1, t + 1, 0))

            steps(act, body)

            def attention(f, vbank, vcount, vslot, before, after):
                def exps(p, n):
                    i, name = n % 2, f"sc{n % 2}"
                    act.wait_ge(mx_done, group(f, p, n) + 1)
                    act.wait_ge(filled[f"tp{i}"], least(use(f, f"tp{i}", p, n // 2)))
                    for k in range(4):
                        h = head(n % 4, k)
                        last = a(pr[i][:, k, :], bank[name][:, k * S:(k + 1) * S], ACT.Exp, bias=mx[i][:, k:k + 1],
                                 accum_out=psum[n // 4][:, h:h + 1])
                    last.then_inc(drained[name], 1)

                def high_probs(p, n):
                    name = f"tp{n % 2}"
                    act.wait_ge(pv_done, least(group(f, p, n) - 1))
                    act.wait_ge(filled[name], use(f, name, p, n // 2) + 1)
                    a(pH[n % 2][:], four(name), ACT.Copy).then_inc(pH_done, 1)

                def value_part(i, p, r, src):
                    ready, done = ((drained[vbank], va_done), (vrest_done, vb_done))[i]
                    act.wait_ge(ready, vcount(p) if i == 0 else att(f, p) + 1)
                    a(v16[r][:, :, :, i, :].rearrange("p j h d -> p (j h) d"),
                      src[:].rearrange("p j (h d) -> p (j h) d", d=DH), ACT.Copy).then_inc(done, 1)

                def body(t, r):
                    q = 1 - r
                    for n in range(8):
                        if n >= 3 and on(t, 0, PAIRS - 1):
                            high_probs(t, n - 3)
                        if n < 3 and on(t, 1, PAIRS):
                            high_probs(t - 1, n + 5)
                        if on(t, 0, PAIRS - 1):
                            exps(t, n)
                        if n in before and on(t, -1, PAIRS - 2):
                            before[n](t + 1, q)
                        if n in after and on(t, 1, PAIRS):
                            after[n](t - 1, q)
                        if n == vslot and on(t, -1, PAIRS - 2):
                            value_part(0, t + 1, q, vf)
                        if n == vslot + 2 and on(t, -1, PAIRS - 2):
                            value_part(1, t + 1, q, vrest)

                steps(act, body)

            def queries(f, i):
                def part(p, r):
                    act.wait_ge(filled["pj1"], pj_before(f, 1, p, 1) + 1)
                    for o in range(C):
                        last = a(qT[r][:, o, :], bank["pj1"][:, o * T:(o + 1) * T], ACT.Identity,
                                 bias=bq[i][:, o:o + 1], scale=(0.25, 0.0625)[i])
                    last.then_inc(drained["pj1"], 1)
                return part

            act.wait_ge(s_bf, 1)
            attention(1, "pj1", lambda p: dr_before(1, 1, p, 0) + 1, 5,
                      {2: lambda p, r: copy_out("pj0", xnT[r][:], pj_before(1, 0, p, 0)),
                       6: queries(1, 0)}, {})

            def body(t, r):
                q = 1 - r
                p = t + 1
                if on(t, 0, PAIRS - 1):
                    copy_out("pj0", nmT[r][:, :], pj_before(2, 0, t, 1))
                for c in range(FF):
                    if c == 1 and on(t, -1, PAIRS - 2):
                        copy_out("pj0", xnT[q][:], pj_before(2, 0, p, 0))
                    if on(t, 0, PAIRS - 1):
                        name = ("sc0", "sc1", "tp0", "tp1")[c % 4]
                        act.wait_ge(filled[name], use(2, name, t, c // 4) + 1)
                        a(hT[r][:, c, :], bank[name][:, 0:T], ACT.Relu, bias=V("b1", c)).then_inc(drained[name], 1)
                    if c == 6 and on(t, -1, PAIRS - 2):
                        act.wait_ge(lsh_done, p + 1)
                        a(le[:, :, 0:NB], lsh[:], ACT.Exp).then_inc(le_done, 1)

            steps(act, body)

            attention(3, "pj1", lambda p: dr_before(3, 1, p, 0) + 1, 5,
                      {2: lambda p, r: copy_out("pj0", xnT[r][:], pj_before(3, 0, p, 0)), 6: queries(3, 1)},
                      {7: lambda p, r: copy_out("pj0", hdT[:], pj_after(3, 0, p, 0))})

            def both(p, r):
                copy_out("pj0", xnT[r][:], pj_before(4, 0, p, 0))
                copy_out("pj1", cnT[r][:], pj_before(4, 1, p, 0))

            attention(4, "pj0", lambda p: dr_before(4, 0, p, 2) + 1, 5,
                      {2: both, 7: lambda p, r: copy_out("pj1", qT[r][:], pj_before(4, 1, p, 2), 0.25)},
                      {7: lambda p, r: copy_out("pj0", hdT[:], pj_after(4, 0, p, 0))})

            def body(t, r):
                q = 1 - r
                p = t + 1
                for e in range(E + SH):
                    if on(t, 0, PAIRS - 1):
                        act.wait_ge(filled[f"sc{e % 2}"], use(5, f"sc{e % 2}", t, e // 2) + 1)
                        act.wait_ge(hm_done, least(10 * t + e - 1))
                        a(sg[e % 2][:], bank[f"sc{e % 2}"][:, 0:T], ACT.Silu).then_inc(sg_done, 1)
                    if e == 4 and on(t, -1, PAIRS - 2):
                        copy_out("pj0", xnT[q][:], pj_before(5, 0, p, 0))
                    if e == 6 and on(t, -1, PAIRS - 2):
                        act.wait_ge(filled["pj1"], pj_before(5, 1, p, 0) + 1)
                        act.wait_ge(comb_done, p)
                        a(ls[:, :, 0:E], bank["pj1"][:, 0:2 * E].rearrange("p (j e) -> p j e", j=2),
                          ACT.Sigmoid).then_inc(sig_done, 1)

            steps(act, body)

        @block.gpsimd
        def _(pool):
            g = nc.gpsimd
            g.memset(started[:, 1:2], 0.0).then_inc(x_ready[1], 1)
            g.memset(mhalf[:], -0.5).then_inc(s_small, 1)
            g.memset(nm[:], 0.0).then_inc(s_small, 1)
            g.memset(tops[:], -1.0).then_inc(s_small, 1)
            g.memset(tops5[:], -1.0).then_inc(s_small, 1)
            g.memset(le[:], -1.0).then_inc(s_small, 1)
            g.memset(ls[:], -1.0).then_inc(s_small, 1)
            pool.wait_ge(s_small, 1)

            def inverse(m, e, dst, s_in, s_mid, s_out_, n):
                pool.wait_ge(s_in, apart(pool, n + 1))
                g.tensor_scalar(e[:], m[:, :, 1:2].rearrange("p j o -> p (j o)"), EPS, None, ALU.add).then_inc(s_mid, 1)
                pool.wait_ge(s_mid, apart(pool, n + 1))
                g.tensor_tensor(dst[:], e[:], mhalf[:, 0:2], ALU.pow).then_inc(s_out_, 1)

            def x_inverse(f, p, r):
                inverse(mv[r], ve[r], rstd[r], mv_done, ve_done, rstd_done, pair(f, p))

            def body(t, r):
                if on(t, -1, PAIRS - 2):
                    x_inverse(0, t + 1, 1 - r)

            steps(pool, body)

            def parts(r, i):
                return v16[r][:, :, :, i, :].rearrange("p j h d -> p (j h) d")

            def by_head(ap):
                return ap.rearrange("p j (h d) -> p (j h) d", d=DH)

            def value_rest(f, p, r):
                pool.wait_ge(va_done, apart(pool, att(f, p) + 1))
                g.tensor_tensor(by_head(vrest[:]), by_head(vf[:]), parts(r, 0), ALU.subtract).then_inc(vrest_done, 1)

            def value_last(f, p, r):
                pool.wait_ge(vb_done, apart(pool, att(f, p) + 1))
                g.tensor_tensor(parts(r, 2), by_head(vrest[:]), parts(r, 1), ALU.subtract).then_inc(vc_done, 1)

            def body(t, r):
                q = 1 - r
                if on(t, -1, PAIRS - 2):
                    x_inverse(1, t + 1, q)
                if on(t, 1, PAIRS):
                    for j in two:
                        pool.wait_ge(drained[f"ov{j}"], apart(pool, use(1, f"ov{j}", t - 1) + 1))
                    g.tensor_tensor(xp(t - 1), xp(t - 1), hd[q][:], ALU.add).then_inc(x_ready[1], 1)
                if on(t, -1, PAIRS - 2):
                    value_rest(1, t + 1, q)
                    value_last(1, t + 1, q)

            steps(pool, body)

            def body(t, r):
                if on(t, -1, PAIRS - 2):
                    x_inverse(2, t + 1, 1 - r)
                    pool.wait_ge(xn_done, apart(pool, pair(2, t + 1) + 1))
                    g.tensor_tensor(xp(t + 1), xp(t + 1), over(R("b2"), 2), ALU.add).then_inc(xadd, 1)

            steps(pool, body)

            for i, name in enumerate(("gq", "gk", "gv", "go")):
                pool.wait_ge(filled[f"pj{i % 2}"], pj_base(3, i % 2) - PJ_FOLD + i // 2 + 1)
                for c in range(C):
                    last = g.tensor_scalar(Wx[:, i, c, :], Wx[:, i, c, :], V(name, c), None, ALU.mult)
                last.then_inc(s_folded, 1)

            def body(t, r):
                q = 1 - r
                p = t + 1
                if on(t, -1, PAIRS - 2):
                    x_inverse(3, p, q)
                    pool.wait_ge(xn_done, apart(pool, pair(3, p) + 1))
                    g.tensor_tensor(xp(p), xp(p), xn[q][:], ALU.add).then_inc(xmid, 1)
                    pool.wait_ge(xmid, apart(pool, p + 1))
                    g.tensor_tensor(xp(p), xp(p), over(R("bo1"), 2), ALU.add).then_inc(xadd, 1)
                if on(t, -1, PAIRS - 2):
                    value_rest(3, p, q)
                    value_last(3, p, q)

            steps(pool, body)

            def body(t, r):
                q = 1 - r
                p = t + 1
                if on(t, -1, PAIRS - 2):
                    x_inverse(4, p, q)
                    pool.wait_ge(rstd_done, apart(pool, pair(4, p) + 1))
                    g.tensor_tensor(v2[q][:], rstd[q][:], rstd[q][:], ALU.mult).then_inc(v2_done, 1)
                    pool.wait_ge(v2_done, apart(pool, 4 * p + 1))
                    g.tensor_tensor(v3[q][:], v2[q][:], mv[q][:, :, 1:2].rearrange("p j o -> p (j o)"),
                                    ALU.mult).then_inc(v2_done, 1)
                    pool.wait_ge(v2_done, apart(pool, 4 * p + 2))
                    g.tensor_scalar(v4[q][:], v3[q][:], EPS, None, ALU.add).then_inc(v2_done, 1)
                    pool.wait_ge(v2_done, apart(pool, 4 * p + 3))
                    g.tensor_tensor(v5[q][:], v4[q][:], mhalf[:, 0:2], ALU.pow).then_inc(v2_done, 1)
                    pool.wait_ge(v2_done, apart(pool, 4 * p + 4))
                    g.tensor_tensor(rq[q][:], v5[q][:], rstd[q][:], ALU.mult).then_inc(rq_done, 1)
                    inverse(cmv[q], cve[q], crs[q], cmv_done, cve_done, crs_done, p)
                    pool.wait_ge(xn_done, apart(pool, pair(4, p) + 1))
                    g.tensor_tensor(xp(p), xp(p), over(bias4[:, 3, :], 2), ALU.add).then_inc(xadd, 1)
                if on(t, 1, PAIRS):
                    inverse(hmv, hve, hrs, hmv_done, hve_done, hrs_done, t - 1)
                if on(t, -1, PAIRS - 2):
                    for i, name in enumerate(("cosq", "cosk")):
                        pool.wait_ge(drained[f"pj{i}"], apart(pool, dr_before(4, i, p, 1) + 1))
                        g.tensor_tensor(rc[:, i].rearrange("p j (h d) -> p (j h) d", d=DH),
                                        rt[:, i].rearrange("p j (h d) -> p (j h) d", d=DH),
                                        over(R(name), 2 * H), ALU.mult).then_inc(rc_done, 1)
                    for i in two:
                        pool.wait_ge(rc_done, apart(pool, 2 * p + i + 1))
                        pool.wait_ge(rs_done, apart(pool, 2 * p + i + 1))
                        g.tensor_tensor(ro[:, i], rc[:, i], rs[:, i], ALU.add).then_inc(ro_done, 1)
                    value_rest(4, p, q)
                    value_last(4, p, q)

            steps(pool, body)

            def body(t, r):
                if on(t, -1, PAIRS - 2):
                    x_inverse(5, t + 1, 1 - r)

            steps(pool, body)



def kernel(**inputs):
    import concourse.bacc as bacc
    from concourse.bass_utils import run_bass_kernel_spmd

    g = {k: np.asarray(v) for k, v in inputs.items()}

    def tok(a):
        return a.transpose(1, 0, 2)

    def chunks(w):
        return w.reshape(-1, P, w.shape[1]).transpose(1, 0, 2)

    def cols(a):
        return a.reshape(-1, P).T

    def rep(a):
        return np.broadcast_to(a.reshape(1, -1), (P, a.size))

    one = np.float32
    inv = (one(1.0) / one(10000.0) ** (np.arange(0, DH, 2, dtype=np.float32) / one(DH))).astype(one)
    at = np.arange(S, dtype=np.float32)
    sign = np.where(np.arange(DH) % 2, 1.0, -1.0).astype(one)

    def angles(pos):
        return np.repeat((pos[:, None] * inv[None, :]).astype(one), 2, axis=1).astype(np.float64)

    aq, ak = angles(at - S // 2), angles(at)
    half = (np.arange(P) // DH) % 2
    vec = {"bq0": cols(g["L0_xattn_bq"]), "bk0": cols(g["L0_xattn_bk"]), "b1": cols(g["L0_ffn_b1"]),
           "bq1": cols(g["L1_attn_b_qkv"][:D]), "bk1": cols(g["L1_attn_b_qkv"][D:2 * D]),
           "gq": cols(g["L1_xattn_ln_q_w"]), "gk": cols(g["L1_xattn_ln_k_w"]),
           "gv": cols(g["L1_xattn_ln_v_w"]), "go": cols(g["L1_xattn_ln_o_w"]),
           "even": (half == 0).astype(one)[:, None], "odd": (half == 1).astype(one)[:, None]}
    rows = {"bv0": rep(g["L0_xattn_bv"]), "br": rep(g["L0_ffn_b_router"]), "b2": rep(g["L0_ffn_b2"]),
            "bv1": rep(g["L1_attn_b_qkv"][2 * D:]), "bo1": rep(g["L1_attn_b_o"]),
            "bxq": rep(g["L1_xattn_b_q"]), "bxk": rep(g["L1_xattn_b_k"]),
            "bxv": rep(g["L1_xattn_b_v"]), "bxo": rep(g["L1_xattn_b_o"]),
            "cosq": np.cos(aq).astype(one), "sinq": (np.sin(aq) * sign).astype(one),
            "cosk": np.cos(ak).astype(one), "sink": (np.sin(ak) * sign).astype(one)}
    expand = np.zeros((P, FF * P), one)
    for b in range(NB):
        expand[b, b * BLOCK:(b + 1) * BLOCK] = NEG
    causal = np.where(np.tril(np.ones((S, S), bool)), 0.0, NEG).astype(one)
    tokens = g["itok_Bx1xSx1_0_63"].reshape(B, S)
    wx = [g[f"L1_xattn_w_{n}"].T for n in "qkvo"]
    lnb = [np.broadcast_to(cols(g[f"L1_xattn_ln_{n}_b"])[:, :, None], (P, C, P)) for n in "qkvo"]
    arrays = dict(
        x=tok(g["x"]), ctxT=chunks(g["ctx_1024"].reshape(B * S, D).T), ctx=tok(g["ctx_1024"]),
        tokq=tokens.T, tokk=np.broadcast_to(tokens[None], (P, B, S)),
        mask=np.ascontiguousarray(g["mask_BxSxS2_bf0"].transpose(1, 0, 2)).view(np.int32), ident=np.eye(P, dtype=one),
        causal=causal, expand=expand, vec=np.concatenate([vec[n] for n in VEC], 1),
        rows=np.concatenate([rows[n] for n in ROWS], 1), lnb=np.stack(lnb, 1),
        w_qk=chunks(g["L0_attn_qk"]), w_ov=chunks(g["L0_attn_ov"]),
        w_q0=chunks(g["L0_xattn_Wq"].T), w_k0=chunks(g["L0_xattn_Wk"].T), w_v0=chunks(g["L0_xattn_Wv"].T),
        w_r0=chunks(g["L0_ffn_w_router"]), w_1=chunks(g["L0_ffn_w1"].T), w_2=chunks(g["L0_ffn_w2"].T),
        w_qkv=chunks(g["L1_attn_w_qkv"].T), w_o1=chunks(g["L1_attn_w_o"].T),
        w_x=np.stack([chunks(w) for w in wx], 1), w_g=chunks(g["L1_ffn_gate_weight"].T),
        w_gate=chunks(g["L1_ffn_w_gate"].reshape(E * EI, D).T), w_up=chunks(g["L1_ffn_w_up"].reshape(E * EI, D).T),
        w_down=g["L1_ffn_w_down"].transpose(2, 0, 1), ws_gate=chunks(g["L1_ffn_ws_gate"].T),
        ws_up=chunks(g["L1_ffn_ws_up"].T), ws_down=chunks(g["L1_ffn_ws_down"].T))
    nc = bacc.Bacc("TRN2", target_bir_lowering=False, num_devices=1)
    feed, args = {}, {}
    for name, a in arrays.items():
        a = np.ascontiguousarray(a)
        feed[f"in_{name}"] = a
        args[name] = nc.dram_tensor(f"in_{name}", a.shape, mybir.dt.from_np(a.dtype), kind="ExternalInput").ap()
    args["out"] = nc.dram_tensor("out_x", (P, B, D), F32, kind="ExternalOutput").ap()
    program(nc, **args)
    got = run_bass_kernel_spmd(nc, [feed], core_ids=[0]).results[0]["out_x"]
    return np.ascontiguousarray(got.transpose(1, 0, 2))
```

```python
from contextlib import ExitStack

import numpy as np

import concourse.bass as bass
from concourse import mybir

P = 128
F32 = mybir.dt.float32
BF16 = mybir.dt.bfloat16
F16 = mybir.dt.float16
U8 = mybir.dt.uint8
I32 = mybir.dt.int32
ALU = mybir.AluOpType
ACT = mybir.ActivationFunctionType
AX = mybir.AxisListType

B, S, D = 16, 128, 256
C = D // P
H, DH = 16, 16
PAIRS = B // 2
T = 2 * S
NB, BLOCK, TOPB = 16, 64, 4
FF = NB * BLOCK // P
E, EI, SHI = 8, 128, 256
SH = SHI // P
TOPE = 2
ROUTE_SCALE = 2.5
EPS = 1e-5
NEG = -1.0e30

VEC = {}
for _name, _n in (("bq0", C), ("bk0", C), ("b1", FF), ("bq1", C), ("bk1", C), ("gq", C), ("gk", C),
                  ("gv", C), ("go", C), ("even", 1), ("odd", 1)):
    VEC[_name] = (sum(n for _, n in VEC.values()), _n)
NVEC = sum(n for _, n in VEC.values())
ROWS = {}
for _name, _n in (("bv0", D), ("br", NB), ("b2", D), ("bv1", D), ("bo1", D), ("bxq", D), ("bxk", D),
                  ("bxv", D), ("bxo", D), ("cosq", DH), ("sinq", DH), ("cosk", DH), ("sink", DH)):
    ROWS[_name] = (sum(n for _, n in ROWS.values()), _n)
NROW = sum(n for _, n in ROWS.values())


def program(nc, x, ctxT, ctx, tokq, tokk, mask, ident, causal, expand, vec, rows, lnb,
            w_qk, w_ov, w_q0, w_k0, w_v0, w_r0, w_1, w_2, w_qkv, w_o1, w_x, w_g, w_gate, w_up,
            w_down, ws_gate, ws_up, ws_down, out):
    stack = ExitStack()
    with stack:
        def sb(name, shape, dt=F32):
            return stack.enter_context(nc.sbuf_tensor(name, shape, dt))

        def sem(name):
            return stack.enter_context(nc.semaphore(name))

        X = sb("X", [P, B, D])
        idn = sb("idn", [P, P])
        idnb = sb("idnb", [P, P], BF16)
        caus = sb("caus", [P, P])
        expb = sb("expb", [P, FF * P], BF16)
        vecs = sb("vecs", [P, NVEC])
        rws = sb("rws", [P, NROW])
        lnbs = sb("lnbs", [P, 4, C, P])
        bias4 = sb("bias4", [P, 4, D])
        mask4 = sb("mask4", [P, B, S // 4], I32)
        mask8 = mask4[:].rearrange("p b s -> p (b s)").bitcast(U8).rearrange("p (b s) -> p b s", b=B)
        tq = sb("tq", [P, B], I32)
        mb0 = sb("mb0", [P, B, S], BF16)
        mb1 = sb("mb1", [P, B, S], BF16)
        bq = [sb(f"bq{i}", [P, C]) for i in range(2)]
        mhalf = sb("mhalf", [P, 4])
        Wqk, Wov = sb("Wqk", [P, C, D]), sb("Wov", [P, C, D])
        Wq0, Wk0, Wv0 = sb("Wq0", [P, C, D]), sb("Wk0", [P, C, D]), sb("Wv0", [P, C, D])
        Wr0 = sb("Wr0", [P, C, NB])
        W1, W2 = sb("W1", [P, C, FF * P]), sb("W2", [P, FF, D])
        Wqkv, Wo1 = sb("Wqkv", [P, C, 3 * D]), sb("Wo1", [P, C, D])
        Wx = sb("Wx", [P, 4, C, D])
        Wg = sb("Wg", [P, C, E])
        Wgate, Wup = sb("Wgate", [P, C, E * EI]), sb("Wup", [P, C, E * EI])
        Wdown = sb("Wdown", [P, E, D])
        Wsg, Wsu, Wsd = sb("Wsg", [P, C, SHI]), sb("Wsu", [P, C, SHI]), sb("Wsd", [P, SH, D])

        def V(name, c=0):
            o = VEC[name][0] + c
            return vecs[:, o:o + 1]

        def R(name):
            o, n = ROWS[name]
            return rws[:, o:o + n]

        two = range(2)
        bst = [sb(f"bst{r}", [P, 2, 6]) for r in two]
        mv = [sb(f"mv{r}", [P, 2, 2]) for r in two]
        ve = [sb(f"ve{r}", [P, 2]) for r in two]
        rstd = [sb(f"rstd{r}", [P, 2]) for r in two]
        xn = [sb(f"xn{r}", [P, 2, D]) for r in two]
        xnT = [sb(f"xnT{r}", [P, C, T]) for r in two]

        names = ["pj0", "pj1", "sc0", "sc1", "tp0", "tp1", "ov0", "ov1"]
        bank = {n: stack.enter_context(nc.psum_tensor(n, [P, 512], F32)) for n in names}
        filled = {n: sem(f"filled_{n}") for n in names}
        drained = {n: sem(f"drained_{n}") for n in names}
        used = dict.fromkeys(names, 0)

        qT = [sb(f"qT{r}", [P, C, T]) for r in two]
        kM = [sb(f"kM{r}", [P, C, 2, 2, S]) for r in two]
        vf, vrest = sb("vf", [P, 2, D]), sb("vrest", [P, 2, D])
        v16 = [sb(f"v16{r}", [P, 2, H, 3, DH], BF16) for r in two]
        mx = [sb(f"mx{r}", [P, 4]) for r in two]
        sh = [sb(f"sh{r}", [P, 2, S]) for r in two]
        pr = [sb(f"pr{r}", [P, 4, S]) for r in two]
        pT = [sb(f"pT{r}", [P, 2, S]) for r in two]
        pH = [sb(f"pH{r}", [P, 4, S], F16) for r in two]
        pL = [sb(f"pL{r}", [P, 4, S], F16) for r in two]
        psum = [sb(f"psum{r}", [P, H]) for r in two]
        hb = [sb(f"hb{r}", [P, H, DH]) for r in two]
        rin = [sb(f"rin{r}", [P, H]) for r in two]
        hd = [sb(f"hd{r}", [P, 2, D]) for r in two]
        cbst = [sb(f"cbst{r}", [P, 2, 6]) for r in two]
        cmv = [sb(f"cmv{r}", [P, 2, 2]) for r in two]
        cve = [sb(f"cve{r}", [P, 2]) for r in two]
        crs = [sb(f"crs{r}", [P, 2]) for r in two]
        v2 = [sb(f"v2{r}", [P, 2]) for r in two]
        rq = [sb(f"rq{r}", [P, 2]) for r in two]
        cn = [sb(f"cn{r}", [P, 2, D]) for r in two]
        cnT = [sb(f"cnT{r}", [P, C, T]) for r in two]
        cT = [sb(f"cT{r}", [P, C, T]) for r in two]
        cx = cT
        hst = sb("hst", [P, 2, 6])
        hmv = sb("hmv", [P, 2, 2])
        hve = sb("hve", [P, 2])
        hrs = sb("hrs", [P, 2])
        hdT = sb("hdT", [P, C, T])
        hT = [sb(f"hT{r}", [P, FF, T]) for r in two]
        tk = hT[0][:].rearrange("p a b -> p (a b)").bitcast(I32).rearrange("p (b s) -> p b s", b=B)
        expd = hT[1][:].rearrange("p a b -> p (a b)")[:, 0:FF * P]
        parts = [hT[i // 2][:].rearrange("p a b -> p (a b)")[:, (i % 2) * 1024:(i % 2 + 1) * 1024]
                 .rearrange("p (i j d) -> p i j d", i=2, j=2) for i in range(4)]
        rt, rc, rs, ro = parts
        lg = sb("lg", [P, 2, NB])
        lmx = sb("lmx", [P, 2])
        lsh = sb("lsh", [P, 2, NB])
        le = sb("le", [P, 2, NB + 8 - TOPB])
        ls = sb("ls", [P, 2, E + 8 - TOPE])
        nmx = [sb(f"nmx{r}", [P, 2]) for r in two]
        rsum = [sb(f"rsum{r}", [P, 2]) for r in two]
        tops5 = sb("tops5", [P, 2, 8])
        kept5 = sb("kept5", [P, 2, E + 8 - TOPE])
        deni, rden = sb("deni", [P, 2]), sb("rden", [P, 2])
        sel = sb("sel", [P, 2, E])
        v3, v4, v5 = ([sb(f"{n}{r}", [P, 2]) for r in two] for n in ("va3", "va4", "va5"))
        hn = sb("hn", [P, 2, D])
        top = sb("top", [P, 2, 8])
        tops = sb("tops", [P, 2, 8])
        kept = sb("kept", [P, 2, NB + 8 - TOPB])
        nm = sb("nm", [P, 2, P])
        nmT = [sb(f"nmT{r}", [P, T], BF16) for r in two]
        sg = [sb(f"sg{r}", [P, T]) for r in two]
        hm = [sb(f"hm{r}", [P, T]) for r in two]
        comb = [sb(f"comb{r}", [P, 2, E]) for r in two]
        den = sb("den", [P, 2])
        started = sb("started", [P, 5])

        def sems(names):
            return [sem(n) for n in names.split()]

        s_x0, s_x1, s_const, s_mask = sems("s_x0 s_x1 s_const s_mask")
        s_ct, s_cx = sems("s_ct0 s_ct1"), sems("s_cx0 s_cx1")
        s_w = [sem(f"s_w{f}") for f in range(6)]
        s_small = sem("s_small")
        s_bf, s_eq, s_mb = sems("s_bf s_eq s_mb")
        s_folded = sem("s_folded")
        (st_done, mv_done, ve_done, rstd_done, xn_done) = sems(
            "st_done mv_done ve_done rstd_done xn_done")
        x_ready = [sem(f"x_ready{f}") for f in range(5)]
        xadd = sem("xadd")
        s_out = sem("s_out")
        mx0_done, nmx0_done, sm0_done, ri0_done = sems(
            "mx0_done nmx0_done sm0_done ri0_done")
        mx_done, pH_done, pv_done, hb_done, va_done, vrest_done, vb_done, vc_done = sems(
            "mx_done pH_done pv_done hb_done va_done vrest_done vb_done vc_done")
        xmid = sem("xmid")
        cst_done, cmv_done, cve_done, crs_done, cn_done = sems(
            "cst_done cmv_done cve_done crs_done cn_done")
        v2_done, rq_done = sems("v2_done rq_done")
        rc_done, rs_done, ro_done, rcq_done, roq_done = sems(
            "rc_done rs_done ro_done rcq_done roq_done")
        hst_done, hmv_done, hve_done, hrs_done, hn_done = sems("hst_done hmv_done hve_done hrs_done hn_done")
        lmx_done, lsh_done, le_done, top_done, tops_done, kept_done, nm_done = sems(
            "lmx_done lsh_done le_done top_done tops_done kept_done nm_done")
        sig_done, top5_done, tops5_done, den_done, kept5_done, sel_done, rden_done, comb_done = sems(
            "sig_done top5_done tops5_done den_done kept5_done sel_done rden_done comb_done")
        sg_done, hm_done = sems("sg_done hm_done")

        def least(n):
            return max(n, 0) if isinstance(n, int) else n

        def past(n):
            return n + 1

        count_reg = {}

        def apart(eng, n):
            if isinstance(n, int):
                return max(n, 0)
            if eng not in count_reg:
                count_reg[eng] = stack.enter_context(eng.register("count"))
            eng.reg_mov(count_reg[eng], n)
            eng.wait_ge(s_const, 48)
            return count_reg[eng]

        def steps(eng, body):
            body(0, 0)
            with eng.Fori(1, PAIRS - 2, 2) as t:
                body(t, 1)
                body(t + 1, 0)
            body(PAIRS - 1, 1)

        def on(t, lo, hi):
            return not isinstance(t, int) or lo <= t <= hi

        PJ_BEFORE = [(1, 1), (2, 2), (2, 1), (2, 2), (3, 4), (1, 1)]
        PJ_AFTER = [(0, 0), (0, 0), (0, 0), (1, 1), (1, 1), (0, 0)]
        PJ_AFTER_D = [(0, 0), (0, 0), (0, 0), (1, 0), (1, 0), (0, 0)]
        PJ_FOLD = 2

        def pj_base(f, b, after=PJ_AFTER):
            n = sum(PAIRS * (PJ_BEFORE[g][b] + after[g][b]) for g in range(f))
            return n + PJ_FOLD * (f >= 3)

        def pj_before(f, b, p, i, after=PJ_AFTER):
            n = pj_base(f, b, after) + PJ_BEFORE[f][b] * p + i
            if isinstance(p, int) and p == 0 and f > 0:
                n -= after[f - 1][b]
            if (f, b, i) == (4, 0, 2):
                return n + after[f][b] * (max(p - 1, 0) if isinstance(p, int) else p - 1)
            return n + after[f][b] * (max(p - 2, 0) if isinstance(p, int) else p - 2)

        def pj_after(f, b, p, i, after=PJ_AFTER):
            n = pj_base(f, b, after) + after[f][b] * p + i
            if isinstance(p, int) and p == PAIRS - 1:
                n += PJ_BEFORE[f + 1][b] if after is PJ_AFTER or (f, b) != (4, 1) else 0
            if (f, b) == (4, 0) and (not isinstance(p, int) or p + 3 <= PAIRS):
                n -= 1
            return n + PJ_BEFORE[f][b] * (min(p + 3, PAIRS) if isinstance(p, int) else p + 3)

        def dr_before(f, b, p, i):
            return pj_before(f, b, p, i, PJ_AFTER_D)

        def dr_step(f, b, p):
            done = p - 1 if not isinstance(p, int) else max(p - 1, 0)
            return pj_base(f, b, PJ_AFTER_D) + PJ_BEFORE[f][b] * (p + 1) + PJ_AFTER_D[f][b] * done

        def dr_after(f, b, p, i):
            return pj_after(f, b, p, i, PJ_AFTER_D)

        PER_PAIR = {"sc0": [1, 4, 2, 4, 4, 5], "sc1": [0, 4, 2, 4, 4, 5],
                    "tp0": [1, 4, 2, 4, 4, 5], "tp1": [1, 4, 2, 4, 4, 5],
                    "ov0": [0, 1, 0, 1, 1, 0], "ov1": [0, 1, 0, 1, 1, 0]}

        def use(f, name, p, i=0):
            return PAIRS * sum(PER_PAIR[name][:f]) + PER_PAIR[name][f] * p + i

        ATT = {1: 0, 3: 1, 4: 2}

        def group(f, p, n):
            return PAIRS * 8 * ATT[f] + 8 * p + n

        def head(g, i):
            return 8 * (i // 2) + 2 * g + i % 2

        def pair(f, p):
            return PAIRS * f + p

        def att(f, p):
            return PAIRS * ATT[f] + p

        def landed(p, r):
            return 8 * p + 16 - 8 * r

        def xadds(f, n):
            return PAIRS * (f - 2) + n

        block = stack.enter_context(nc.Block())

        def xp(p):
            return X[:, bass.ds(2 * p, 2), :]

        def xs(p, j):
            return X[:, bass.ds(2 * p + j, 1), :].rearrange("p o d -> p (o d)")

        def heads(ap):
            return ap.rearrange("p (h d) -> p h d", h=H)

        def over(ap, n):
            return ap.unsqueeze(1).to_broadcast([P, n, ap.shape[1]])

        def along(ap, n):
            return ap.unsqueeze(2).to_broadcast([P, ap.shape[1], n])

        def four(name):
            return bank[name][:, :].rearrange("p (a s) -> p a s", a=4)

        @block.sync
        def _(sp):
            sp.dma_start(X[:, 0:2, :], x[:, 0:2, :]).then_inc(s_x0, 16)
            for dst, src in ((idn, ident), (caus, causal), (vecs, vec)):
                sp.dma_start(dst[:], src).then_inc(s_const, 16)
            for dst, src in ((Wqk, w_qk), (Wov, w_ov)):
                sp.dma_start(dst[:], src).then_inc(s_w[0], 16)
            sp.dma_start(X[:, 2:B, :], x[:, 2:B, :]).then_inc(s_x1, 16)
            for dst, src in ((mask4[:], mask), (tq[:], tokq), (tk, tokk)):
                sp.dma_start(dst, src).then_inc(s_mask, 16)
            for r in two:
                sp.dma_start(cT[r][:], ctxT[:, :, r * T:(r + 1) * T]).then_inc(s_ct[r], 16)
            for dst, src in ((rws, rows), (Wq0, w_q0), (Wk0, w_k0), (Wv0, w_v0)):
                sp.dma_start(dst[:], src).then_inc(s_w[1], 16)
            for dst, src in ((Wr0[:], w_r0), (W1[:], w_1), (W2[:], w_2), (expd, expand)):
                sp.dma_start(dst, src).then_inc(s_w[2], 16)
            for dst, src in ((Wqkv, w_qkv), (Wo1, w_o1)):
                sp.dma_start(dst[:], src).then_inc(s_w[3], 16)
            for dst, src in ((Wx, w_x), (lnbs, lnb)):
                sp.dma_start(dst[:], src).then_inc(s_w[4], 16)
            for dst, src in ((Wg, w_g), (Wgate, w_gate), (Wup, w_up), (Wdown, w_down),
                             (Wsg, ws_gate), (Wsu, ws_up), (Wsd, ws_down)):
                sp.dma_start(dst[:], src).then_inc(s_w[5], 16)
            with sp.Fori(2, PAIRS - 1, 2) as p:
                for r in two:
                    sp.wait_ge(filled["pj1"], pj_before(1, 1, p + r - 2, 0) + 1)
                    sp.dma_start(cT[r][:], ctxT[:, :, bass.ds((p + r) * T, T)]).then_inc(s_ct[r], 16)
            for r in two:
                sp.wait_ge(filled["pj1"], pj_before(1, 1, PAIRS - 2 + r, 0) + 1)
                sp.dma_start(cx[r][:], ctx[:, 2 * r:2 * r + 2, :]).then_inc(s_cx[r], 16)
            with sp.Fori(2, PAIRS - 1, 2) as p:
                for r in two:
                    sp.wait_ge(cn_done, least(p + r - 1))
                    sp.dma_start(cx[r][:], ctx[:, bass.ds(2 * (p + r), 2), :]).then_inc(s_cx[r], 16)
            for p in range(PAIRS):
                sp.wait_ge(drained["tp1"], use(5, "tp1", p, 4) + 1)
                sp.dma_start(out[:, 2 * p:2 * p + 2, :], X[:, 2 * p:2 * p + 2, :]).then_inc(s_out, 16)
            sp.wait_ge(s_out, 16 * PAIRS)

        @block.tensor
        def _(pe):
            mm = nc.tensor.matmul

            def turn(f, p, r):
                pe.wait_ge(xn_done, pair(f, p) + 1)
                pe.wait_ge(drained["pj0"], least(dr_before(f, 0, p, 0)))
                turn_pair("pj0", xn[r])

            def turn_pair(name, src):
                for c in range(C):
                    for j in two:
                        o = c * T + j * S
                        last = nc.tensor.transpose(bank[name][:, o:o + S], src[:, j, c * P:(c + 1) * P], idn[:])
                last.then_inc(filled[name], 1)

            def across(name, w, act, col=0):
                for o in range(C):
                    for c in range(C):
                        last = mm(bank[name][:, o * T:(o + 1) * T], w[:, c, col + o * P:col + (o + 1) * P],
                                  act[:, c, :], start=c == 0, stop=c == C - 1)
                last.then_inc(filled[name], 1)

            def along_tokens(name, act, w, n=D, col=0):
                for j in two:
                    for c in range(C):
                        last = mm(bank[name][:, j * n:(j + 1) * n], act[:, c, j * S:(j + 1) * S],
                                  w[:, c, col:col + n], start=c == 0, stop=c == C - 1)
                last.then_inc(filled[name], 1)


            def body0(t, r):
                q = 1 - r
                if on(t, 1, PAIRS):
                    p = t - 1
                    pe.wait_ge(sm0_done, p + 1)
                    for j in two:
                        last = nc.tensor.transpose(bank["tp0"][:, j * S:(j + 1) * S], pr[q][:, j, :], idn[:])
                    last.then_inc(filled["tp0"], 1)
                if on(t, 0, PAIRS - 1):
                    pe.wait_ge(drained["pj1"], dr_before(0, 1, t, 0) + 1)
                    pe.wait_ge(drained["sc0"], least(use(0, "sc0", t)))
                    for j in two:
                        s = slice(j * S, (j + 1) * S)
                        for c in range(C):
                            last = mm(bank["sc0"][:, s], qT[r][:, c, s], xnT[r][:, c, s],
                                      start=c == 0, stop=c == C - 1)
                    last.then_inc(filled["sc0"], 1)
                if on(t, 1, PAIRS):
                    p = t - 1
                    pe.wait_ge(drained["tp0"], use(0, "tp0", p) + 1)
                    for c in range(C):
                        for j in two:
                            o = c * T + j * S
                            last = mm(bank["tp1"][:, o:o + S], xn[q][:, j, c * P:(c + 1) * P], pT[q][:, j, :],
                                      start=True, stop=True)
                    last.then_inc(filled["tp1"], 1)
                if on(t, -1, PAIRS - 2):
                    turn(0, t + 1, q)
                if on(t, 1, PAIRS):
                    pe.wait_ge(drained["tp1"], use(0, "tp1", p) + 1)
                    pe.wait_ge(x_ready[0], past(p))
                    along_tokens("ov0", cnT[q], Wov)
                if on(t, -1, PAIRS - 2):
                    p = t + 1
                    pe.wait_ge(drained["pj0"], dr_before(0, 0, p, 0) + 1)
                    pe.wait_ge(drained["pj1"], least(dr_before(0, 1, p, 0)))
                    across("pj1", Wqk, xnT[q])


            IDLE = {1: (1, 1, 1, 0, 0, 1, 0, 1), 3: (1, 1, 1, 0, 0, 1, 0, 1), 4: (2, 2, 2, 0, 0, 0, 1, 2)}

            def scores(f, p, r, n, masks):
                name, j, g = f"sc{n % 2}", n // 4, n % 4
                pe.wait_ge(drained[name], least(use(f, name, p, n // 2)))
                if masks is not None:
                    mm(bank[name][:, :], idnb[:],
                       masks[:, bass.ds(2 * p + j, 1), :].to_broadcast([P, 4, S]), start=True, stop=False,
                       skip_group_check=True)
                rows32 = slice(32 * g, 32 * g + 32)
                for c in range(C):
                    last = mm(bank[name][:, c * T:(c + 1) * T], qT[r][rows32, c, j * S:(j + 1) * S],
                              kM[r][rows32, c, j, :, :], start=masks is None, stop=True,
                              skip_group_check=True)
                last.then_inc(filled[name], 1)

            def turn_probs(f, p, n):
                name = f"tp{n % 2}"
                pe.wait_ge(drained[name], use(f, name, p, n // 2))
                for i in range(IDLE[f][(n + 2) % 8]):
                    mm(bank[name][:, :], idnb[:], mb0[:, 0:4, :], start=True, stop=True)
                pe.wait_ge(drained[f"sc{n % 2}"], use(f, f"sc{n % 2}", p, n // 2) + 1)
                for i in range(4):
                    last = nc.tensor.transpose(bank[name][:, i * S:(i + 1) * S], pr[n % 2][:, i, :], idn[:])
                last.then_inc(filled[name], 1)

            def probs_times_values(f, p, r, n):
                j, g = n // 4, n % 4
                pe.wait_ge(drained[f"tp{n % 2}"], use(f, f"tp{n % 2}", p, n // 2) + 1)
                if g == 0 and isinstance(p, int) and p == 0 and j == 0 and f != 4:
                    pe.wait_ge(x_ready[f - 1], past(PAIRS))
                if n == 0:
                    pe.wait_ge(vc_done, att(f, p) + 1)
                for i in range(4):
                    h = head(g, i)
                    o = bank[f"ov{j}"][:, h * 2 * DH:(h + 1) * 2 * DH]
                    mm(o, pH[n % 2][:, i, :], v16[r][:, j, h, 0:2, :], start=True, stop=False,
                       skip_group_check=True)
                    mm(o[:, DH:2 * DH], pH[n % 2][:, i, :], v16[r][:, j, h, 2, :], start=False, stop=False,
                       skip_group_check=True)
                    last = mm(o, pL[n % 2][:, i, :], v16[r][:, j, h, 0:2, :], start=False, stop=True,
                              skip_group_check=True)
                last.then_inc(pv_done, 1)

            def attention(f, masks, before, after, qkv, first={}, first_after={}):
                def body(t, r):
                    q = 1 - r
                    for n in range(8):
                        if n in first and on(t, -1, PAIRS - 2):
                            first[n](t + 1, q)
                        if n in first_after and on(t, 1, PAIRS):
                            first_after[n](t - 1, q)
                        if on(t, 0, PAIRS - 1):
                            if n == 0:
                                qkv(t)
                            scores(f, t, r, n, masks)
                        if n >= 2 and on(t, 0, PAIRS - 1):
                            turn_probs(f, t, n - 2)
                        if n < 2 and on(t, 1, PAIRS):
                            turn_probs(f, t - 1, n + 6)
                        if n >= 4 and on(t, 0, PAIRS - 1):
                            probs_times_values(f, t, r, n - 4)
                        if n < 4 and on(t, 1, PAIRS):
                            probs_times_values(f, t - 1, q, n + 4)
                        if n in before and on(t, -1, PAIRS - 2):
                            before[n](t + 1, q)
                        if n in after and on(t, 1, PAIRS):
                            after[n](t - 1, q)

                return body


            def project_q1(p, r):
                pe.wait_ge(drained["pj1"], least(dr_before(1, 1, p, 1)))
                across("pj1", Wq0, xnT[r])

            def project_k1(p, r):
                pe.wait_ge(s_ct[r], landed(p, r))
                pe.wait_ge(drained["pj0"], dr_before(1, 0, p, 0) + 1)
                across("pj0", Wk0, cT[r])

            def project_v1(p, r):
                pe.wait_ge(drained["pj1"], least(dr_before(1, 1, p, 0)))
                along_tokens("pj1", cT[r], Wv0)

            def ready1(p):
                for b in two:
                    pe.wait_ge(drained[f"pj{b}"], least(dr_step(1, b, p)))

            body1 = attention(1, mb0, {2: lambda p, r: turn(1, p, r), 3: project_k1, 4: project_v1, 6: project_q1},
                      {}, ready1)


            def second(p, r, j):
                if j == 0:
                    pe.wait_ge(drained["tp1"], use(2, "tp1", p, 1) + 1)
                    pe.wait_ge(x_ready[2], past(p))
                for d in range(FF):
                    last = mm(bank["ov0"][:, j * D:(j + 1) * D], hT[r][:, d, j * S:(j + 1) * S],
                              W2[:, d, :], start=d == 0, stop=d == FF - 1)
                if j == 1:
                    last.then_inc(filled["ov0"], 1)

            def body2(t, r):
                q = 1 - r
                if on(t, 1, PAIRS):
                    second(t - 1, q, 0)
                if on(t, 0, PAIRS - 1):
                    pe.wait_ge(nm_done, t + 1)
                    pe.wait_ge(drained["pj0"], dr_before(2, 0, t, 1))
                    for j in two:
                        last = nc.tensor.transpose(bank["pj0"][:, j * S:(j + 1) * S], nm[:, j, :], idn[:])
                    last.then_inc(filled["pj0"], 1)
                if on(t, 1, PAIRS):
                    second(t - 1, q, 1)
                if on(t, 0, PAIRS - 1):
                    pe.wait_ge(drained["pj0"], dr_before(2, 0, t, 1) + 1)
                for c in range(FF):
                    if c == 1 and on(t, -1, PAIRS - 2):
                        turn(2, t + 1, q)
                    if c == 3 and on(t, -1, PAIRS - 2):
                        p = t + 1
                        pe.wait_ge(drained["pj0"], dr_before(2, 0, p, 0) + 1)
                        pe.wait_ge(drained["pj1"], dr_before(2, 1, p, 0))
                        along_tokens("pj1", xnT[q], Wr0, NB)
                    if on(t, 0, PAIRS - 1):
                        name = ("sc0", "sc1", "tp0", "tp1")[c % 4]
                        pe.wait_ge(drained[name], use(2, name, t, c // 4))
                        mm(bank[name][:, 0:T], expb[:, c * P:(c + 1) * P], nmT[r][:, :], start=True, stop=False)
                        for d in range(C):
                            last = mm(bank[name][:, 0:T], W1[:, d, c * P:(c + 1) * P], xnT[r][:, d, :],
                                      start=False, stop=d == C - 1)
                        last.then_inc(filled[name], 1)



            def project_q3(p, r):
                pe.wait_ge(drained["pj1"], least(dr_before(3, 1, p, 1)))
                across("pj1", Wqkv, xnT[r], 0)

            def project_k3(p, r):
                pe.wait_ge(drained["pj0"], least(dr_before(3, 0, p, 1)))
                across("pj0", Wqkv, xnT[r], D)

            def project_v3(p, r):
                pe.wait_ge(drained["pj0"], dr_before(3, 0, p, 0) + 1)
                pe.wait_ge(drained["pj1"], least(dr_before(3, 1, p, 0)))
                pe.wait_ge(x_ready[3], least(past(p - 2)))
                along_tokens("pj1", xnT[r], Wqkv, D, 2 * D)

            def turn_heads3(p, r):
                for j in two:
                    pe.wait_ge(drained[f"ov{j}"], use(3, f"ov{j}", p) + 1)
                pe.wait_ge(drained["pj0"], least(dr_after(3, 0, p, 0)))
                turn_pair("pj0", hd[r])

            def project_out3(p, r):
                pe.wait_ge(drained["pj0"], dr_after(3, 0, p, 0) + 1)
                pe.wait_ge(drained["pj1"], least(dr_after(3, 1, p, 0)))
                pe.wait_ge(x_ready[3], past(p))
                along_tokens("pj1", hdT, Wo1)

            def ready3(p):
                for b in two:
                    pe.wait_ge(drained[f"pj{b}"], least(dr_step(3, b, p)))

            body3 = attention(3, None, {2: lambda p, r: turn(3, p, r), 3: project_k3, 4: project_v3, 6: project_q3},
                      {7: project_out3}, ready3, {}, {7: turn_heads3})


            def turn_context(p, r):
                pe.wait_ge(cn_done, p + 1)
                pe.wait_ge(drained["pj1"], least(dr_before(4, 1, p, 0)))
                pe.wait_ge(x_ready[4], least(past(p - 2)))
                turn_pair("pj1", cn[r])

            def project_k4(p, r):
                pe.wait_ge(drained["pj1"], dr_before(4, 1, p, 0) + 1)
                along_tokens("pj1", cnT[r], Wx[:, 1])
                turn(4, p, r)

            def project_q4(p, r):
                pe.wait_ge(drained["pj0"], dr_before(4, 0, p, 0) + 1)
                along_tokens("pj0", xnT[r], Wx[:, 0])

            def project_v4(p, r):
                pe.wait_ge(drained["pj1"], least(dr_before(4, 1, p, 2)))
                along_tokens("pj1", cnT[r], Wx[:, 2])

            def turn_k(p, r):
                pe.wait_ge(ro_done, p + 1)
                pe.wait_ge(drained["pj1"], least(dr_before(4, 1, p, 3)))
                turn_pair("pj1", ro[:, 1])

            def turn_q(p, r):
                pe.wait_ge(roq_done, p + 1)
                pe.wait_ge(drained["pj0"], least(dr_before(4, 0, p, 2)))
                turn_pair("pj0", ro[:, 0])

            def turn_heads4(p, r):
                pe.wait_ge(hn_done, p + 1)
                pe.wait_ge(drained["pj0"], least(dr_after(4, 0, p, 0)))
                turn_pair("pj0", hn)

            def project_out4(p, r):
                pe.wait_ge(drained["pj0"], dr_after(4, 0, p, 0) + 1)
                pe.wait_ge(drained["pj1"], least(dr_after(4, 1, p, 0)))
                pe.wait_ge(x_ready[4], past(p))
                along_tokens("pj1", hdT, Wx[:, 3])

            def ready4(p):
                for b in two:
                    pe.wait_ge(drained[f"pj{b}"], least(dr_step(4, b, p)))

            body4 = attention(4, mb1, {2: turn_context, 3: project_k4, 4: project_q4, 5: project_v4, 6: turn_k},
                      {6: turn_heads4, 7: project_out4}, ready4, {7: turn_q})


            def up(t, r, e):
                name = f"sc{e % 2}"
                if isinstance(t, int) and t == 0 and e < 2:
                    pe.wait_ge(drained[name], least(use(5, name, 0)))
                else:
                    pe.wait_ge(hm_done, least(10 * t + e - 1))
                for i, w in enumerate((Wgate, Wup) if e < E else (Wsg, Wsu)):
                    o = e * P if e < E else (e - E) * P
                    for c in range(C):
                        last = mm(bank[name][:, i * T:(i + 1) * T], w[:, c, o:o + P], xnT[r][:, c, :],
                                  start=c == 0, stop=c == C - 1)
                last.then_inc(filled[name], 1)

            def down(t, e):
                name = f"tp{e % 2}"
                pe.wait_ge(hm_done, 10 * t + e + 1)
                pe.wait_ge(drained[name], least(use(5, name, t, e // 2)))
                w = Wdown[:, e, :] if e < E else Wsd[:, e - E, :]
                for j in two:
                    last = mm(bank[name][:, j * D:(j + 1) * D], hm[e % 2][:, j * S:(j + 1) * S], w,
                              start=True, stop=True)
                last.then_inc(filled[name], 1)

            def body5(t, r):
                q = 1 - r
                if on(t, 0, PAIRS - 1):
                    pe.wait_ge(drained["pj0"], dr_before(5, 0, t, 0) + 1)
                for e in range(E + SH):
                    if on(t, 0, PAIRS - 1):
                        up(t, r, e)
                        if e >= 2:
                            down(t, e - 2)
                    if on(t, 1, PAIRS) and e < 2:
                        down(t - 1, E + SH - 2 + e)
                    if e == 4 and on(t, -1, PAIRS - 2):
                        turn(5, t + 1, q)
                    if e == 6 and on(t, -1, PAIRS - 2):
                        pe.wait_ge(drained["pj0"], dr_before(5, 0, t + 1, 0) + 1)
                        if isinstance(t, int) and t == -1:
                            pe.wait_ge(drained["pj1"], least(dr_before(5, 1, 0, 0)))
                            pe.wait_ge(x_ready[4], past(PAIRS - 1))
                        else:
                            pe.wait_ge(sig_done, t + 1)
                        along_tokens("pj1", xnT[q], Wg, E)

            pe.wait_ge(s_const, 48)
            pe.wait_ge(s_w[0], 32)
            body0(-1, 1)
            steps(pe, body0)
            pe.wait_ge(s_w[1], 64)
            body1(-1, 1)
            body0(PAIRS, 0)
            pe.wait_ge(s_mb, 1)
            pe.wait_ge(s_bf, 1)
            steps(pe, body1)
            pe.wait_ge(s_w[2], 64)
            body2(-1, 1)
            body1(PAIRS, 0)
            pe.wait_ge(s_bf, 2)
            steps(pe, body2)
            pe.wait_ge(s_w[4], 32)
            for i in range(4):
                name = f"pj{i % 2}"
                pe.wait_ge(drained[name], least(pj_base(3, i % 2, PJ_AFTER_D) - PJ_FOLD + i // 2))
                for c in range(C):
                    last = mm(bank[name][:, 0:D], lnbs[:, i, c, :], Wx[:, i, c, :], start=c == 0, stop=c == C - 1)
                last.then_inc(filled[name], 1)
            pe.wait_ge(s_w[3], 32)
            body3(-1, 1)
            body2(PAIRS, 0)
            steps(pe, body3)
            pe.wait_ge(s_folded, 4)
            body4(-1, 1)
            body3(PAIRS, 0)
            pe.wait_ge(s_mb, 2)
            pe.wait_ge(x_ready[3], past(PAIRS))
            steps(pe, body4)
            pe.wait_ge(s_w[5], 7 * 16)
            body5(-1, 1)
            pe.wait_ge(sig_done, 1)
            body4(PAIRS, 0)
            pe.wait_ge(x_ready[4], past(PAIRS))
            steps(pe, body5)
            body5(PAIRS, 0)

        @block.vector
        def _(dve):
            v = nc.vector

            def stats(src, b, m, s_b, s_m, n):
                for j in two:
                    last = v.bn_stats(b[:, j, :], src(j))
                last.then_inc(s_b, 1)
                dve.wait_ge(s_b, apart(dve, n + 1))
                for j in two:
                    last = v.bn_aggr(m[:, j, :], b[:, j, :])
                last.then_inc(s_m, 1)

            def x_stats(f, p, r):
                if f == 0:
                    dve.wait_ge(s_x0 if isinstance(p, int) and p == 0 else s_x1, 16)
                else:
                    dve.wait_ge(x_ready[f - 1], past(p + 1))
                stats(lambda j: xs(p, j), bst[r], mv[r], st_done, mv_done, pair(f, p))

            def normalise(dst, src, m, s, done):
                for j in two:
                    last = v.tensor_scalar(dst[:, j, :], src(j), m[:, j, 0:1], s[:, j:j + 1],
                                           ALU.subtract, ALU.mult)
                last.then_inc(done, 1)

            def x_norm(f, p, r):
                if f == 4:
                    dve.wait_ge(rq_done, p + 1)
                else:
                    dve.wait_ge(rstd_done, pair(f, p) + 1)
                if f == 3:
                    dve.wait_ge(xadd, least(xadds(3, p - 1)))
                normalise(xn[r], lambda j: xs(p, j), mv[r], rq[r] if f == 4 else rstd[r], xn_done)

            def body0(t, r):
                q = 1 - r
                if on(t, -1, PAIRS - 2):
                    x_stats(0, t + 1, q)
                if on(t, 0, PAIRS - 1):
                    dve.wait_ge(filled["sc0"], use(0, "sc0", t) + 1)
                    v.tensor_tensor(sh[r][:, 0:2, :], bank["sc0"][:, 0:T].rearrange("p (j s) -> p j s", j=2),
                                    over(caus[:], 2), ALU.add).then_inc(drained["sc0"], 1)
                    dve.wait_ge(drained["sc0"], use(0, "sc0", t) + 1)
                    v.tensor_reduce(mx[r][:, 0:2], sh[r][:, 0:2, :], AX.X, ALU.max).then_inc(mx0_done, 1)
                    dve.wait_ge(mx0_done, t + 1)
                    v.tensor_scalar(nmx[r][:, 0:2], mx[r][:, 0:2], -1.0 / 16.0, None, ALU.mult).then_inc(nmx0_done, 1)
                if on(t, 1, PAIRS):
                    p = t - 1
                    dve.wait_ge(sm0_done, p + 1)
                    v.reciprocal(rin[q][:, 0:2], rsum[q][:, 0:2]).then_inc(ri0_done, 1)
                if on(t, -1, PAIRS - 2):
                    if on(t, 1, PAIRS):
                        dve.wait_ge(filled["tp1"], least(use(0, "tp1", t - 1) + 1))
                    x_norm(0, t + 1, q)
                if on(t, 1, PAIRS):
                    p = t - 1
                    dve.wait_ge(ri0_done, p + 1)
                    dve.wait_ge(filled["ov0"], p + 1)
                    for j in two:
                        last = v.scalar_tensor_tensor(xs(p, j), bank["ov0"][:, j * D:(j + 1) * D],
                                                      rin[q][:, j:j + 1], xs(p, j), ALU.mult, ALU.add)
                    last.then_inc(x_ready[0], 1)


            def maxima(f, p, n):
                name = f"sc{n % 2}"
                dve.wait_ge(filled[name], use(f, name, p, n // 2) + 1)
                v.tensor_reduce(mx[n % 2][:, :], four(name), AX.X, ALU.max, negate=True).then_inc(mx_done, 1)

            def low_probs(f, p, n):
                name = f"tp{n % 2}"
                dve.wait_ge(pH_done, group(f, p, n) + 1)
                v.tensor_tensor(pL[n % 2][:], four(name), pH[n % 2][:], ALU.subtract).then_inc(drained[name], 1)

            def inverse_sums(f, p, j):
                for i in two:
                    dve.wait_ge(drained[f"sc{i}"], use(f, f"sc{i}", p, 2 * j + 1) + 1)
                v.reciprocal(rin[j][:], psum[j][:])

            def norm_heads(f, p, r, j):
                dve.wait_ge(pv_done, group(f, p, 4 * j + 4))
                v.tensor_reduce(hb[j][:], bank[f"ov{j}"][:, :].rearrange("p (h a d) -> p h d a", h=H, a=2),
                                AX.X, ALU.add).then_inc(hb_done, 1)
                dve.wait_ge(hb_done, 2 * att(f, p) + j + 1)
                v.tensor_tensor(heads(hd[r][:, j, :]), hb[j][:], along(rin[j][:], DH),
                                ALU.mult).then_inc(drained[f"ov{j}"], 1)

            def masked_keys(name, r, bias, o, done):
                src = bank[name][:, o * T:(o + 1) * T].rearrange("p (j s) -> p j s", j=2)
                for i, m in enumerate(("even", "odd")):
                    if bias:
                        last = v.tensor_scalar(kM[r][:, o, :, i, :], src, V(bias, o), V(m), ALU.add, ALU.mult)
                    else:
                        last = v.tensor_scalar(kM[r][:, o, :, i, :], src, V(m), None, ALU.mult)
                if o == C - 1:
                    last.then_inc(done, 1)

            def values(f, p, name, bias):
                dve.wait_ge(vc_done, least(att(f, p)))
                v.tensor_tensor(vf[:], bank[name][:, :].rearrange("p (j d) -> p j d", j=2), over(bias, 2),
                                ALU.add).then_inc(drained[name], 1)

            def add_to_x(name, p, done, n):
                dve.wait_ge(xadd, n)
                v.tensor_tensor(xp(p), bank[name][:, :].rearrange("p (j d) -> p j d", j=2), xp(p),
                                ALU.add).then_inc(done, 1)

            def attention(f, before, after, residual=None):
                def body(t, r):
                    q = 1 - r
                    for n in range(8):
                        if n == 0 and on(t, -1, PAIRS - 2):
                            x_stats(f, t + 1, q)
                        if on(t, 0, PAIRS - 1):
                            maxima(f, t, n)
                        if n >= 3 and on(t, 0, PAIRS - 1):
                            low_probs(f, t, n - 3)
                        if n < 3 and on(t, 1, PAIRS):
                            low_probs(f, t - 1, n + 5)
                        if n == 0 and on(t, 1, PAIRS):
                            inverse_sums(f, t - 1, 1)
                            norm_heads(f, t - 1, q, 0)
                        if n == 4 and on(t, 1, PAIRS):
                            norm_heads(f, t - 1, q, 1)
                        if n == 4 and on(t, 0, PAIRS - 1):
                            inverse_sums(f, t, 0)
                        if n == (2 if f == 4 else 1) and on(t, -1, PAIRS - 2):
                            x_norm(f, t + 1, q)
                        if n in after and on(t, 1, PAIRS):
                            after[n](t - 1, q)
                        if n in before and on(t, -1, PAIRS - 2):
                            before[n](t + 1, q)
                        if n == 7 and residual is not None and on(t, 1, PAIRS):
                            residual(t - 1, q)

                return body

            def keys1(p, r, o):
                dve.wait_ge(filled["pj0"], pj_before(1, 0, p, 1) + 1)
                masked_keys("pj0", r, "bk0", o, drained["pj0"])

            def vals1(p, r):
                dve.wait_ge(filled["pj1"], pj_before(1, 1, p, 0) + 1)
                values(1, p, "pj1", R("bv0"))

            body1 = attention(1, {4: lambda p, r: keys1(p, r, 0), 5: lambda p, r: (vals1(p, r), keys1(p, r, 1))}, {})


            def body2(t, r):
                q = 1 - r
                p = t + 1
                if on(t, -1, PAIRS - 2):
                    x_stats(2, p, q)
                    x_norm(2, p, q)
                if on(t, 1, PAIRS):
                    dve.wait_ge(filled["ov0"], PAIRS + t)
                    add_to_x("ov0", t - 1, x_ready[2], xadds(2, t))
                if on(t, -1, PAIRS - 2):
                    dve.wait_ge(filled["pj1"], pj_before(2, 1, p, 0) + 1)
                    v.tensor_tensor(lg[:], bank["pj1"][:, 0:2 * NB].rearrange("p (j e) -> p j e", j=2),
                                    over(R("br"), 2), ALU.add).then_inc(drained["pj1"], 1)
                    dve.wait_ge(drained["pj1"], dr_before(2, 1, p, 0) + 1)
                    v.tensor_reduce(lmx[:], lg[:], AX.X, ALU.max).then_inc(lmx_done, 1)
                    dve.wait_ge(lmx_done, p + 1)
                    v.tensor_tensor(lsh[:], lg[:], along(lmx[:], NB), ALU.subtract).then_inc(lsh_done, 1)
                    dve.wait_ge(le_done, apart(dve, p + 1))
                    for j in two:
                        last = v.max(top[:, j, :], le[:, j, :])
                    last.then_inc(top_done, 1)
                    dve.wait_ge(top_done, p + 1)
                    v.tensor_copy(tops[:, :, 0:TOPB], top[:, :, 0:TOPB]).then_inc(tops_done, 1)
                    dve.wait_ge(tops_done, apart(dve, p + 1))
                    for j in two:
                        last = v.match_replace(kept[:, j, :], tops[:, j, :], le[:, j, :], -2.0)
                    last.then_inc(kept_done, 1)
                    dve.wait_ge(kept_done, p + 1)
                    v.tensor_scalar(nm[:, :, 0:NB], kept[:, :, 0:NB], -1.5, None, ALU.is_gt).then_inc(nm_done, 1)


            def keys3(p, r, o):
                dve.wait_ge(filled["pj0"], pj_before(3, 0, p, 1) + 1)
                masked_keys("pj0", r, "bk1", o, drained["pj0"])

            def vals3(p, r):
                dve.wait_ge(filled["pj1"], pj_before(3, 1, p, 0) + 1)
                values(3, p, "pj1", R("bv1"))

            def residual3(p, r):
                dve.wait_ge(filled["pj1"], pj_after(3, 1, p, 0) + 1)
                add_to_x("pj1", p, x_ready[3], xadds(3, p + 1))

            body3 = attention(3, {4: lambda p, r: keys3(p, r, 0), 5: lambda p, r: (vals3(p, r), keys3(p, r, 1))},
                              {}, residual3)

            def cs(r):
                return lambda j: cx[r][:, j, :]

            def ctx_stats(p, r):
                dve.wait_ge(s_cx[r], landed(p, r))
                stats(cs(r), cbst[r], cmv[r], cst_done, cmv_done, p)

            def ctx_norm(p, r):
                dve.wait_ge(crs_done, p + 1)
                normalise(cn[r], cs(r), cmv[r], crs[r], cn_done)

            def biased(p, i):
                dve.wait_ge(filled[f"pj{i}"], pj_before(4, i, p, 1) + 1)
                v.tensor_tensor(rt[:, i], bank[f"pj{i}"][:, :].rearrange("p (j d) -> p j d", j=2),
                                over(bias4[:, i, :], 2), ALU.add).then_inc(drained[f"pj{i}"], 1)

            def swapped(p, i):
                dve.wait_ge(drained[f"pj{i}"], dr_before(4, i, p, 1) + 1)
                src = rt[:, i].rearrange("p j (h d) -> p (j h) d", d=DH)
                dst = rs[:, i].rearrange("p j (h d) -> p (j h) d", d=DH)
                sine = over(R(("sinq", "sink")[i]), 2 * H)
                v.tensor_tensor(dst[:, :, 0:DH:2], src[:, :, 1:DH:2], sine[:, :, 0:DH:2], ALU.mult)
                return v.tensor_tensor(dst[:, :, 1:DH:2], src[:, :, 0:DH:2], sine[:, :, 1:DH:2], ALU.mult)

            def rotate_k(p, r):
                dve.wait_ge(rc_done, least(p))
                biased(p, 1)
                dve.wait_ge(ro_done, least(p))
                swapped(p, 1).then_inc(rs_done, 1)

            def rotate_q(p, r):
                biased(p, 0)
                swapped(p, 0)
                v.tensor_tensor(rc[:, 0].rearrange("p j (h d) -> p (j h) d", d=DH),
                                rt[:, 0].rearrange("p j (h d) -> p (j h) d", d=DH),
                                over(R("cosq"), 2 * H), ALU.mult).then_inc(rcq_done, 1)

            def rotated_q(p, r):
                dve.wait_ge(rcq_done, p + 1)
                v.tensor_tensor(ro[:, 0], rc[:, 0], rs[:, 0], ALU.add).then_inc(roq_done, 1)

            def vals4(p, r):
                dve.wait_ge(filled["pj1"], pj_before(4, 1, p, 2) + 1)
                values(4, p, "pj1", bias4[:, 2, :])

            def keys4(p, r, o):
                dve.wait_ge(filled["pj1"], pj_before(4, 1, p, 3) + 1)
                masked_keys("pj1", r, None, o, drained["pj1"])

            def head_stats(p, r):
                for j in two:
                    dve.wait_ge(drained[f"ov{j}"], use(4, f"ov{j}", p) + 1)
                stats(lambda j: hd[r][:, j, :], hst, hmv, hst_done, hmv_done, p)

            def head_norm(p, r):
                dve.wait_ge(hrs_done, p + 1)
                normalise(hn, lambda j: hd[r][:, j, :], hmv, hrs, hn_done)

            def residual4(p, r):
                dve.wait_ge(filled["pj1"], pj_after(4, 1, p, 0) + 1)
                add_to_x("pj1", p, x_ready[4], xadds(4, p + 1))

            body4 = attention(4, {0: ctx_stats, 1: ctx_norm, 3: rotate_k,
                          4: rotate_q, 5: lambda p, r: (rotated_q(p, r), vals4(p, r)),
                          6: lambda p, r: keys4(p, r, 0), 7: lambda p, r: keys4(p, r, 1)},
                      {4: head_stats, 5: head_norm}, residual4)

            def body5(t, r):
                q = 1 - r
                for e in range(E + SH):
                    if on(t, 0, PAIRS - 1):
                        dve.wait_ge(sg_done, 10 * t + e + 1)
                        dve.wait_ge(filled[f"tp{e % 2}"], least(use(5, f"tp{e % 2}", t, e // 2)))
                        v.tensor_tensor(hm[e % 2][:], sg[e % 2][:], bank[f"sc{e % 2}"][:, T:2 * T],
                                        ALU.mult).then_inc(hm_done, 1)
                    if e >= 2 and on(t, 0, PAIRS - 1):
                        accumulate(t, r, e - 2)
                    if e < 2 and on(t, 1, PAIRS):
                        accumulate(t - 1, q, E + SH - 2 + e)
                    p = t + 1
                    if e == 0 and on(t, -1, PAIRS - 2):
                        x_stats(5, p, q)
                    if e == 1 and on(t, -1, PAIRS - 2):
                        x_norm(5, p, q)
                    if e == 7 and on(t, -1, PAIRS - 2):
                        weights(p, q)

            def accumulate(p, r, e):
                name = f"tp{e % 2}"
                dve.wait_ge(filled[name], use(5, name, p, e // 2) + 1)
                if e:
                    other = f"tp{(e - 1) % 2}"
                    dve.wait_ge(drained[other], least(use(5, other, p, (e - 1) // 2) + 1))
                if e < E:
                    for j in two:
                        last = v.scalar_tensor_tensor(xs(p, j), bank[name][:, j * D:(j + 1) * D],
                                                      comb[r][:, j, e:e + 1], xs(p, j), ALU.mult, ALU.add)
                else:
                    last = v.tensor_tensor(xp(p), bank[name][:, :].rearrange("p (j d) -> p j d", j=2), xp(p),
                                           ALU.add)
                last.then_inc(drained[name], 1)

            def weights(p, r):
                dve.wait_ge(sig_done, apart(dve, p + 1))
                for j in two:
                    last = v.max(top[:, j, :], ls[:, j, :])
                last.then_inc(top5_done, 1)
                dve.wait_ge(top5_done, p + 1)
                v.tensor_copy(tops5[:, :, 0:TOPE], top[:, :, 0:TOPE]).then_inc(tops5_done, 1)
                v.tensor_reduce(den[:], top[:, :, 0:TOPE], AX.X, ALU.add).then_inc(den_done, 1)
                dve.wait_ge(tops5_done, apart(dve, p + 1))
                for j in two:
                    last = v.match_replace(kept5[:, j, :], tops5[:, j, :], ls[:, j, :], -2.0)
                last.then_inc(kept5_done, 1)
                dve.wait_ge(den_done, p + 1)
                v.tensor_scalar(deni[:], den[:], 1e-20, None, ALU.add).then_inc(sel_done, 1)
                dve.wait_ge(kept5_done, p + 1)
                v.scalar_tensor_tensor(sel[:], kept5[:, :, 0:E], -1.5, ls[:, :, 0:E], ALU.is_lt,
                                       ALU.mult).then_inc(sel_done, 1)
                dve.wait_ge(sel_done, 2 * p + 2)
                v.reciprocal(rden[:], deni[:]).then_inc(rden_done, 1)
                dve.wait_ge(rden_done, p + 1)
                for j in two:
                    last = v.tensor_scalar(comb[r][:, j, :], sel[:, j, :], rden[:, j:j + 1], ROUTE_SCALE,
                                           ALU.mult, ALU.mult)
                last.then_inc(comb_done, 1)

            for f in (0, 2, 3, 4):
                v.memset(started[:, f:f + 1], 0.0).then_inc(x_ready[f], 1)
            body0(-1, 1)
            dve.wait_ge(s_const, 48)
            for i in two:
                o = VEC[f"bq{i}"][0]
                v.tensor_scalar(bq[i][:], vecs[:, o:o + C], (0.25, 0.0625)[i], None, ALU.mult)
            v.tensor_copy(idnb[:], idn[:]).then_inc(s_bf, 1)
            steps(dve, body0)
            dve.wait_ge(s_w[1], 64)
            body1(-1, 1)
            body0(PAIRS, 0)
            dve.wait_ge(s_mask, 48)
            v.tensor_scalar(mb0[:], mask8, NEG, None, ALU.mult).then_inc(s_mb, 1)
            v.tensor_tensor(mb1[:], tk, along(tq[:], S), ALU.not_equal).then_inc(s_eq, 1)
            dve.wait_ge(s_eq, 1)
            v.scalar_tensor_tensor(mb1[:], mb1[:], NEG, over(caus[:], B), ALU.mult, ALU.add).then_inc(s_mb, 1)
            steps(dve, body1)
            dve.wait_ge(s_w[2], 64)
            v.tensor_copy(expb[:], expd).then_inc(s_bf, 1)
            body2(-1, 1)
            body1(PAIRS, 0)
            steps(dve, body2)
            for i, name in enumerate(("bxq", "bxk", "bxv", "bxo")):
                dve.wait_ge(filled[f"pj{i % 2}"], pj_base(3, i % 2) - PJ_FOLD + i // 2 + 1)
                v.tensor_tensor(bias4[:, i, :], bank[f"pj{i % 2}"][:, 0:D], R(name),
                                ALU.add).then_inc(drained[f"pj{i % 2}"], 1)
            body3(-1, 1)
            body2(PAIRS, 0)
            steps(dve, body3)
            body4(-1, 1)
            body3(PAIRS, 0)
            steps(dve, body4)
            body5(-1, 1)
            body4(PAIRS, 0)
            steps(dve, body5)
            body5(PAIRS, 0)

        @block.scalar
        def _(act):
            a = nc.scalar.activation

            def copy_out(name, dst, n, scale=1.0):
                act.wait_ge(filled[name], n + 1)
                src = bank[name][:, 0:int(np.prod(dst.shape[1:]))]
                if len(dst.shape) == 3:
                    src = src.rearrange("p (a b) -> p a b", b=dst.shape[-1])
                a(dst, src, ACT.Copy, scale=scale).then_inc(drained[name], 1)

            def body0(t, r):
                q = 1 - r
                p = t - 1
                if on(t, 1, PAIRS):
                    copy_out("tp0", pT[q][:, 0:2, :], use(0, "tp0", p))
                if on(t, 0, PAIRS - 1):
                    act.wait_ge(nmx0_done, t + 1)
                    for j in two:
                        last = a(pr[r][:, j, :], sh[r][:, j, :], ACT.Exp, bias=nmx[r][:, j:j + 1], scale=1.0 / 16.0,
                                 accum_out=rsum[r][:, j:j + 1])
                    last.then_inc(sm0_done, 1)
                if on(t, 1, PAIRS):
                    copy_out("tp1", cnT[q][:], use(0, "tp1", p))
                if on(t, -1, PAIRS - 2):
                    copy_out("pj0", xnT[q][:], pj_before(0, 0, t + 1, 0))
                    copy_out("pj1", qT[q][:], pj_before(0, 1, t + 1, 0))


            def attention(f, vbank, vcount, vslots, before, first={}, first_after={}, after={}):
                def exps(p, n):
                    i, name = n % 2, f"sc{n % 2}"
                    act.wait_ge(mx_done, group(f, p, n) + 1)
                    act.wait_ge(filled[f"tp{i}"], least(use(f, f"tp{i}", p, n // 2)))
                    for k in range(4):
                        h = head(n % 4, k)
                        last = a(pr[i][:, k, :], bank[name][:, k * S:(k + 1) * S], ACT.Exp, bias=mx[i][:, k:k + 1],
                                 accum_out=psum[n // 4][:, h:h + 1])
                    last.then_inc(drained[name], 1)

                def high_probs(p, n):
                    name = f"tp{n % 2}"
                    act.wait_ge(pv_done, least(group(f, p, n) - 1))
                    act.wait_ge(filled[name], use(f, name, p, n // 2) + 1)
                    a(pH[n % 2][:], four(name), ACT.Copy).then_inc(pH_done, 1)

                def value_part(i, p, r, src):
                    ready, done = ((drained[vbank], va_done), (vrest_done, vb_done))[i]
                    act.wait_ge(ready, vcount(p) if i == 0 else att(f, p) + 1)
                    a(v16[r][:, :, :, i, :].rearrange("p j h d -> p (j h) d"),
                      src[:].rearrange("p j (h d) -> p (j h) d", d=DH), ACT.Copy).then_inc(done, 1)

                def body(t, r):
                    q = 1 - r
                    for n in range(8):
                        if n in first and on(t, -1, PAIRS - 2):
                            first[n](t + 1, q)
                        if n in first_after and on(t, 1, PAIRS):
                            first_after[n](t - 1, q)
                        if n >= 3 and on(t, 0, PAIRS - 1):
                            high_probs(t, n - 3)
                        if n < 3 and on(t, 1, PAIRS):
                            high_probs(t - 1, n + 5)
                        if on(t, 0, PAIRS - 1):
                            exps(t, n)
                        if n in before and on(t, -1, PAIRS - 2):
                            before[n](t + 1, q)
                        if n in after and on(t, 1, PAIRS):
                            after[n](t - 1, q)
                        if n == vslots[0] and on(t, -1, PAIRS - 2):
                            value_part(0, t + 1, q, vf)
                        if n == vslots[1] and on(t, -1, PAIRS - 2):
                            value_part(1, t + 1, q, vrest)

                return body

            def queries(f, i):
                def part(p, r):
                    act.wait_ge(filled["pj1"], pj_before(f, 1, p, 1) + 1)
                    for o in range(C):
                        last = a(qT[r][:, o, :], bank["pj1"][:, o * T:(o + 1) * T], ACT.Identity,
                                 bias=bq[i][:, o:o + 1], scale=(0.25, 0.0625)[i])
                    last.then_inc(drained["pj1"], 1)
                return part

            body1 = attention(1, "pj1", lambda p: dr_before(1, 1, p, 0) + 1, (5, 7),
                      {2: lambda p, r: copy_out("pj0", xnT[r][:], pj_before(1, 0, p, 0)),
                       }, {7: queries(1, 0)})

            def body2(t, r):
                q = 1 - r
                p = t + 1
                if on(t, 0, PAIRS - 1):
                    copy_out("pj0", nmT[r][:, :], pj_before(2, 0, t, 1))
                for c in range(FF):
                    if c == 1 and on(t, -1, PAIRS - 2):
                        copy_out("pj0", xnT[q][:], pj_before(2, 0, p, 0))
                    if on(t, 0, PAIRS - 1):
                        name = ("sc0", "sc1", "tp0", "tp1")[c % 4]
                        act.wait_ge(filled[name], use(2, name, t, c // 4) + 1)
                        a(hT[r][:, c, :], bank[name][:, 0:T], ACT.Relu, bias=V("b1", c)).then_inc(drained[name], 1)
                    if c == 6 and on(t, -1, PAIRS - 2):
                        act.wait_ge(lsh_done, p + 1)
                        a(le[:, :, 0:NB], lsh[:], ACT.Exp).then_inc(le_done, 1)


            body3 = attention(3, "pj1", lambda p: dr_before(3, 1, p, 0) + 1, (5, 7),
                      {2: lambda p, r: copy_out("pj0", xnT[r][:], pj_before(3, 0, p, 0))}, {7: queries(3, 1)},
                      {7: lambda p, r: copy_out("pj0", hdT[:], pj_after(3, 0, p, 0))})

            body4 = attention(4, "pj1", lambda p: dr_before(4, 1, p, 2) + 1, (6, 7),
                      {2: lambda p, r: copy_out("pj1", cnT[r][:], pj_before(4, 1, p, 0)),
                       3: lambda p, r: copy_out("pj0", xnT[r][:], pj_before(4, 0, p, 0))},
                      {7: lambda p, r: copy_out("pj0", qT[r][:], pj_before(4, 0, p, 2), 0.25)},
                      {}, {6: lambda p, r: copy_out("pj0", hdT[:], pj_after(4, 0, p, 0))})

            def body5(t, r):
                q = 1 - r
                p = t + 1
                for e in range(E + SH):
                    if on(t, 0, PAIRS - 1):
                        act.wait_ge(filled[f"sc{e % 2}"], use(5, f"sc{e % 2}", t, e // 2) + 1)
                        act.wait_ge(hm_done, least(10 * t + e - 1))
                        a(sg[e % 2][:], bank[f"sc{e % 2}"][:, 0:T], ACT.Silu).then_inc(sg_done, 1)
                    if e == 4 and on(t, -1, PAIRS - 2):
                        copy_out("pj0", xnT[q][:], pj_before(5, 0, p, 0))
                    if e == 6 and on(t, -1, PAIRS - 2):
                        act.wait_ge(filled["pj1"], pj_before(5, 1, p, 0) + 1)
                        act.wait_ge(comb_done, p)
                        a(ls[:, :, 0:E], bank["pj1"][:, 0:2 * E].rearrange("p (j e) -> p j e", j=2),
                          ACT.Sigmoid).then_inc(sig_done, 1)

            body0(-1, 1)
            steps(act, body0)
            act.wait_ge(s_bf, 1)
            body1(-1, 1)
            body0(PAIRS, 0)
            steps(act, body1)
            body2(-1, 1)
            body1(PAIRS, 0)
            steps(act, body2)
            body3(-1, 1)
            body2(PAIRS, 0)
            steps(act, body3)
            body4(-1, 1)
            body3(PAIRS, 0)
            steps(act, body4)
            body5(-1, 1)
            body4(PAIRS, 0)
            steps(act, body5)
            body5(PAIRS, 0)

        @block.gpsimd
        def _(pool):
            g = nc.gpsimd
            g.memset(started[:, 1:2], 0.0).then_inc(x_ready[1], 1)
            g.memset(mhalf[:], -0.5).then_inc(s_small, 1)
            g.memset(nm[:], 0.0).then_inc(s_small, 1)
            g.memset(tops[:], -1.0).then_inc(s_small, 1)
            g.memset(tops5[:], -1.0).then_inc(s_small, 1)
            g.memset(le[:], -1.0).then_inc(s_small, 1)
            g.memset(ls[:], -1.0).then_inc(s_small, 1)
            pool.wait_ge(s_small, 1)

            def inverse(m, e, dst, s_in, s_mid, s_out_, n):
                pool.wait_ge(s_in, apart(pool, n + 1))
                g.tensor_scalar(e[:], m[:, :, 1:2].rearrange("p j o -> p (j o)"), EPS, None, ALU.add).then_inc(s_mid, 1)
                pool.wait_ge(s_mid, apart(pool, n + 1))
                g.tensor_tensor(dst[:], e[:], mhalf[:, 0:2], ALU.pow).then_inc(s_out_, 1)

            def x_inverse(f, p, r):
                inverse(mv[r], ve[r], rstd[r], mv_done, ve_done, rstd_done, pair(f, p))

            def body0(t, r):
                if on(t, -1, PAIRS - 2):
                    x_inverse(0, t + 1, 1 - r)


            def parts(r, i):
                return v16[r][:, :, :, i, :].rearrange("p j h d -> p (j h) d")

            def by_head(ap):
                return ap.rearrange("p j (h d) -> p (j h) d", d=DH)

            def value_rest(f, p, r):
                pool.wait_ge(va_done, apart(pool, att(f, p) + 1))
                g.tensor_tensor(by_head(vrest[:]), by_head(vf[:]), parts(r, 0), ALU.subtract).then_inc(vrest_done, 1)

            def value_last(f, p, r):
                pool.wait_ge(vb_done, apart(pool, att(f, p) + 1))
                g.tensor_tensor(parts(r, 2), by_head(vrest[:]), parts(r, 1), ALU.subtract).then_inc(vc_done, 1)

            def body1(t, r):
                q = 1 - r
                if on(t, -1, PAIRS - 2):
                    x_inverse(1, t + 1, q)
                if on(t, 1, PAIRS):
                    for j in two:
                        pool.wait_ge(drained[f"ov{j}"], apart(pool, use(1, f"ov{j}", t - 1) + 1))
                    g.tensor_tensor(xp(t - 1), xp(t - 1), hd[q][:], ALU.add).then_inc(x_ready[1], 1)
                if on(t, -1, PAIRS - 2):
                    value_rest(1, t + 1, q)
                    value_last(1, t + 1, q)


            def body2(t, r):
                if on(t, -1, PAIRS - 2):
                    x_inverse(2, t + 1, 1 - r)
                    pool.wait_ge(xn_done, apart(pool, pair(2, t + 1) + 1))
                    g.tensor_tensor(xp(t + 1), xp(t + 1), over(R("b2"), 2), ALU.add).then_inc(xadd, 1)


            def body3(t, r):
                q = 1 - r
                p = t + 1
                if on(t, -1, PAIRS - 2):
                    x_inverse(3, p, q)
                    pool.wait_ge(xn_done, apart(pool, pair(3, p) + 1))
                    g.tensor_tensor(xp(p), xp(p), xn[q][:], ALU.add).then_inc(xmid, 1)
                    pool.wait_ge(xmid, apart(pool, p + 1))
                    g.tensor_tensor(xp(p), xp(p), over(R("bo1"), 2), ALU.add).then_inc(xadd, 1)
                if on(t, -1, PAIRS - 2):
                    value_rest(3, p, q)
                    value_last(3, p, q)


            def body4(t, r):
                q = 1 - r
                p = t + 1
                if on(t, -1, PAIRS - 2):
                    x_inverse(4, p, q)
                    pool.wait_ge(rstd_done, apart(pool, pair(4, p) + 1))
                    g.tensor_tensor(v2[q][:], rstd[q][:], rstd[q][:], ALU.mult).then_inc(v2_done, 1)
                    pool.wait_ge(v2_done, apart(pool, 4 * p + 1))
                    g.tensor_tensor(v3[q][:], v2[q][:], mv[q][:, :, 1:2].rearrange("p j o -> p (j o)"),
                                    ALU.mult).then_inc(v2_done, 1)
                    pool.wait_ge(v2_done, apart(pool, 4 * p + 2))
                    g.tensor_scalar(v4[q][:], v3[q][:], EPS, None, ALU.add).then_inc(v2_done, 1)
                    pool.wait_ge(v2_done, apart(pool, 4 * p + 3))
                    g.tensor_tensor(v5[q][:], v4[q][:], mhalf[:, 0:2], ALU.pow).then_inc(v2_done, 1)
                    pool.wait_ge(v2_done, apart(pool, 4 * p + 4))
                    g.tensor_tensor(rq[q][:], v5[q][:], rstd[q][:], ALU.mult).then_inc(rq_done, 1)
                    inverse(cmv[q], cve[q], crs[q], cmv_done, cve_done, crs_done, p)
                    pool.wait_ge(xn_done, apart(pool, pair(4, p) + 1))
                    g.tensor_tensor(xp(p), xp(p), over(bias4[:, 3, :], 2), ALU.add).then_inc(xadd, 1)
                if on(t, -1, PAIRS - 2):
                    pool.wait_ge(drained["pj1"], apart(pool, dr_before(4, 1, p, 1) + 1))
                    g.tensor_tensor(rc[:, 1].rearrange("p j (h d) -> p (j h) d", d=DH),
                                    rt[:, 1].rearrange("p j (h d) -> p (j h) d", d=DH),
                                    over(R("cosk"), 2 * H), ALU.mult).then_inc(rc_done, 1)
                    pool.wait_ge(rc_done, apart(pool, p + 1))
                    pool.wait_ge(rs_done, apart(pool, p + 1))
                    g.tensor_tensor(ro[:, 1], rc[:, 1], rs[:, 1], ALU.add).then_inc(ro_done, 1)
                if on(t, 1, PAIRS):
                    inverse(hmv, hve, hrs, hmv_done, hve_done, hrs_done, t - 1)
                if on(t, -1, PAIRS - 2):
                    value_rest(4, p, q)
                    value_last(4, p, q)


            def body5(t, r):
                if on(t, -1, PAIRS - 2):
                    x_inverse(5, t + 1, 1 - r)

            body0(-1, 1)
            steps(pool, body0)
            body1(-1, 1)
            body0(PAIRS, 0)
            pool.wait_ge(s_w[1], 64)
            steps(pool, body1)
            body2(-1, 1)
            body1(PAIRS, 0)
            steps(pool, body2)
            body3(-1, 1)
            body2(PAIRS, 0)
            for i, name in enumerate(("gq", "gk", "gv", "go")):
                pool.wait_ge(filled[f"pj{i % 2}"], pj_base(3, i % 2) - PJ_FOLD + i // 2 + 1)
                for c in range(C):
                    last = g.tensor_scalar(Wx[:, i, c, :], Wx[:, i, c, :], V(name, c), None, ALU.mult)
                last.then_inc(s_folded, 1)
            steps(pool, body3)
            body4(-1, 1)
            body3(PAIRS, 0)
            steps(pool, body4)
            body5(-1, 1)
            body4(PAIRS, 0)
            steps(pool, body5)
            body5(PAIRS, 0)


def kernel(**inputs):
    import concourse.bacc as bacc
    from concourse.bass_utils import run_bass_kernel_spmd

    g = {k: np.asarray(v) for k, v in inputs.items()}

    def tok(a):
        return a.transpose(1, 0, 2)

    def chunks(w):
        return w.reshape(-1, P, w.shape[1]).transpose(1, 0, 2)

    def cols(a):
        return a.reshape(-1, P).T

    def rep(a):
        return np.broadcast_to(a.reshape(1, -1), (P, a.size))

    one = np.float32
    inv = (one(1.0) / one(10000.0) ** (np.arange(0, DH, 2, dtype=np.float32) / one(DH))).astype(one)
    at = np.arange(S, dtype=np.float32)
    sign = np.where(np.arange(DH) % 2, 1.0, -1.0).astype(one)

    def angles(pos):
        return np.repeat((pos[:, None] * inv[None, :]).astype(one), 2, axis=1).astype(np.float64)

    aq, ak = angles(at - S // 2), angles(at)
    half = (np.arange(P) // DH) % 2
    vec = {"bq0": cols(g["L0_xattn_bq"]), "bk0": cols(g["L0_xattn_bk"]), "b1": cols(g["L0_ffn_b1"]),
           "bq1": cols(g["L1_attn_b_qkv"][:D]), "bk1": cols(g["L1_attn_b_qkv"][D:2 * D]),
           "gq": cols(g["L1_xattn_ln_q_w"]), "gk": cols(g["L1_xattn_ln_k_w"]),
           "gv": cols(g["L1_xattn_ln_v_w"]), "go": cols(g["L1_xattn_ln_o_w"]),
           "even": (half == 0).astype(one)[:, None], "odd": (half == 1).astype(one)[:, None]}
    rows = {"bv0": rep(g["L0_xattn_bv"]), "br": rep(g["L0_ffn_b_router"]), "b2": rep(g["L0_ffn_b2"]),
            "bv1": rep(g["L1_attn_b_qkv"][2 * D:]), "bo1": rep(g["L1_attn_b_o"]),
            "bxq": rep(g["L1_xattn_b_q"]), "bxk": rep(g["L1_xattn_b_k"]),
            "bxv": rep(g["L1_xattn_b_v"]), "bxo": rep(g["L1_xattn_b_o"]),
            "cosq": np.cos(aq).astype(one), "sinq": (np.sin(aq) * sign).astype(one),
            "cosk": np.cos(ak).astype(one), "sink": (np.sin(ak) * sign).astype(one)}
    expand = np.zeros((P, FF * P), one)
    for b in range(NB):
        expand[b, b * BLOCK:(b + 1) * BLOCK] = NEG
    causal = np.where(np.tril(np.ones((S, S), bool)), 0.0, NEG).astype(one)
    tokens = g["itok_Bx1xSx1_0_63"].reshape(B, S)
    wx = [g[f"L1_xattn_w_{n}"].T for n in "qkvo"]
    lnb = [np.broadcast_to(cols(g[f"L1_xattn_ln_{n}_b"])[:, :, None], (P, C, P)) for n in "qkvo"]
    arrays = dict(
        x=tok(g["x"]), ctxT=chunks(g["ctx_1024"].reshape(B * S, D).T), ctx=tok(g["ctx_1024"]),
        tokq=tokens.T, tokk=np.broadcast_to(tokens[None], (P, B, S)),
        mask=np.ascontiguousarray(g["mask_BxSxS2_bf0"].transpose(1, 0, 2)).view(np.int32), ident=np.eye(P, dtype=one),
        causal=causal, expand=expand, vec=np.concatenate([vec[n] for n in VEC], 1),
        rows=np.concatenate([rows[n] for n in ROWS], 1), lnb=np.stack(lnb, 1),
        w_qk=chunks(g["L0_attn_qk"]), w_ov=chunks(g["L0_attn_ov"]),
        w_q0=chunks(g["L0_xattn_Wq"].T), w_k0=chunks(g["L0_xattn_Wk"].T), w_v0=chunks(g["L0_xattn_Wv"].T),
        w_r0=chunks(g["L0_ffn_w_router"]), w_1=chunks(g["L0_ffn_w1"].T), w_2=chunks(g["L0_ffn_w2"].T),
        w_qkv=chunks(g["L1_attn_w_qkv"].T), w_o1=chunks(g["L1_attn_w_o"].T),
        w_x=np.stack([chunks(w) for w in wx], 1), w_g=chunks(g["L1_ffn_gate_weight"].T),
        w_gate=chunks(g["L1_ffn_w_gate"].reshape(E * EI, D).T), w_up=chunks(g["L1_ffn_w_up"].reshape(E * EI, D).T),
        w_down=g["L1_ffn_w_down"].transpose(2, 0, 1), ws_gate=chunks(g["L1_ffn_ws_gate"].T),
        ws_up=chunks(g["L1_ffn_ws_up"].T), ws_down=chunks(g["L1_ffn_ws_down"].T))
    nc = bacc.Bacc("TRN2", target_bir_lowering=False, num_devices=1)
    feed, args = {}, {}
    for name, a in arrays.items():
        a = np.ascontiguousarray(a)
        feed[f"in_{name}"] = a
        args[name] = nc.dram_tensor(f"in_{name}", a.shape, mybir.dt.from_np(a.dtype), kind="ExternalInput").ap()
    args["out"] = nc.dram_tensor("out_x", (P, B, D), F32, kind="ExternalOutput").ap()
    program(nc, **args)
    got = run_bass_kernel_spmd(nc, [feed], core_ids=[0]).results[0]["out_x"]
    return np.ascontiguousarray(got.transpose(1, 0, 2))
```
